# Optimizing a Trainium2 kernel written in Bass

```python
import numpy as np
import jax
import jax.numpy as jnp

def _softmax(x, axis=-1):
    return jax.nn.softmax(x, axis=axis)

def _gelu(x):
    return jax.nn.gelu(x, approximate=True)

def _silu(x):
    return jax.nn.silu(x)

def _sigmoid(x):
    return jax.nn.sigmoid(x)

def _layernorm(x, axis=-1, eps=1e-05):
    m = jnp.mean(x, axis=axis, keepdims=True)
    v = jnp.var(x, axis=axis, keepdims=True)
    return (x - m) / jnp.sqrt(v + eps)

def _scatter_add(tgt, idx, src, axis=0):
    return tgt.at[idx].add(src)

def _segment_sum(src, seg, n):
    return jax.ops.segment_sum(src, seg, n)
kernel_name = 'mk_adaln_d2_jaxref_r8_ed8240'

def setup_inputs(seed: int=0):
    np.random.seed(seed)
    _w = jnp.asarray

    def _L0_attn_setup():
        import jax, jax.numpy as jnp
        import numpy as np
        ROPE_BASE = 10000.0
        ROPE_SCALE = 1.0
        ATTN_SCALE = 0.08838834764831845
        WINDOW = 128
        EPS = 1e-06

        def rms_norm(x, scale):
            var = jnp.mean(jnp.square(x), axis=-1, keepdims=True)
            return x * jax.lax.rsqrt(var + EPS) * scale

        def apply_rope(x, positions):
            H = x.shape[-1]
            frac = jnp.arange(0, H, 2, dtype=jnp.float32) / H
            timescale = ROPE_BASE ** frac
            sinusoid = positions[..., None].astype(jnp.float32) / timescale
            sinusoid = sinusoid / ROPE_SCALE
            sin = jnp.sin(sinusoid)[:, :, None, :]
            cos = jnp.cos(sinusoid)[:, :, None, :]
            x1, x2 = jnp.split(x, 2, axis=-1)
            return jnp.concatenate([x1 * cos - x2 * sin, x2 * cos + x1 * sin], axis=-1).astype(x.dtype)
        key = jax.random.key(seed)
        ks = jax.random.split(key, 4)
        B, T, D, N, K, H = (1, 512, 256, 16, 8, 128)
        return {'x': jax.random.normal(ks[0], (B, T, D), jnp.float32), 'q_kernel': jax.random.normal(ks[1], (N, D, H), jnp.float32) * D ** (-0.5), 'kv_kernel': jax.random.normal(ks[2], (2, K, D, H), jnp.float32) * D ** (-0.5), 'out_kernel': jax.random.normal(ks[3], (N, H, D), jnp.float32) * (N * H) ** (-0.5), 'q_norm_scale': jnp.ones((H,), jnp.float32), 'k_norm_scale': jnp.ones((H,), jnp.float32)}
    _L0_attn_in = _L0_attn_setup()

    def _L0_ffn_setup():
        import jax, jax.numpy as jnp
        import numpy as np
        B, S, H, I, E, TOP_K, NS = (2, 256, 256, 176, 8, 2, 2)
        SI = I * NS
        INIT = 0.02
        key = jax.random.key(seed)
        ks = jax.random.split(key, 9)
        f32 = jnp.float32
        return {'hidden_states': jax.random.normal(ks[0], (B, S, H), f32), 'router_w': jax.random.normal(ks[1], (E, H), f32) * INIT, 'gate_w': jax.random.normal(ks[2], (E, H, I), f32) * INIT, 'up_w': jax.random.normal(ks[3], (E, H, I), f32) * INIT, 'down_w': jax.random.normal(ks[4], (E, I, H), f32) * INIT, 's_gate_w': jax.random.normal(ks[5], (H, SI), f32) * INIT, 's_gate_b': jnp.zeros((SI,), f32), 's_up_w': jax.random.normal(ks[6], (H, SI), f32) * INIT, 's_up_b': jnp.zeros((SI,), f32), 's_down_w': jax.random.normal(ks[7], (SI, H), f32) * INIT, 's_down_b': jnp.zeros((H,), f32)}
    _L0_ffn_in = _L0_ffn_setup()
    _L0_c = _w((lambda *s: np.random.randn(*s).astype(np.float32) * 0.05)(16, 256))
    _L0_wmod = _w((lambda *s: np.random.randn(*s).astype(np.float32) * 0.05)(256, 6 * 256) * 256 ** (-0.5))

    def _L1_attn_setup():
        import jax, jax.numpy as jnp
        import numpy as np
        N_HEAD = 32
        HEAD_ID = 0
        MASKED_BIAS = -10000.0
        key = jax.random.key(seed)
        k1, k2, k3 = jax.random.split(key, 3)
        B, S, E = (1, 256, 256)
        hidden_states = jax.random.normal(k1, (B, S, E), dtype=jnp.float32)
        W_attn = jax.random.normal(k2, (E, 3 * E), dtype=jnp.float32) * (1.0 / np.sqrt(E))
        b_attn = jnp.zeros((3 * E,), dtype=jnp.float32)
        W_proj = jax.random.normal(k3, (E, E), dtype=jnp.float32) * (1.0 / np.sqrt(E))
        b_proj = jnp.zeros((E,), dtype=jnp.float32)
        return {'hidden_states': hidden_states, 'W_attn': W_attn, 'b_attn': b_attn, 'W_proj': W_proj, 'b_proj': b_proj}
    _L1_attn_in = _L1_attn_setup()

    def _L1_ffn_setup():
        import jax, jax.numpy as jnp
        import numpy as np
        B, S, D, H = (4, 256, 256, 1024)

        def fwht(x):
            orig_shape = x.shape
            n = orig_shape[-1]
            x = x.reshape(-1, n)
            h = 1
            while h < n:
                xb = x.reshape(-1, n // (2 * h), 2, h)
                a = xb[:, :, 0, :]
                b = xb[:, :, 1, :]
                x = jnp.stack([a + b, a - b], axis=2).reshape(-1, n)
                h *= 2
            scale = jnp.asarray(1.0 / np.sqrt(n), dtype=x.dtype)
            return (x * scale).reshape(orig_shape)
        key = jax.random.key(seed)
        kx, k1, k2, k3 = jax.random.split(key, 4)
        x = jax.random.normal(kx, (B, S, D), dtype=jnp.float32)
        W1 = jax.random.normal(k1, (H, D), dtype=jnp.float32) * (1.0 / np.sqrt(D))
        W2 = jax.random.normal(k2, (D, H), dtype=jnp.float32) * (1.0 / np.sqrt(H))
        W3 = jax.random.normal(k3, (H, D), dtype=jnp.float32) * (1.0 / np.sqrt(D))
        return {'x': x, 'W1': W1, 'W2': W2, 'W3': W3}
    _L1_ffn_in = _L1_ffn_setup()
    _L1_c = _w((lambda *s: np.random.randn(*s).astype(np.float32) * 0.05)(16, 256))
    _L1_wmod = _w((lambda *s: np.random.randn(*s).astype(np.float32) * 0.05)(256, 6 * 256) * 256 ** (-0.5))
    _d = {'L0_attn_x': _L0_attn_in['x'], 'L0_attn_q_kernel': _L0_attn_in['q_kernel'], 'L0_attn_kv_kernel': _L0_attn_in['kv_kernel'], 'L0_attn_out_kernel': _L0_attn_in['out_kernel'], 'L0_attn_q_norm_scale': _L0_attn_in['q_norm_scale'], 'L0_attn_k_norm_scale': _L0_attn_in['k_norm_scale'], 'L0_ffn_router_w': _L0_ffn_in['router_w'], 'L0_ffn_gate_w': _L0_ffn_in['gate_w'], 'L0_ffn_up_w': _L0_ffn_in['up_w'], 'L0_ffn_down_w': _L0_ffn_in['down_w'], 'L0_ffn_s_gate_w': _L0_ffn_in['s_gate_w'], 'L0_ffn_s_gate_b': _L0_ffn_in['s_gate_b'], 'L0_ffn_s_up_w': _L0_ffn_in['s_up_w'], 'L0_ffn_s_up_b': _L0_ffn_in['s_up_b'], 'L0_ffn_s_down_w': _L0_ffn_in['s_down_w'], 'L0_ffn_s_down_b': _L0_ffn_in['s_down_b'], 'L0_c': _L0_c, 'L0_wmod': _L0_wmod, 'L1_attn_W_attn': _L1_attn_in['W_attn'], 'L1_attn_b_attn': _L1_attn_in['b_attn'], 'L1_attn_W_proj': _L1_attn_in['W_proj'], 'L1_attn_b_proj': _L1_attn_in['b_proj'], 'L1_ffn_W1': _L1_ffn_in['W1'], 'L1_ffn_W2': _L1_ffn_in['W2'], 'L1_ffn_W3': _L1_ffn_in['W3'], 'L1_c': _L1_c, 'L1_wmod': _L1_wmod}
    _x0 = _d['L0_attn_x']
    _d['L0_attn_x'] = jax.random.normal(jax.random.fold_in(jax.random.key(seed), 1), (16, 256, 256), dtype=_x0.dtype)
    del _x0
    return _d

def reference(L0_attn_x, L0_attn_q_kernel, L0_attn_kv_kernel, L0_attn_out_kernel, L0_attn_q_norm_scale, L0_attn_k_norm_scale, L0_ffn_router_w, L0_ffn_gate_w, L0_ffn_up_w, L0_ffn_down_w, L0_ffn_s_gate_w, L0_ffn_s_gate_b, L0_ffn_s_up_w, L0_ffn_s_up_b, L0_ffn_s_down_w, L0_ffn_s_down_b, L0_c, L0_wmod, L1_attn_W_attn, L1_attn_b_attn, L1_attn_W_proj, L1_attn_b_proj, L1_ffn_W1, L1_ffn_W2, L1_ffn_W3, L1_c, L1_wmod):

    def _L0_attn_ref(x, q_kernel, kv_kernel, out_kernel, q_norm_scale, k_norm_scale):
        import jax, jax.numpy as jnp
        import numpy as np
        ROPE_BASE = 10000.0
        ROPE_SCALE = 1.0
        ATTN_SCALE = 0.08838834764831845
        WINDOW = 128
        EPS = 1e-06

        def rms_norm(x, scale):
            var = jnp.mean(jnp.square(x), axis=-1, keepdims=True)
            return x * jax.lax.rsqrt(var + EPS) * scale

        def apply_rope(x, positions):
            H = x.shape[-1]
            frac = jnp.arange(0, H, 2, dtype=jnp.float32) / H
            timescale = ROPE_BASE ** frac
            sinusoid = positions[..., None].astype(jnp.float32) / timescale
            sinusoid = sinusoid / ROPE_SCALE
            sin = jnp.sin(sinusoid)[:, :, None, :]
            cos = jnp.cos(sinusoid)[:, :, None, :]
            x1, x2 = jnp.split(x, 2, axis=-1)
            return jnp.concatenate([x1 * cos - x2 * sin, x2 * cos + x1 * sin], axis=-1).astype(x.dtype)
        B, T, D = x.shape
        N, _, H = q_kernel.shape
        K = kv_kernel.shape[1]
        G = N // K
        q = jnp.einsum('btd,ndh->btnh', x, q_kernel)
        kv = jnp.einsum('bsd,ckdh->cbskh', x, kv_kernel)
        k, v = (kv[0], kv[1])
        q = rms_norm(q, q_norm_scale)
        k = rms_norm(k, k_norm_scale)
        positions = jnp.broadcast_to(jnp.arange(T)[None, :], (B, T))
        q = apply_rope(q, positions)
        k = apply_rope(k, positions)
        i = jnp.arange(T)[:, None]
        j = jnp.arange(T)[None, :]
        mask = (j <= i) & (i - j < WINDOW)
        qg = q.reshape(B, T, K, G, H)
        logits = jnp.einsum('btkgh,bskh->bkgts', qg * ATTN_SCALE, k)
        logits = jnp.where(mask[None, None, None], logits, jnp.finfo(logits.dtype).min)
        probs = jax.nn.softmax(logits, axis=-1)
        enc = jnp.einsum('bkgts,bskh->btkgh', probs, v).reshape(B, T, N, H)
        return jnp.einsum('btnh,nhd->btd', enc, out_kernel)

    def _L0_ffn_ref(hidden_states, router_w, gate_w, up_w, down_w, s_gate_w, s_gate_b, s_up_w, s_up_b, s_down_w, s_down_b):
        import jax, jax.numpy as jnp
        import numpy as np
        B, S, H, I, E, TOP_K, NS = (2, 256, 256, 176, 8, 2, 2)
        SI = I * NS
        INIT = 0.02
        b, s, h = hidden_states.shape
        x = hidden_states.reshape(-1, h)
        T = x.shape[0]
        num_experts = router_w.shape[0]
        logits = x @ router_w.T
        probs = jax.nn.softmax(logits.astype(jnp.float32), axis=-1)
        topk_w, topk_idx = jax.lax.top_k(probs, TOP_K)
        topk_w = topk_w / jnp.sum(topk_w, axis=-1, keepdims=True)
        combine = jnp.zeros((T, num_experts), probs.dtype)
        combine = combine.at[jnp.arange(T)[:, None], topk_idx].add(topk_w)

        def expert_step(acc, ws):
            gw, uw, dw, ce = ws
            out = jax.nn.silu(x @ gw) * (x @ uw) @ dw
            return (acc + ce[:, None].astype(out.dtype) * out, None)
        moe_out, _ = jax.lax.scan(expert_step, jnp.zeros_like(x), (gate_w, up_w, down_w, combine.T))
        shared = jax.nn.silu(x @ s_gate_w + s_gate_b) * (x @ s_up_w + s_up_b) @ s_down_w + s_down_b
        return (moe_out + shared).reshape(b, s, h)

    def _L1_attn_ref(hidden_states, W_attn, b_attn, W_proj, b_proj):
        import jax, jax.numpy as jnp
        import numpy as np
        N_HEAD = 32
        HEAD_ID = 0
        MASKED_BIAS = -10000.0
        B, S, E = hidden_states.shape
        H = N_HEAD
        D = E // H
        m = 2.0 ** (-(8.0 / H) * (HEAD_ID + 1))
        qkv = hidden_states @ W_attn + b_attn
        q, k, v = jnp.split(qkv, 3, axis=-1)
        q = q.reshape(B, S, H, D).transpose(0, 2, 1, 3)
        k = k.reshape(B, S, H, D).transpose(0, 2, 1, 3)
        v = v.reshape(B, S, H, D).transpose(0, 2, 1, 3)
        scores = jnp.einsum('bhqd,bhkd->bhqk', q, k) / jnp.sqrt(jnp.float32(D))
        rows = jnp.arange(S)[:, None]
        cols = jnp.arange(S)[None, :]
        causal = cols <= rows
        scores = jnp.where(causal, scores, jnp.float32(MASKED_BIAS))
        alibi = jnp.where(causal, (cols - rows).astype(scores.dtype), 0.0)
        scores = scores + alibi * m
        probs = jax.nn.softmax(scores, axis=-1)
        attn = jnp.einsum('bhqk,bhkd->bhqd', probs, v)
        attn = attn.transpose(0, 2, 1, 3).reshape(B, S, E)
        out = attn @ W_proj + b_proj
        return out

    def _L1_ffn_ref(x, W1, W2, W3):
        import jax, jax.numpy as jnp
        import numpy as np
        B, S, D, H = (4, 256, 256, 1024)

        def fwht(x):
            orig_shape = x.shape
            n = orig_shape[-1]
            x = x.reshape(-1, n)
            h = 1
            while h < n:
                xb = x.reshape(-1, n // (2 * h), 2, h)
                a = xb[:, :, 0, :]
                b = xb[:, :, 1, :]
                x = jnp.stack([a + b, a - b], axis=2).reshape(-1, n)
                h *= 2
            scale = jnp.asarray(1.0 / np.sqrt(n), dtype=x.dtype)
            return (x * scale).reshape(orig_shape)
        up_gate = jnp.einsum('bsd,hd->bsh', x, W1)
        up_lin = jnp.einsum('bsd,hd->bsh', x, W3)
        hidden = jax.nn.silu(up_gate) * up_lin
        hidden = fwht(hidden)
        out = jnp.einsum('bsh,dh->bsd', hidden, W2)
        return out
    x = L0_attn_x
    mod = (_silu(L0_c) @ L0_wmod).reshape(L0_c.shape[0], 6, 1, -1)
    sa, ca, ga, sb, cb, gb = (mod[:, 0], mod[:, 1], mod[:, 2], mod[:, 3], mod[:, 4], mod[:, 5])
    ga = (2 * (ga >= 0) - 1) * jnp.maximum(jnp.abs(ga), 0.25)
    gb = (2 * (gb >= 0) - 1) * jnp.maximum(jnp.abs(gb), 0.25)
    h = _layernorm(x, axis=-1) * (1 + ca) + sa
    x = x + ga * _L0_attn_ref(h, L0_attn_q_kernel, L0_attn_kv_kernel, L0_attn_out_kernel, L0_attn_q_norm_scale, L0_attn_k_norm_scale)
    h = _layernorm(x, axis=-1) * (1 + cb) + sb
    x = x + gb * _L0_ffn_ref(h, L0_ffn_router_w, L0_ffn_gate_w, L0_ffn_up_w, L0_ffn_down_w, L0_ffn_s_gate_w, L0_ffn_s_gate_b, L0_ffn_s_up_w, L0_ffn_s_up_b, L0_ffn_s_down_w, L0_ffn_s_down_b)
    mod = (_silu(L1_c) @ L1_wmod).reshape(L1_c.shape[0], 6, 1, -1)
    sa, ca, ga, sb, cb, gb = (mod[:, 0], mod[:, 1], mod[:, 2], mod[:, 3], mod[:, 4], mod[:, 5])
    ga = (2 * (ga >= 0) - 1) * jnp.maximum(jnp.abs(ga), 0.25)
    gb = (2 * (gb >= 0) - 1) * jnp.maximum(jnp.abs(gb), 0.25)
    h = _layernorm(x, axis=-1) * (1 + ca) + sa
    x = x + ga * _L1_attn_ref(h, L1_attn_W_attn, L1_attn_b_attn, L1_attn_W_proj, L1_attn_b_proj)
    h = _layernorm(x, axis=-1) * (1 + cb) + sb
    x = x + gb * _L1_ffn_ref(h, L1_ffn_W1, L1_ffn_W2, L1_ffn_W3)
    return x

_drawn_inputs = setup_inputs


def setup_inputs(seed=0):
    import zlib

    import numpy as np

    out = dict(_drawn_inputs(seed))
    spreads = {'L0_attn_q_norm_scale': (1.0, 0.6),
     'L0_attn_k_norm_scale': (1.0, 0.6),
     'L0_ffn_s_gate_b': (0.0, 0.8),
     'L0_ffn_s_up_b': (0.0, 0.8),
     'L0_ffn_s_down_b': (0.0, 1.262),
     'L1_attn_b_attn': (0.0, 1.358),
     'L1_attn_b_proj': (0.0, 1.381)}
    factors = {'L0_ffn_router_w': 8.0,
     'L0_ffn_gate_w': 8.0,
     'L0_ffn_up_w': 8.0,
     'L0_ffn_down_w': 8.0,
     'L0_ffn_s_gate_w': 8.0,
     'L0_ffn_s_up_w': 8.0,
     'L0_ffn_s_down_w': 8.0}
    for name, (base, spread) in spreads.items():
        noise = np.random.default_rng([zlib.crc32(name.encode()), seed]).standard_normal(out[name].shape)
        drawn = base * np.exp(spread * noise) if base else spread * noise
        out[name] = jnp.asarray(drawn.astype(out[name].dtype))
    for name, factor in factors.items():
        out[name] = (out[name] * factor).astype(out[name].dtype)
    return out
```

```python
from contextlib import ExitStack

import numpy as np

import concourse.bass as bass
from concourse import mybir

F32 = mybir.dt.float32
F16 = mybir.dt.float16
I32 = mybir.dt.int32
ALU = mybir.AluOpType
ACT = mybir.ActivationFunctionType
AX = mybir.AxisListType

P = 128
B, T, D = 16, 256, 256
TT = T // P
DC = D // P
NH, NKV, HD = 16, 8, 128
WINDOW = 128
ATT_SCALE = 0.08838834764831845
EXPERTS, INNER, SHARED = 8, 176, 352
HID0 = EXPERTS * INNER + SHARED
J0 = -(-HID0 // P)
HP = J0 * P
JB = (EXPERTS * INNER) // P
H1, HD1 = 32, 8
HID1 = 1024
J1 = HID1 // P
WS = 64.0
NEG = -1e30

COLS = {}
_at = 0
for _name, _n in (("qkv", DC * NKV * 512), ("o", NH * D), ("g", DC * HP), ("u", DC * HP), ("d", J0 * D),
                  ("r", DC * EXPERTS), ("a1", DC * 3 * D), ("p1", DC * D), ("w1", DC * HID1), ("w3", DC * HID1)):
    COLS[_name] = _at
    _at += _n
NW = _at
COLS["w2"] = NW
NW2 = NW + J1 * D
CHUNK = next(n for n in range(1500, 0, -1) if NW % n == 0 and n % 4 == 0)
NCHUNK = NW // CHUNK

BG, BU = 0, (J0 - JB) * P
BD = 2 * BU
BA = BD + D
BP = BA + 3 * D
NB = BP + D

K_ID, K_M0, K_M1, K_HM, K_IO, K_BS, K_EPS = 0, 128, 512, 896, 900, 908, 910
NC = 912

AFTER_AT0 = {0: [], 1: [("lnc", 0, 1)], 10: [("res0", 0), ("lna", 1, 0)], 11: [("lnb", 1, 0)],
             12: [("lnc", 1, 0)], 13: [("rt", 0)], 15: [("ct", 0)], 18: [("res0", 1), ("lna", 1, 1)]}
AFTER_FF0 = {0: [("lnb", 1, 1)], 2: [("lnc", 1, 1)], 4: [("rt", 1)], 7: [("ct", 1)],
             15: [("resf", 0, 0), ("lna", 2, 0)], 16: [("lnb", 2, 0)], 18: [("lnc", 2, 0)], 20: [("q1", 0)],
             22: [("k1", 0)], 24: [("v1", 0)], 25: [("qm", 0)], 29: [("resf", 0, 1), ("lna", 2, 1)]}
AFTER_AT1 = {0: [("lnb", 2, 1)], 1: [("lnc", 2, 1)], 2: [("k1", 1)], 3: [("v1", 1)], 4: [("q1", 1)],
             7: [("qm", 1)], 9: [("pvr", 0)], 10: [("at", 0)], 11: [("pj", 0), ("lna", 3, 0)],
             12: [("lnb", 3, 0)], 13: [("lnc", 3, 0)], 17: [("pvr", 1)]}
AFTER_FF1 = {0: [("at", 1)], 1: [("pj", 1), ("lna", 3, 1)], 2: [("lnb", 3, 1)], 3: [("lnc", 3, 1)],
             9: [("resf", 1, 0)], 17: [("resf", 1, 1)]}
ORDER = [("mc", 0), ("mc", 1), ("lna", 0, 0), ("lnb", 0, 0), ("lnc", 0, 0), ("lna", 0, 1), ("lnb", 0, 1)]
for _u in range(19):
    ORDER += [("at0", _u)] + AFTER_AT0.get(_u, [])
for _v in range(2 * J0 + 2):
    ORDER += [("ff0", _v)] + AFTER_FF0.get(_v, [])
for _w in range(18):
    ORDER += [("at1", _w)] + AFTER_AT1.get(_w, [])
for _v in range(2 * J1 + 2):
    ORDER += [("ff1", _v)] + AFTER_FF1.get(_v, [])

MISC, MISC_HI = {}, {}
_hi = 0
for _item in ORDER:
    _uses = []
    if _item[0] == "at0" and 1 <= _item[1] <= 16:
        _uses = [("t1", _item[1] - 1, _t) for _t in range(TT)]
    elif _item[0] in ("lnc", "rt", "ct", "q1", "k1", "v1", "at", "pj"):
        _uses = [_item]
    for _k in _uses:
        MISC[_k] = len(MISC) + 1
        if _k[0] in ("t1", "q1", "k1", "v1", "at"):
            _hi += 1
            MISC_HI[_k] = _hi
NPAIR = B // 2
U0 = 2 * NKV
W1G = 16
CHAIN = 1100


class Signal:

    def __init__(self, handle, per, unit=1):
        self.handle, self.per, self.unit = handle, per, unit

    def count(self, i, n):
        return i * (self.per * self.unit) + (self.per + n) * self.unit


def build(nc, x_in, wall, w2t, brow, cf, hadm, rope, nsc, sel_in, ct_in, wmod, out, gates_dram):
    ctx = ExitStack()
    with ctx:
        def sb(name, shape, dt):
            return ctx.enter_context(nc.sbuf_tensor(name, shape, dt))

        def sem(name):
            return ctx.enter_context(nc.semaphore(name))

        signals = []

        def signal(name, per, unit=1):
            signals.append(Signal(sem(name), per, unit))
            return signals[-1]

        whi = sb("whi", [P, NW2], F16)
        wlo = sb("wlo", [P, NW2], F16)
        brows = sb("brows", [2, NB], F16)
        sel = sb("sel", [17, HP], F16)
        ones = sb("ones", [2, T], F16)
        con = sb("con", [P, NC], F32)
        ropec = sb("ropec", [P, TT, 3, HD], F32)
        ropes = sb("ropes", [P, TT, 3, HD], F32)
        modt = sb("modt", [P, B, 16], F32)
        mcol = sb("mcol", [P, 2, 16], F32)
        xin = sb("xin", [P, 2, TT, D], F32)
        xs = sb("xs", [P, 2, TT, D], F32)
        gate = sb("gate", [P, 2, 2, D], F32)
        hth = sb("hth", [P, 2, DC, T], F16)
        htl = sb("htl", [P, 2, DC, T], F16)
        hf = sb("hf", [P, 2 * T], F32)
        xn = sb("xn", [P, TT, D], F32)
        vh0 = sb("vh0", [P, 4, TT, HD], F16)
        vl0 = sb("vl0", [P, 4, TT, HD], F16)
        k1h = sb("k1h", [P, 2, DC, T], F16)
        k1l = sb("k1l", [P, 2, DC, T], F16)
        v1h = sb("v1h", [P, 2, TT, D], F16)
        v1l = sb("v1l", [P, 2, TT, D], F16)
        q1h = sb("q1h", [P, DC * T], F16)
        q1l = sb("q1l", [P, DC * T], F16)
        qmh = sb("qmh", [P, 4, DC * T], F16)
        qml = sb("qml", [P, 4, DC * T], F16)
        ctt = sb("ctt", [17, 2, T], F16)
        small = sb("small", [P, 512], F32)
        NARENA = 18 * 256
        arena = sb("arena", [P, NARENA], F32)

        spot = [0]

        def small_at(n):
            spot[0] += n
            assert spot[0] <= 512
            return small[:, spot[0] - n:spot[0]]

        st6 = small_at(TT * 6).rearrange("p (t k) -> p t k", t=TT)
        mv = small_at(TT * 2).rearrange("p (t k) -> p t k", t=TT)
        lv = small_at(TT)
        lr = small_at(2 * TT)
        half = small_at(8)
        ss = small_at(6)
        ms = small_at(6)
        r0 = small_at(12).rearrange("p (k n) -> p k n", k=2)
        rs0 = small_at(24).rearrange("p (k n) -> p k n", k=4)
        mx0 = small_at(8).rearrange("p (k n) -> p k n", k=2)
        nb0 = small_at(8).rearrange("p (k n) -> p k n", k=2)
        sm0 = small_at(8).rearrange("p (k n) -> p k n", k=2)
        ri0 = small_at(8).rearrange("p (k n) -> p k n", k=2)
        rt_l = small_at(16).rearrange("p (t e) -> p t e", t=TT)
        rt_e = small_at(16).rearrange("p (t e) -> p t e", t=TT)
        rt_a = small_at(16).rearrange("p (t e) -> p t e", t=TT)
        rt_k = small_at(16).rearrange("p (t e) -> p t e", t=TT)
        rt_k2 = small_at(16).rearrange("p (t e) -> p t e", t=TT)
        rt_m = small_at(8).rearrange("p (k t) -> p k t", t=TT)
        c17 = small_at(34).rearrange("p (t e) -> p t e", t=TT)
        mx1 = small_at(16).rearrange("p (k n) -> p k n", k=2)
        nb1 = small_at(16).rearrange("p (k n) -> p k n", k=2)
        sum1 = small_at(2 * 64).rearrange("p (s t h) -> p s t h", s=2, t=TT)
        ri1 = small_at(64).rearrange("p (t h) -> p t h", t=TT)
        ch16 = small_at(8).bitcast(F16).rearrange("p (t e) -> p t e", t=TT)

        def carve(spots):
            at, found = 0, []
            for words, dt in spots:
                a = arena[:, at:at + words]
                found.append(a if dt == F32 else a.bitcast(F16))
                at += words
            assert at <= NARENA, at
            return found

        ra, rb, qkh, qkl, smx, pth, ptl, ench, encl = carve(
            [(768, F32), (768, F32), (384, F16), (384, F16), (768, F32), (384, F16), (384, F16),
             (256, F16), (256, F16)])
        ra = ra.rearrange("p (t k h) -> p t k h", t=TT, k=3)
        rb = rb.rearrange("p (t k h) -> p t k h", t=TT, k=3)
        qkh = qkh.rearrange("p (k n) -> p k n", k=3)
        qkl = qkl.rearrange("p (k n) -> p k n", k=3)
        smx = smx.rearrange("p (k n) -> p k n", k=2)
        pth = pth.rearrange("p (k n) -> p k n", k=6)
        ptl = ptl.rearrange("p (k n) -> p k n", k=6)
        ench = ench.rearrange("p (t k n) -> p t k n", t=TT, k=2)
        encl = encl.rearrange("p (t k n) -> p t k n", t=TT, k=2)
        th, fa, fh, fl = carve([(2 * T, F32), (3 * T, F32), (3 * T // 2, F16), (3 * T // 2, F16)])
        th = th.rearrange("p (k n) -> p k n", k=2)
        fa = fa.rearrange("p (k n) -> p k n", k=3)
        fh = fh.rearrange("p (k n) -> p k n", k=3)
        fl = fl.rearrange("p (k n) -> p k n", k=3)
        s1, p1h, p1l = carve([(2 * 4 * 384, F32), (768, F16), (768, F16)])
        s1 = s1.rearrange("p (b j n) -> p b j n", b=2, j=4)
        p1h = p1h.rearrange("p (k j n) -> p k j n", k=3, j=4)
        p1l = p1l.rearrange("p (k j n) -> p k j n", k=3, j=4)

        ident = con[:, K_ID:K_ID + 128]
        mask0 = con[:, K_M0:K_M0 + 384]
        bias1 = con[:, K_M1:K_M1 + 384]
        iota = con[:, K_IO:K_IO + 8]

        bank = [ctx.enter_context(nc.psum_tensor(f"bank{k}", [P, 512], F32)) for k in range(8)]
        misc = bank[2]

        def w_of(name, at, n):
            a = COLS[name] + at
            return whi[:, a:a + n], wlo[:, a:a + n]

        wm = whi[:, 0:2 * 2 * DC * 1536].bitcast(F32).rearrange("p (l c n) -> p l c n", l=2, c=DC)
        ha = wlo[:, 0:4096].bitcast(F32)
        hb = wlo[:, 4096:8192].bitcast(F32)
        had = wlo[:, 8192:8448].bitcast(F32)
        rcos = wlo[:, 8448:8960].bitcast(F32).rearrange("p (t n) -> p t n", t=TT)
        rsin = wlo[:, 8960:9472].bitcast(F32).rearrange("p (t n) -> p t n", t=TT)
        nsn = wlo[:, 9472:10240].bitcast(F32).rearrange("p (k n) -> p k n", k=3)
        nsw = wlo[:, 10240:11008].bitcast(F32).rearrange("p (k n) -> p k n", k=3)
        braw = wlo[0:2, 11008:11008 + 2 * NB].bitcast(F32)
        sc = wlo[:, 16384:16512].bitcast(F32).rearrange("p (l c n) -> p l c n", l=2, c=DC)
        st = wlo[:, 16512:16640].bitcast(F32).rearrange("p (l c n) -> p l c n", l=2, c=DC)
        gsb = wlo[0:B, 16640:16640 + 2 * 4 * D].bitcast(F32)
        gtmp = wlo[0:B, 18688:18688 + 2 * 4 * D].bitcast(F32)
        bhi = wlo[0:2, 20736:20736 + NB]
        blo = wlo[0:2, 20736 + NB:20736 + 2 * NB]

        ld_con = sem("ld_con")
        ld_c = sem("ld_c")
        ld_wm = sem("ld_wm")
        ld_w2 = sem("ld_w2")
        ld_rope = sem("ld_rope")
        ld_b = sem("ld_b")
        ld_sel = sem("ld_sel")
        set_tanh = sem("set_tanh")
        set_v = sem("set_v")
        set_mm = sem("set_mm")
        set_had = sem("set_had")
        set_hi = sem("set_hi")
        st_gates = sem("st_gates")
        had_step = sem("had_step")

        blk = nc.Block()
        with blk as block:
            @block.sync
            def _(sp):
                sp.dma_start(sc[:, :, :, :], ct_in).then_inc(ld_c, 16)
                sp.dma_start(wm[:, :, :, :], wmod).then_inc(ld_wm, 16)
                sp.dma_start(ha, w2t).then_inc(ld_w2, 16)
                sp.dma_start(had, hadm).then_inc(ld_w2, 16)
                sp.dma_start(con[:, :], cf).then_inc(ld_con, 16)
                sp.dma_start(rcos, rope[:, 0]).then_inc(ld_rope, 16)
                sp.dma_start(rsin, rope[:, 1]).then_inc(ld_rope, 16)
                sp.dma_start(nsn, nsc[0].partition_broadcast(P)).then_inc(ld_rope, 16)
                sp.dma_start(nsw, nsc[1].partition_broadcast(P)).then_inc(ld_rope, 16)
                sp.dma_start(braw, brow.partition_broadcast(2)).then_inc(ld_b, 16)
                sp.dma_start(sel[:, :], sel_in).then_inc(ld_sel, 16)
                sp.wait_ge(set_v, 16)
                sp.dma_start(gates_dram, gsb).then_inc(st_gates, 16)
                sp.wait_ge(st_gates, 16)
                sp.wait_ge(ld_con, 16)
                sp.wait_ge(ld_sel, 16)

            @block.scalar
            def _(act):
                act.wait_ge(ld_c, 16)
                nc.scalar.activation(st[:, :, :, :], sc[:, :, :, :], ACT.Tanh, scale=0.5).then_inc(set_tanh, 1)
                for q in range(4):
                    act.wait_ge(set_had, q + 1)
                    nc.scalar.activation(whi[:, NW + q * 512:NW + (q + 1) * 512], bank[4 + q][:, :], ACT.Copy,
                                         scale=WS / 32.0).then_inc(set_hi, 1)

            @block.tensor
            def _(pe):
                pe.wait_ge(set_v, 2)
                pe.wait_ge(ld_wm, 16)
                for l in range(2):
                    for k, part in enumerate((1, 0, 4, 3)):
                        for c2 in range(DC):
                            n = l * 8 + k * 2 + c2
                            for c in range(DC):
                                last = nc.tensor.matmul(bank[0][:, n * B:(n + 1) * B],
                                                        wm[:, l, c, part * D + c2 * P:part * D + (c2 + 1) * P],
                                                        st[:, l, c, :], start=(c == 0), stop=(c == DC - 1))
                last.then_inc(set_mm, 1)
                for l in range(2):
                    for k, part in enumerate((2, 5)):
                        for c in range(DC):
                            last = nc.tensor.matmul(bank[1 + l][0:B, k * D:(k + 1) * D], st[:, l, c, :],
                                                    wm[:, l, c, part * D:(part + 1) * D],
                                                    start=(c == 0), stop=(c == DC - 1))
                last.then_inc(set_mm, 1)
                pe.wait_ge(set_v, 18)
                pe.wait_ge(ld_w2, 32)
                for q in range(4):
                    nc.tensor.matmul(bank[4 + q][:, :], had, hb[:, q * 512:(q + 1) * 512],
                                     start=True, stop=True).then_inc(set_had, 1)

            @block.gpsimd
            def _(pool):
                pool.memset(half, -0.5)
                pool.memset(ones[:, :], 1.0)
                pool.memset(c17[:, :, 8:9], 1.0)

            @block.vector
            def _(dve):
                n = [0]

                def link(ins):
                    n[0] += 1
                    ins.then_inc(set_v, 1)
                    dve.wait_ge(set_v, n[0])

                dve.wait_ge(set_tanh, 1)
                link(nc.vector.tensor_scalar(st[:, :, :, :], st[:, :, :, :], 1.0, 0.5, ALU.add, ALU.mult))
                link(nc.vector.tensor_tensor(st[:, :, :, :], st[:, :, :, :], sc[:, :, :, :], ALU.mult))
                dve.wait_ge(set_mm, 1)
                src = bank[0][:, 0:16 * B].rearrange("p (n b) -> p b n", b=B)
                link(nc.vector.tensor_copy(modt[:, :, :], src))
                for l in range(2):
                    for k in (0, 2):
                        a = l * 8 + k * 2
                        link(nc.vector.tensor_scalar(modt[:, :, a:a + 2], modt[:, :, a:a + 2], 1.0, None, ALU.add))
                dve.wait_ge(set_mm, 2)
                for l in range(2):
                    g = bank[1 + l][0:B, :]
                    a, b = gsb[:, l * 512:(l + 1) * 512], gtmp[:, l * 512:(l + 1) * 512]
                    link(nc.vector.tensor_scalar(a, g, 0.0, 2.0 / WS, ALU.is_ge, ALU.mult))
                    link(nc.vector.tensor_scalar(a, a, -1.0 / WS, None, ALU.add))
                    link(nc.vector.tensor_scalar(b, g, -1.0, None, ALU.mult))
                    link(nc.vector.tensor_tensor(b, b, g, ALU.max))
                link(nc.vector.scalar_tensor_tensor(out=gsb, in0=gtmp, scalar=0.25, in1=gsb,
                                                    op0=ALU.max, op1=ALU.mult))
                assert n[0] == 16, n[0]
                dve.wait_ge(ld_w2, 32)
                bufs = [(ha, hb), (hb, ha), (ha, hb)]
                for k, (src, dst) in enumerate(bufs):
                    v = [z.rearrange("p (o two i) -> p o two i", two=2, i=D << k) for z in (src, dst)]
                    ins = nc.vector.tensor_tensor(v[1][:, :, 0, :], v[0][:, :, 0, :], v[0][:, :, 1, :], ALU.add)
                    ins2 = nc.vector.tensor_tensor(v[1][:, :, 1, :], v[0][:, :, 0, :], v[0][:, :, 1, :], ALU.subtract)
                    if k < 2:
                        ins2.then_inc(had_step, 1)
                        dve.wait_ge(had_step, k + 1)
                        continue
                    ins2.then_inc(set_v, 2)
                    n[0] += 2
                dve.wait_ge(ld_rope, 64)
                for k in range(3):
                    for t in range(TT):
                        nc.vector.tensor_tensor(ropec[:, t, k, :], rcos[:, t, :], nsn[:, k, :], ALU.mult)
                        nc.vector.tensor_tensor(ropes[:, t, k, :], rsin[:, t, :], nsw[:, k, :], ALU.mult)
                dve.wait_ge(ld_b, 16)
                dve.wait_ge(ld_con, 16)
                link(nc.vector.tensor_scalar(bhi, braw, WS, None, ALU.mult))
                link(nc.vector.scalar_tensor_tensor(out=blo, in0=braw, scalar=WS, in1=bhi,
                                                    op0=ALU.mult, op1=ALU.subtract))
                link(nc.vector.tensor_scalar(bhi, bhi, con[0:2, K_BS:K_BS + 1], None, ALU.mult))
                link(nc.vector.scalar_tensor_tensor(out=brows[:, :], in0=blo, scalar=con[0:2, K_BS + 1:K_BS + 2],
                                                    in1=bhi, op0=ALU.mult, op1=ALU.add))
                for q in range(4):
                    dve.wait_ge(set_hi, q + 1)
                    a = slice(NW + q * 512, NW + (q + 1) * 512)
                    nc.vector.scalar_tensor_tensor(out=wlo[:, a], in0=bank[4 + q][:, :], scalar=WS / 32.0,
                                                   in1=whi[:, a], op0=ALU.mult, op1=ALU.subtract)

        RING = 3
        stage = [arena[:, k * CHUNK:(k + 1) * CHUNK] for k in range(RING)]
        assert RING * CHUNK <= NARENA
        ld_stage = [sem(f"ld_stage{k}") for k in range(RING)]
        w_hi = sem("w_hi")
        w_lo = sem("w_lo")

        ld_x = [signal(f"ld_x{s}", 1, 16) for s in range(2)]
        ld_g = [signal(f"ld_g{s}", 2, 16) for s in range(2)]
        st_x = [signal(f"st_x{s}", 1, 16) for s in range(2)]
        ln_stats = signal("ln_stats", 8)
        ln_rstd = signal("ln_rstd", 8)
        ln_norm = signal("ln_norm", 8)
        h_hi = signal("h_hi", 8)
        h_lo = signal("h_lo", 8)
        misc_mm = signal("misc_mm", len(MISC))
        misc_hi = signal("misc_hi", len(MISC_HI))
        misc_free = signal("misc_free", len(MISC))
        qkv_mm = signal("qkv_mm", 2 * U0)
        qkv_act = signal("qkv_act", 2 * U0)
        rope_mul = signal("rope_mul", 2 * U0)
        rope_sum = signal("rope_sum", 2 * U0)
        qk_rstd = signal("qk_rstd", U0)
        k_norm = signal("k_norm", 2 * U0)
        s_mm = signal("s_mm", 2 * U0)
        s_max = signal("s_max", 4 * U0)
        s_shift = signal("s_shift", U0)
        s_exp = signal("s_exp", 4 * U0)
        p_norm = signal("p_norm", 4 * U0)
        pt_mm = signal("pt_mm", 2 * U0)
        pt_hi = signal("pt_hi", 2 * U0)
        pt_lo = signal("pt_lo", 2 * U0)
        enc_mm = signal("enc_mm", U0)
        enc_hi = signal("enc_hi", U0)
        enc_lo = signal("enc_lo", U0)
        o_mm = signal("o_mm", 8)
        o_read = signal("o_read", 8)
        NGU = 2 * J0 + 2 * J1
        gu_mm = signal("gu_mm", NGU)
        gu_tanh = signal("gu_tanh", NGU)
        gu_read = signal("gu_read", NGU)
        ce_mm = signal("ce_mm", 2 * J0)
        ce_read = signal("ce_read", 2 * J0)
        hid_hi = signal("hid_hi", NGU)
        hid_lo = signal("hid_lo", NGU)
        rt_exp = signal("rt_exp", 2)
        rt_sub = signal("rt_sub", 2)
        c_ready = signal("c_ready", 2)
        qm_ready = signal("qm_ready", 2)
        a_mm = signal("a_mm", 3 * W1G)
        a_max = signal("a_max", 8 * W1G)
        a_shift = signal("a_shift", 2 * W1G)
        a_exp = signal("a_exp", 8 * W1G)
        at_mm = signal("at_mm", 3 * W1G)
        at_hi = signal("at_hi", 3 * W1G)
        at_lo = signal("at_lo", 3 * W1G)
        v_chain = signal("v_chain", CHAIN)
        g_chain = signal("g_chain", 2 * U0 + 8)

        passed_pool = sem("passed_pool")
        passed_dve = sem("passed_dve")

        with nc.Block() as block:
            @block.sync
            def _(sp):
                for n in range(NCHUNK):
                    if n >= RING:
                        sp.wait_ge(w_lo, n - RING + 1)
                    sp.dma_start(stage[n % RING], wall[:, n * CHUNK:(n + 1) * CHUNK]).then_inc(ld_stage[n % RING], 16)
                for z in signals:
                    sp.sem_inc(z.handle, z.per * z.unit)

            @block.scalar
            def _(act):
                for n in range(NCHUNK):
                    act.wait_ge(ld_stage[n % RING], 16 * (n // RING + 1))
                    nc.scalar.activation(whi[:, n * CHUNK:(n + 1) * CHUNK], stage[n % RING], ACT.Copy,
                                         scale=WS).then_inc(w_hi, 1)

            @block.vector
            def _(dve):
                for n in range(NCHUNK):
                    dve.wait_ge(w_hi, n + 1)
                    nc.vector.scalar_tensor_tensor(out=wlo[:, n * CHUNK:(n + 1) * CHUNK], in0=stage[n % RING],
                                                   scalar=WS, in1=whi[:, n * CHUNK:(n + 1) * CHUNK],
                                                   op0=ALU.mult, op1=ALU.subtract).then_inc(w_lo, 1)

        def n_ln(k, s):
            return 2 * k + s + 1

        def n_o(stage_, s):
            return 2 * stage_ + s + 1

        def n_gu(f, v):
            return (2 * J0 if f else 0) + v + 1

        def ff_dims(f):
            return (J1 if f else J0), ("w1" if f else "g"), ("w3" if f else "u"), ("w2" if f else "d")

        o_bank = {(0, 0): 7, (0, 1): 7, (1, 0): 7, (1, 1): 6, (2, 0): 7, (2, 1): 7, (3, 0): 7, (3, 1): 6}

        with nc.Block() as block:
            @block.sync
            def _(sp):
                with sp.Fori(0, NPAIR) as i:
                    for s in range(2):
                        sp.wait_ge(o_read.handle, o_read.count(i, n_o(0, s) - 8))
                        sp.dma_start(xin[:, s], x_in[2 * i + s].rearrange("(t p) d -> p t d", p=P)).then_inc(ld_x[s].handle, 16)
                    for l in range(2):
                        for s in range(2):
                            if l == 0:
                                sp.wait_ge(o_read.handle, o_read.count(i, n_o(3, s) - 8))
                            else:
                                sp.wait_ge(o_read.handle, o_read.count(i, n_o(1, s)))
                            sp.dma_start(gate[:, s], gates_dram[2 * i + s, l * 512:(l + 1) * 512]
                                         .rearrange("(k n) -> k n", k=2).partition_broadcast(P)).then_inc(ld_g[s].handle, 16)

            @block.tensor
            def _(pe):
                def mm3(dst, lhs, rhs, start, stop, skip=False):
                    nc.tensor.matmul(dst, lhs[0], rhs[0], start=start, stop=False, skip_group_check=skip)
                    nc.tensor.matmul(dst, lhs[0], rhs[1], start=False, stop=False, skip_group_check=skip)
                    return nc.tensor.matmul(dst, lhs[1], rhs[0], start=False, stop=stop, skip_group_check=skip)

                with pe.Fori(0, NPAIR) as i:
                    def wait(z, n):
                        pe.wait_ge(z.handle, z.count(i, n))

                    def misc_begin(key):
                        wait(misc_free, MISC[key] - 1)

                    def transposes4(src):
                        for c in range(DC):
                            for t in range(TT):
                                last = nc.tensor.transpose(misc[:, c * T + t * P:c * T + (t + 1) * P],
                                                           src[:, t, c * P:(c + 1) * P], ident)
                        last.then_inc(misc_mm.handle, 1)

                    def h_of(s, c, t=None):
                        if t is None:
                            return hth[:, s, c, :], htl[:, s, c, :]
                        return hth[:, s, c, t * P:(t + 1) * P], htl[:, s, c, t * P:(t + 1) * P]

                    def at0(u):
                        if 1 <= u <= U0:
                            for t in range(TT):
                                misc_begin(("t1", u - 1, t))
                                wait(rope_sum, 2 * (u - 1) + t + 1)
                                wait(k_norm, 2 * (u - 1) + t + 1)
                                for k in range(3):
                                    last = nc.tensor.transpose(misc[:, k * P:(k + 1) * P], ra[:, t, k, :], ident)
                                last.then_inc(misc_mm.handle, 1)
                        if 2 <= u <= U0 + 1:
                            wait(p_norm, 4 * (u - 1))
                            wait(pt_lo, 2 * (u - 2))
                            for k in range(2):
                                last = nc.tensor.transpose(bank[5][:, k * P:(k + 1) * P], smx[:, k, 0:P], ident)
                            last.then_inc(pt_mm.handle, 1)
                            wait(pt_lo, 2 * (u - 2) + 1)
                            for kt in range(2):
                                for k in range(2):
                                    last = nc.tensor.transpose(bank[5][:, (2 * kt + k) * P:(2 * kt + k + 1) * P],
                                                               smx[:, k, P + kt * P:P + (kt + 1) * P], ident)
                            last.then_inc(pt_mm.handle, 1)
                        if u < U0:
                            s, g = divmod(u, NKV)
                            if g == 0:
                                wait(h_lo, n_ln(0, s))
                            for t in range(TT):
                                wait(rope_mul, 2 * (u - 1) + t + 1)
                                for c in range(DC):
                                    last = mm3(bank[t][:, :], h_of(s, c, t), w_of("qkv", c * 4096 + g * 512, 512),
                                               c == 0, c == DC - 1)
                                last.then_inc(qkv_mm.handle, 1)
                        if 1 <= u <= U0:
                            wait(misc_free, MISC[("t1", u - 1, 1)])
                            wait(s_max, 4 * (u - 1))
                            for k in range(2):
                                last = mm3(bank[3][:, k * P:(k + 1) * P], (qkh[:, k, 0:P], qkl[:, k, 0:P]),
                                           (qkh[:, 2, 0:P], qkl[:, 2, 0:P]), True, True)
                            last.then_inc(s_mm.handle, 1)
                            for k in range(2):
                                last = mm3(bank[4][:, k * T:(k + 1) * T], (qkh[:, k, P:T], qkl[:, k, P:T]),
                                           (qkh[:, 2, :], qkl[:, 2, :]), True, True)
                            last.then_inc(s_mm.handle, 1)
                        if 3 <= u:
                            s, g = divmod(u - 3, NKV)
                            wait(enc_lo, u - 2)
                            if g == 0:
                                wait(o_read, n_o(3, 0) - 8 if s == 0 else n_o(0, 0))
                            for k in range(2):
                                for t in range(TT):
                                    first = g == 0 and k == 0 and t == 0
                                    last = mm3(bank[7][:, t * D:(t + 1) * D], (ench[:, t, k, :], encl[:, t, k, :]),
                                               w_of("o", (2 * g + k) * D, D), first, g == NKV - 1 and k == 1, skip=True)
                            if g == NKV - 1:
                                last.then_inc(o_mm.handle, 1)
                        if 2 <= u <= U0 + 1:
                            wait(pt_lo, 2 * (u - 1))
                            wait(enc_lo, u - 2)
                            if u == 2:
                                wait(o_read, 0)
                            v = (u - 2) % 4
                            mm3(bank[6][:, 0:T], (vh0[:, v, 0, :], vl0[:, v, 0, :]),
                                (pth[:, 0:2, :], ptl[:, 0:2, :]), True, True)
                            mm3(bank[6][:, T:2 * T], (vh0[:, v, 0, :], vl0[:, v, 0, :]),
                                (pth[:, 2:4, :], ptl[:, 2:4, :]), True, False)
                            last = mm3(bank[6][:, T:2 * T], (vh0[:, v, 1, :], vl0[:, v, 1, :]),
                                       (pth[:, 4:6, :], ptl[:, 4:6, :]), False, True)
                            last.then_inc(enc_mm.handle, 1)

                    def ff(f, v):
                        J, wg, wu, wd = ff_dims(f)
                        stage_ = 3 if f else 1
                        if v < 2 * J:
                            s, j = divmod(v, J)
                            n = n_gu(f, v)
                            if j == 0:
                                wait(h_lo, n_ln(3 if f else 1, s))
                            wait(gu_read, n - 2)
                            bk = bank[(n - 1) % 2]
                            bias = not f and j >= JB
                            for k, name in enumerate((wg, wu)):
                                for c in range(DC):
                                    last = mm3(bk[:, k * T:(k + 1) * T],
                                               w_of(name, c * J * P + j * P, P), h_of(s, c), c == 0,
                                               c == DC - 1 and not bias)
                                if bias:
                                    a = (BG, BU)[k] + (j - JB) * P
                                    last = nc.tensor.matmul(bk[:, k * T:(k + 1) * T], brows[:, a:a + P], ones[:, :],
                                                            start=False, stop=True)
                            last.then_inc(gu_mm.handle, 1)
                            if not f:
                                if j == 0:
                                    wait(misc_free, MISC[("ct", s)])
                                wait(ce_read, v + 1 - 2)
                                nc.tensor.matmul(bank[3 + v % 2][:, 0:T], sel[:, j * P:(j + 1) * P], ctt[:, s, :],
                                                 start=True, stop=True).then_inc(ce_mm.handle, 1)
                        if v >= 2:
                            s, j = divmod(v - 2, J)
                            n = n_gu(f, v - 2)
                            wait(hid_lo, n)
                            ob = bank[o_bank[(stage_, s)]]
                            if j == 0:
                                if s == 0:
                                    wait(o_read, n_o(stage_ - 1, 1))
                                else:
                                    wait(o_read, n_o(stage_ - 2, 1) if f == 0 else n_o(1, 1))
                            z = (n - 1) % 3
                            for t in range(TT):
                                last = mm3(ob[:, t * D:(t + 1) * D],
                                           (fh[:, z, t * P:(t + 1) * P], fl[:, z, t * P:(t + 1) * P]),
                                           w_of(wd, j * D, D), j == 0 and t == 0, f == 1 and j == J - 1, skip=True)
                                if not f and j == J - 1:
                                    last = nc.tensor.matmul(ob[:, t * D:(t + 1) * D], ones[:, 0:P], brows[:, BD:BD + D],
                                                            start=False, stop=True, skip_group_check=True)
                            if j == J - 1:
                                last.then_inc(o_mm.handle, 1)

                    def at1(w):
                        if w < W1G:
                            s, gr = divmod(w, 8)
                            c, g = divmod(gr, 4)
                            if gr == 0:
                                wait(qm_ready, s + 1)
                                wait(misc_free, MISC[("k1", s)])
                            wait(a_max, 8 * w)
                            rows = slice(32 * g, 32 * g + 32)
                            for j in range(4):
                                q = slice(c * T, c * T + P)
                                last = mm3(bank[0][:, j * P:(j + 1) * P], (qmh[rows, j, q], qml[rows, j, q]),
                                           (k1h[rows, s, c, 0:P], k1l[rows, s, c, 0:P]), True, True)
                            last.then_inc(a_mm.handle, 1)
                            for j in range(4):
                                q = slice(c * T + P, (c + 1) * T)
                                last = mm3(bank[(1, 3)[j // 2]][:, j % 2 * T:(j % 2 + 1) * T],
                                           (qmh[rows, j, q], qml[rows, j, q]),
                                           (k1h[rows, s, c, :], k1l[rows, s, c, :]), True, True)
                                if j % 2:
                                    last.then_inc(a_mm.handle, 1)
                        if 2 <= w:
                            s, gr = divmod(w - 2, 8)
                            wait(at_lo, 3 * (w - 1))
                            if gr == 0:
                                wait(misc_free, MISC[("v1", s)])
                                wait(o_read, n_o(1, 0) if s == 0 else n_o(2, 0))
                            for j in range(4):
                                d = (4 * gr + j) * HD1
                                for t in range(TT):
                                    for kt in range(t + 1):
                                        b = t + kt
                                        last = mm3(bank[7][:, t * D + d:t * D + d + HD1],
                                                   (p1h[:, b, j, :], p1l[:, b, j, :]),
                                                   (v1h[:, s, kt, d:d + HD1], v1l[:, s, kt, d:d + HD1]),
                                                   gr == 0 and j == 0 and t == 0, kt == t, skip=True)
                            if gr == 7:
                                last.then_inc(o_mm.handle, 1)
                        if 1 <= w <= W1G:
                            y = (w - 1) % 2
                            for b in range(3):
                                if b == 0:
                                    wait(a_exp, 8 * (w - 1) + 4)
                                elif b == 1:
                                    wait(a_exp, 8 * w)
                                wait(at_lo, 3 * (w - 2) + b + 1)
                                if w == 1 and b == 2:
                                    wait(o_read, n_o(1, 1))
                                for j in range(4):
                                    last = nc.tensor.transpose(bank[4 + b][:, j * P:(j + 1) * P],
                                                               s1[:, y, j, b * P:(b + 1) * P], ident)
                                last.then_inc(at_mm.handle, 1)

                    for item in ORDER:
                        kind = item[0]
                        if kind == "at0":
                            at0(item[1])
                        elif kind in ("ff0", "ff1"):
                            ff(int(kind == "ff1"), item[1])
                        elif kind == "at1":
                            at1(item[1])
                        elif kind == "lnc":
                            misc_begin(item)
                            wait(ln_norm, n_ln(item[1], item[2]))
                            transposes4(xn)
                        elif kind == "rt":
                            misc_begin(item)
                            s = item[1]
                            wait(h_lo, n_ln(1, s))
                            for t in range(TT):
                                for c in range(DC):
                                    last = mm3(misc[:, t * EXPERTS:(t + 1) * EXPERTS], h_of(s, c, t),
                                               w_of("r", c * EXPERTS, EXPERTS), c == 0, c == DC - 1)
                            last.then_inc(misc_mm.handle, 1)
                        elif kind == "ct":
                            misc_begin(item)
                            wait(c_ready, item[1] + 1)
                            for t in range(TT):
                                last = nc.tensor.transpose(misc[0:17, t * P:(t + 1) * P], c17[:, t, :], ident)
                            last.then_inc(misc_mm.handle, 1)
                        elif kind in ("q1", "k1"):
                            misc_begin(item)
                            s = item[1]
                            wait(h_lo, n_ln(2, s))
                            a = 0 if kind == "q1" else D
                            for c2 in range(DC):
                                for c in range(DC):
                                    mm3(misc[:, c2 * T:(c2 + 1) * T], w_of("a1", c * 3 * D + a + c2 * P, P),
                                        h_of(s, c), c == 0, False)
                                b = BA + a + c2 * P
                                last = nc.tensor.matmul(misc[:, c2 * T:(c2 + 1) * T], brows[:, b:b + P], ones[:, :],
                                                        start=False, stop=True)
                            last.then_inc(misc_mm.handle, 1)
                        elif kind == "v1":
                            misc_begin(item)
                            s = item[1]
                            wait(h_lo, n_ln(2, s))
                            for t in range(TT):
                                for c in range(DC):
                                    mm3(misc[:, t * D:(t + 1) * D], h_of(s, c, t),
                                        w_of("a1", c * 3 * D + 2 * D, D), c == 0, False)
                                last = nc.tensor.matmul(misc[:, t * D:(t + 1) * D], ones[:, 0:P],
                                                        brows[:, BA + 2 * D:BA + 3 * D], start=False, stop=True)
                            last.then_inc(misc_mm.handle, 1)
                        elif kind == "at":
                            misc_begin(item)
                            wait(o_read, n_o(2, item[1]))
                            transposes4(xn)
                        elif kind == "pj":
                            misc_begin(item)
                            wait(misc_free, MISC[("at", item[1])])
                            for t in range(TT):
                                for c in range(DC):
                                    q = slice(c * T + t * P, c * T + (t + 1) * P)
                                    mm3(misc[:, t * D:(t + 1) * D], (q1h[:, q], q1l[:, q]), w_of("p1", c * D, D),
                                        c == 0, False)
                                last = nc.tensor.matmul(misc[:, t * D:(t + 1) * D], ones[:, 0:P],
                                                        brows[:, BP:BP + D], start=False, stop=True)
                            last.then_inc(misc_mm.handle, 1)

            @block.scalar
            def _(act):
                with act.Fori(0, NPAIR) as i:
                    def wait(z, n):
                        act.wait_ge(z.handle, z.count(i, n))

                    def copy_hi(dst, src, key, scale):
                        wait(misc_mm, MISC[key])
                        nc.scalar.activation(dst, src, ACT.Copy, scale=scale).then_inc(misc_hi.handle, 1)

                    for item in ORDER:
                        kind = item[0]
                        if kind == "at0":
                            u = item[1]
                            if 1 <= u <= U0:
                                for t in range(TT):
                                    copy_hi(qkh[:, :, t * P:(t + 1) * P],
                                            misc[:, 0:3 * P].rearrange("p (k n) -> p k n", k=3),
                                            ("t1", u - 1, t), 1.0 / WS)
                            if 2 <= u <= U0 + 1:
                                for b, (lo, hi) in enumerate(((0, 2), (2, 6))):
                                    wait(pt_mm, 2 * (u - 2) + b + 1)
                                    nc.scalar.activation(pth[:, lo:hi, :], bank[5][:, 0:(hi - lo) * P]
                                                         .rearrange("p (k n) -> p k n", n=P),
                                                         ACT.Copy).then_inc(pt_hi.handle, 1)
                            if u < U0:
                                for t in range(TT):
                                    wait(qkv_mm, 2 * u + t + 1)
                                    nc.scalar.activation(vh0[:, u % 4, t, :], bank[t][:, 3 * P:4 * P], ACT.Copy,
                                                         scale=1.0 / WS)
                                    for k in range(3):
                                        last = nc.scalar.activation(rb[:, t, k, :], bank[t][:, k * P:(k + 1) * P], ACT.Square,
                                                                    accum_out=ss[:, 3 * t + k:3 * t + k + 1])
                                    last.then_inc(qkv_act.handle, 1)
                            if 1 <= u <= U0:
                                wait(s_shift, u)
                                y = (u - 1) % 2
                                for t in range(TT):
                                    for k in range(2):
                                        a = smx[:, k, t * P:t * P + (t + 1) * P]
                                        nc.scalar.activation(a, a, ACT.Exp, bias=nb0[:, y, 2 * t + k:2 * t + k + 1],
                                                             scale=rs0[:, (u - 1) % 4, 3 * t + k:3 * t + k + 1],
                                                             accum_out=sm0[:, y, 2 * t + k:2 * t + k + 1])\
                                            .then_inc(s_exp.handle, 1)
                            if 2 <= u <= U0 + 1:
                                wait(enc_mm, u - 1)
                                nc.scalar.activation(ench[:, :, :, :].rearrange("p t k n -> p (t k n)"), bank[6][:, :],
                                                     ACT.Copy).then_inc(enc_hi.handle, 1)
                        elif kind in ("ff0", "ff1"):
                            f, v = int(kind == "ff1"), item[1]
                            J = ff_dims(f)[0]
                            if v < 2 * J:
                                n = n_gu(f, v)
                                wait(gu_mm, n)
                                nc.scalar.activation(th[:, (n - 1) % 2, :], bank[(n - 1) % 2][:, 0:T], ACT.Tanh,
                                                     scale=0.5 / WS).then_inc(gu_tanh.handle, 1)
                            if 1 <= v <= 2 * J:
                                n = n_gu(f, v - 1)
                                z = (n - 1) % 3
                                if f:
                                    wait(gu_read, n)
                                else:
                                    wait(ce_read, v)
                                nc.scalar.activation(fh[:, z, :], fa[:, z, :], ACT.Copy).then_inc(hid_hi.handle, 1)
                        elif kind == "at1":
                            w = item[1]
                            if w < W1G:
                                s, gr = divmod(w, 8)
                                y = w % 2
                                for t in range(TT):
                                    wait(a_shift, 2 * w + t + 1)
                                    for j in range(4):
                                        a = s1[:, y, j, t * P:t * P + (t + 1) * P]
                                        nc.scalar.activation(a, a, ACT.Exp, bias=nb1[:, y, 4 * t + j:4 * t + j + 1],
                                                             accum_out=sum1[:, s, t, 4 * gr + j:4 * gr + j + 1])\
                                            .then_inc(a_exp.handle, 1)
                            if 1 <= w <= W1G:
                                for b in range(3):
                                    wait(at_mm, 3 * (w - 1) + b + 1)
                                    nc.scalar.activation(p1h[:, b, :, :].rearrange("p j n -> p (j n)"),
                                                         bank[4 + b][:, :], ACT.Copy).then_inc(at_hi.handle, 1)
                        elif kind == "lnc":
                            k, s = item[1:]
                            wait(misc_free, MISC[item])
                            nc.scalar.activation(hth[:, s].rearrange("p c n -> p (c n)"), hf[:, :],
                                                 ACT.Copy).then_inc(h_hi.handle, 1)
                        elif kind == "rt":
                            wait(rt_sub, item[1] + 1)
                            nc.scalar.activation(rt_e, rt_a, ACT.Exp).then_inc(rt_exp.handle, 1)
                        elif kind == "q1":
                            copy_hi(q1h[:, :], misc[:, :], item, 1.0 / WS)
                        elif kind == "k1":
                            copy_hi(k1h[:, item[1]].rearrange("p c n -> p (c n)"), misc[:, :], item, 1.0 / WS)
                        elif kind == "v1":
                            copy_hi(v1h[:, item[1]].rearrange("p c n -> p (c n)"), misc[:, :], item, 1.0 / WS)
                        elif kind == "at":
                            copy_hi(q1h[:, :], misc[:, :], item, 1.0)
                        elif kind == "resf" and item[1] == 1:
                            s = item[2]
                            wait(o_read, n_o(3, s))
                            act.dma_start(out[2 * i + s].rearrange("(t p) d -> p t d", p=P), xs[:, s])\
                               .then_inc(st_x[s].handle, 16)
                for s in range(2):
                    act.wait_ge(st_x[s].handle, 16 * (NPAIR + 1))

            @block.gpsimd
            def _(pool):
                with pool.Fori(0, NPAIR) as i:
                    chained = [0]

                    def wait(z, n):
                        pool.wait_ge(z.handle, z.count(i, n))

                    def link(ins):
                        chained[0] += 1
                        ins.then_inc(g_chain.handle, 1)
                        wait(g_chain, chained[0])

                    for item in ORDER:
                        kind = item[0]
                        if kind == "lna":
                            wait(ln_stats, n_ln(item[1], item[2]))
                            pool.sem_inc(passed_pool, 1)
                            link(nc.gpsimd.tensor_scalar(lv, mv[:, :, 1], 1e-5, None, ALU.add))
                            nc.gpsimd.tensor_tensor(lr[:, 0:TT], lv, half[:, 0:TT], ALU.pow).then_inc(ln_rstd.handle, 1)
                        elif kind == "at0" and item[1] < U0:
                            u = item[1]
                            wait(qkv_act, 2 * (u + 1))
                            pool.sem_inc(passed_pool, 1)
                            link(nc.gpsimd.tensor_scalar(ms, ss, 1.0 / (HD * WS * WS), 1e-6, ALU.mult, ALU.add))
                            link(nc.gpsimd.tensor_tensor(r0[:, u % 2, :], ms, half[:, 0:6], ALU.pow))
                            pool.sem_inc(passed_pool, 1)
                            nc.gpsimd.tensor_scalar(rs0[:, u % 4, :], r0[:, u % 2, :], ATT_SCALE, None, ALU.mult)\
                                .then_inc(qk_rstd.handle, 1)
                            for t in range(TT):
                                wait(rope_mul, 2 * u + t + 1)
                                a, b = (z[:, t].rearrange("p k h -> p (k h)") for z in (ra, rb))
                                nc.gpsimd.tensor_tensor(a, a, b, ALU.add).then_inc(rope_sum.handle, 1)
                        elif kind in ("ff0", "ff1"):
                            f, v = int(kind == "ff1"), item[1]
                            J = ff_dims(f)[0]
                            if 1 <= v <= 2 * J:
                                n = n_gu(f, v - 1)
                                z = (n - 1) % 3
                                wait(hid_hi, n)
                                nc.gpsimd.tensor_tensor(fl[:, z, :], fa[:, z, :], fh[:, z, :], ALU.subtract)\
                                    .then_inc(hid_lo.handle, 1)
                    assert chained[0] == g_chain.per, chained[0]

            @block.vector
            def _(dve):
                with dve.Fori(0, NPAIR) as i:
                    chained = [0]

                    def wait(z, n):
                        dve.wait_ge(z.handle, z.count(i, n))

                    def link(ins):
                        chained[0] += 1
                        ins.then_inc(v_chain.handle, 1)
                        wait(v_chain, chained[0])

                    def split_lo(dst, src, hi, key, scale):
                        wait(misc_hi, MISC_HI[key])
                        nc.vector.scalar_tensor_tensor(out=dst, in0=src, scalar=scale, in1=hi, op0=ALU.mult,
                                                       op1=ALU.subtract).then_inc(misc_free.handle, 1)

                    def residual(ps, s, k, into, base):
                        tmp = hf[:, :].rearrange("p (t d) -> p t d", t=TT)
                        g = gate[:, s, k:k + 1, :].to_broadcast([P, TT, D])
                        n = nc.vector.tensor_tensor(tmp, ps[:, :].rearrange("p (t d) -> p t d", t=TT), g, ALU.mult)
                        return n, lambda: nc.vector.tensor_tensor(into, tmp, base, ALU.add)

                    def at0(u):
                        if 1 <= u <= U0:
                            for t in range(TT):
                                c = slice(t * P, (t + 1) * P)
                                split_lo(qkl[:, :, c], misc[:, 0:3 * P].rearrange("p (k n) -> p k n", k=3),
                                         qkh[:, :, c], ("t1", u - 1, t), 1.0 / WS)
                        if 2 <= u <= U0 + 1:
                            for b, (lo, hi) in enumerate(((0, 2), (2, 6))):
                                wait(pt_hi, 2 * (u - 2) + b + 1)
                                nc.vector.tensor_tensor(ptl[:, lo:hi, :], bank[5][:, 0:(hi - lo) * P]
                                                        .rearrange("p (k n) -> p k n", n=P), pth[:, lo:hi, :],
                                                        ALU.subtract).then_inc(pt_lo.handle, 1)
                        if u < U0:
                            for t in range(TT):
                                wait(qkv_act, 2 * u + t + 1)
                                nc.vector.scalar_tensor_tensor(out=vl0[:, u % 4, t, :], in0=bank[t][:, 3 * P:4 * P],
                                                               scalar=1.0 / WS, in1=vh0[:, u % 4, t, :],
                                                               op0=ALU.mult, op1=ALU.subtract)
                                src = bank[t][:, 0:3 * P].rearrange("p (k h) -> p k h", k=3)
                                nc.vector.tensor_tensor(ra[:, t], src, ropec[:, t], ALU.mult)
                                hh = HD // 2
                                nc.vector.tensor_tensor(rb[:, t, :, 0:hh], src[:, :, hh:HD], ropes[:, t, :, 0:hh], ALU.mult)
                                nc.vector.tensor_tensor(rb[:, t, :, hh:HD], src[:, :, 0:hh], ropes[:, t, :, hh:HD], ALU.mult)\
                                    .then_inc(rope_mul.handle, 1)
                        if 1 <= u <= U0:
                            y = (u - 1) % 2
                            for t in range(TT):
                                wait(s_mm, 2 * (u - 1) + t + 1)
                                dve.sem_inc(passed_dve, 1)
                                n = (t + 1) * P
                                for k in range(2):
                                    nc.vector.tensor_tensor_reduce(
                                        out=smx[:, k, t * P:t * P + n], in0=bank[3 + t][:, k * n:(k + 1) * n],
                                        in1=mask0[:, t * P:t * P + n], scale=1.0, scalar=-3e38, op0=ALU.add,
                                        op1=ALU.max, accum_out=mx0[:, y, 2 * t + k:2 * t + k + 1]).then_inc(s_max.handle, 1)
                            wait(s_max, 4 * u)
                            wait(qk_rstd, u)
                            nc.vector.scalar_tensor_tensor(
                                out=nb0[:, y, :].rearrange("p (t k) -> p t k", t=TT),
                                in0=mx0[:, y, :].rearrange("p (t k) -> p t k", t=TT), scalar=-1.0,
                                in1=rs0[:, (u - 1) % 4, :].rearrange("p (t k) -> p t k", t=TT)[:, :, 0:2],
                                op0=ALU.mult, op1=ALU.mult).then_inc(s_shift.handle, 1)
                        if 2 <= u <= U0 + 1:
                            wait(enc_hi, u - 1)
                            nc.vector.tensor_tensor(encl[:, :, :, :].rearrange("p t k n -> p (t k n)"), bank[6][:, :],
                                                    ench[:, :, :, :].rearrange("p t k n -> p (t k n)"),
                                                    ALU.subtract).then_inc(enc_lo.handle, 1)
                        if u < U0:
                            wait(qk_rstd, u + 1)
                            for t in range(TT):
                                wait(rope_sum, 2 * u + t + 1)
                                nc.vector.tensor_scalar(ra[:, t, 2, :], ra[:, t, 2, :],
                                                        r0[:, u % 2, 3 * t + 2:3 * t + 3], None,
                                                        ALU.mult).then_inc(k_norm.handle, 1)
                        if 1 <= u <= U0:
                            y = (u - 1) % 2
                            wait(s_exp, 4 * u)
                            link(nc.vector.reciprocal(ri0[:, y, :], sm0[:, y, :]))
                            for t in range(TT):
                                for k in range(2):
                                    a = smx[:, k, t * P:t * P + (t + 1) * P]
                                    nc.vector.tensor_scalar(a, a, ri0[:, y, 2 * t + k:2 * t + k + 1], None,
                                                            ALU.mult).then_inc(p_norm.handle, 1)

                    def ff(f, v):
                        J = ff_dims(f)[0]
                        if v >= 2 * J:
                            return
                        n = n_gu(f, v)
                        z, bk = (n - 1) % 3, bank[(n - 1) % 2]
                        wait(gu_tanh, n)
                        link(nc.vector.scalar_tensor_tensor(out=fa[:, z, :], in0=th[:, (n - 1) % 2, :], scalar=1.0,
                                                            in1=bk[:, 0:T], op0=ALU.add, op1=ALU.mult))
                        nc.vector.scalar_tensor_tensor(out=fa[:, z, :], in0=fa[:, z, :],
                                                       scalar=0.5 / (WS * WS) if f else 1.0, in1=bk[:, T:2 * T],
                                                       op0=ALU.mult, op1=ALU.mult).then_inc(gu_read.handle, 1)
                        if not f:
                            wait(gu_read, n)
                            wait(ce_mm, v + 1)
                            nc.vector.tensor_tensor(fa[:, z, :], fa[:, z, :], bank[3 + v % 2][:, 0:T], ALU.mult)\
                                .then_inc(ce_read.handle, 1)

                    def at1(w):
                        if w < W1G:
                            y = w % 2
                            for t in range(TT):
                                n = (t + 1) * P
                                for j in range(4):
                                    if t == 0 and j == 0:
                                        wait(a_mm, 3 * w + 1)
                                    if t == 1 and j % 2 == 0:
                                        wait(a_mm, 3 * w + 2 + j // 2)
                                    dve.sem_inc(passed_dve, 1)
                                    src = bank[0][:, j * P:(j + 1) * P] if t == 0 else \
                                        bank[(1, 3)[j // 2]][:, j % 2 * T:(j % 2 + 1) * T]
                                    nc.vector.tensor_tensor_reduce(
                                        out=s1[:, y, j, t * P:t * P + n], in0=src, in1=bias1[:, t * P:t * P + n],
                                        scale=1.0, scalar=-3e38, op0=ALU.add, op1=ALU.max,
                                        accum_out=mx1[:, y, 4 * t + j:4 * t + j + 1]).then_inc(a_max.handle, 1)
                                wait(a_max, 8 * w + 4 * (t + 1))
                                nc.vector.tensor_scalar(nb1[:, y, 4 * t:4 * t + 4], mx1[:, y, 4 * t:4 * t + 4], -1.0,
                                                        None, ALU.mult).then_inc(a_shift.handle, 1)
                        if 1 <= w <= W1G:
                            for b in range(3):
                                wait(at_hi, 3 * (w - 1) + b + 1)
                                nc.vector.tensor_tensor(p1l[:, b, :, :].rearrange("p j n -> p (j n)"),
                                                        bank[4 + b][:, :],
                                                        p1h[:, b, :, :].rearrange("p j n -> p (j n)"),
                                                        ALU.subtract).then_inc(at_lo.handle, 1)

                    def route(s):
                        nc.vector.tensor_scalar(rt_l, misc[:, 0:TT * EXPERTS].rearrange("p (t e) -> p t e", t=TT),
                                                1.0 / WS, None, ALU.mult).then_inc(misc_free.handle, 1)
                        wait(misc_free, MISC[("rt", s)])
                        bc = lambda k: rt_m[:, k, :].unsqueeze(2).to_broadcast([P, TT, EXPERTS])
                        io = iota.unsqueeze(1).to_broadcast([P, TT, EXPERTS])
                        link(nc.vector.tensor_reduce(rt_m[:, 0, :], rt_l, AX.X, ALU.max))
                        nc.vector.tensor_tensor(rt_a, rt_l, bc(0), ALU.subtract).then_inc(rt_sub.handle, 1)
                        wait(rt_sub, s + 1)

                        def pick(src, k, kept):
                            link(nc.vector.tensor_tensor(kept, src, bc(k), ALU.is_ge))
                            link(nc.vector.tensor_tensor(kept, kept, io, ALU.mult))
                            link(nc.vector.tensor_reduce(rt_m[:, 2, :], kept, AX.X, ALU.max))
                            link(nc.vector.tensor_tensor(kept, io, bc(2), ALU.is_equal))

                        pick(rt_l, 0, rt_k)
                        link(nc.vector.scalar_tensor_tensor(out=rt_l, in0=rt_k, scalar=-3e38, in1=rt_l,
                                                            op0=ALU.mult, op1=ALU.add))
                        link(nc.vector.tensor_reduce(rt_m[:, 1, :], rt_l, AX.X, ALU.max))
                        pick(rt_l, 1, rt_k2)
                        link(nc.vector.tensor_tensor(rt_k, rt_k, rt_k2, ALU.add))
                        wait(rt_exp, s + 1)
                        link(nc.vector.tensor_tensor(rt_e, rt_e, rt_k, ALU.mult))
                        link(nc.vector.tensor_reduce(rt_m[:, 3, :], rt_e, AX.X, ALU.add))
                        link(nc.vector.reciprocal(rt_m[:, 3, :], rt_m[:, 3, :]))
                        link(nc.vector.tensor_tensor(rt_e, rt_e, bc(3), ALU.mult))
                        link(nc.vector.tensor_copy(ch16, rt_e))
                        link(nc.vector.tensor_copy(c17[:, :, 0:8], ch16))
                        nc.vector.tensor_tensor(c17[:, :, 9:17], rt_e, ch16, ALU.subtract).then_inc(c_ready.handle, 1)

                    for item in ORDER:
                        kind = item[0]
                        if kind == "at0":
                            at0(item[1])
                        elif kind in ("ff0", "ff1"):
                            ff(int(kind == "ff1"), item[1])
                        elif kind == "at1":
                            at1(item[1])
                        elif kind == "mc":
                            link(nc.vector.tensor_copy(mcol[:, item[1], :], modt[:, 2 * i + item[1], :]))
                        elif kind == "lna":
                            k, s = item[1:]
                            if k == 0:
                                wait(ld_x[s], 1)
                            src = xin if k == 0 else xs
                            for t in range(TT):
                                ins = nc.vector.bn_stats(st6[:, t, :], src[:, s, t, :])
                            link(ins)
                            dve.sem_inc(passed_dve, 1)
                            for t in range(TT):
                                ins = nc.vector.bn_aggr(mv[:, t, :], st6[:, t, :])
                            ins.then_inc(ln_stats.handle, 1)
                        elif kind == "lnb":
                            k, s = item[1:]
                            src = xin if k == 0 else xs
                            wait(ln_rstd, n_ln(k, s))
                            for t in range(TT):
                                ins = nc.vector.tensor_scalar(xn[:, t, :], src[:, s, t, :], mv[:, t, 0:1],
                                                              lr[:, t:t + 1], ALU.subtract, ALU.mult)
                            ins.then_inc(ln_norm.handle, 1)
                        elif kind == "lnc":
                            k, s = item[1:]
                            wait(misc_mm, MISC[item])
                            for c in range(DC):
                                a = 4 * k + c
                                ins = nc.vector.tensor_scalar(hf[:, c * T:(c + 1) * T], misc[:, c * T:(c + 1) * T],
                                                              mcol[:, s, a:a + 1], mcol[:, s, a + 2:a + 3],
                                                              ALU.mult, ALU.add)
                            ins.then_inc(misc_free.handle, 1)
                            wait(misc_free, MISC[item])
                            wait(h_hi, n_ln(k, s))
                            nc.vector.tensor_tensor(htl[:, s].rearrange("p c n -> p (c n)"), hf[:, :],
                                                    hth[:, s].rearrange("p c n -> p (c n)"), ALU.subtract)\
                                .then_inc(h_lo.handle, 1)
                        elif kind == "rt":
                            wait(misc_mm, MISC[item])
                            route(item[1])
                        elif kind == "ct":
                            wait(misc_mm, MISC[item])
                            nc.vector.tensor_copy(ctt[:, item[1], :], misc[0:17, 0:T]).then_inc(misc_free.handle, 1)
                        elif kind == "res0":
                            s = item[1]
                            wait(o_mm, n_o(0, s))
                            wait(ld_g[s], 1)
                            wait(st_x[s], 0)
                            ins, add = residual(bank[7], s, 0, xs[:, s], xin[:, s])
                            link(ins)
                            add().then_inc(o_read.handle, 1)
                            wait(o_read, n_o(0, s))
                        elif kind == "resf":
                            f, s = item[1:]
                            stage_ = 3 if f else 1
                            wait(o_mm, n_o(stage_, s))
                            ins, add = residual(bank[o_bank[(stage_, s)]], s, 1, xs[:, s], xs[:, s])
                            link(ins)
                            add().then_inc(o_read.handle, 1)
                            wait(o_read, n_o(stage_, s))
                        elif kind == "q1":
                            split_lo(q1l[:, :], misc[:, :], q1h[:, :], item, 1.0 / WS)
                            wait(misc_free, MISC[item])
                        elif kind == "k1":
                            s = item[1]
                            split_lo(k1l[:, s].rearrange("p c n -> p (c n)"), misc[:, :],
                                     k1h[:, s].rearrange("p c n -> p (c n)"), item, 1.0 / WS)
                        elif kind == "v1":
                            s = item[1]
                            split_lo(v1l[:, s].rearrange("p c n -> p (c n)"), misc[:, :],
                                     v1h[:, s].rearrange("p c n -> p (c n)"), item, 1.0 / WS)
                        elif kind == "qm":
                            s = item[1]
                            wait(a_mm, 24 * s)
                            for j in range(4):
                                for src, dst in ((q1h, qmh), (q1l, qml)):
                                    ins = nc.vector.tensor_scalar(dst[:, j, :], src[:, :], con[:, K_HM + j:K_HM + j + 1],
                                                                  None, ALU.mult)
                            ins.then_inc(qm_ready.handle, 1)
                        elif kind == "pvr":
                            s = item[1]
                            link(nc.vector.reciprocal(ri1, sum1[:, s]))
                            wait(o_mm, n_o(2, s))
                            rb1 = ri1.rearrange("p t h -> p (t h)").unsqueeze(2).to_broadcast([P, TT * H1, HD1])
                            nc.vector.tensor_tensor(xn[:, :, :].rearrange("p t (h e) -> p (t h) e", e=HD1),
                                                    bank[7][:, :].rearrange("p (n e) -> p n e", e=HD1), rb1,
                                                    ALU.mult).then_inc(o_read.handle, 1)
                        elif kind == "at":
                            split_lo(q1l[:, :], misc[:, :], q1h[:, :], item, 1.0)
                        elif kind == "pj":
                            s = item[1]
                            wait(misc_mm, MISC[item])
                            wait(ld_g[s], 2)
                            ins, add = residual(misc, s, 0, xs[:, s], xs[:, s])
                            link(ins)
                            add().then_inc(misc_free.handle, 1)
                            wait(misc_free, MISC[item])
                    assert chained[0] <= CHAIN, chained[0]
                    dve.sem_inc(v_chain.handle, CHAIN - chained[0])


def _constants():
    rows = np.arange(P)[:, None]
    con = np.zeros((P, NC), np.float32)
    con[:, K_ID:K_ID + P] = np.eye(P)
    ramp = 2.0 ** (-8.0 / H1)
    for t in range(TT):
        keys = np.arange((t + 1) * P)[None, :]
        q = t * P + rows
        seen = keys <= q
        a, b = t * P, t * P + (t + 1) * P
        con[:, K_M0 + a:K_M0 + b] = np.where(seen & (q - keys < WINDOW), 0.0, NEG)
        con[:, K_M1 + a:K_M1 + b] = np.where(seen, (keys - q) * ramp, NEG)
    for j in range(4):
        con[:, K_HM + j] = (np.arange(P) % 32 // HD1 == j) * (HD1 ** -0.5)
    con[:, K_IO:K_IO + EXPERTS] = np.arange(EXPERTS, 0, -1)
    con[0, K_BS] = 1.0
    con[1, K_BS + 1] = 1.0
    bits = np.arange(P)[:, None] & np.arange(P)[None, :]
    ones = np.array([[bin(v).count("1") % 2 for v in row] for row in bits])
    had = (1.0 - 2.0 * ones).astype(np.float32)
    frac = np.arange(0, HD, 2, dtype=np.float32) / np.float32(HD)
    turn = np.arange(T, dtype=np.float32)[:, None] / (np.float32(10000.0) ** frac)
    cos, sin = np.cos(turn).astype(np.float32), np.sin(turn).astype(np.float32)
    rope = np.stack([np.concatenate([cos, cos], 1), np.concatenate([-sin, sin], 1)])
    rope = np.ascontiguousarray(rope.reshape(2, TT, P, HD).transpose(2, 0, 1, 3))
    sel = np.zeros((17, HP), np.float16)
    for h in range(HID0):
        e = h // INNER
        if e < EXPERTS:
            sel[e, h] = sel[9 + e, h] = 0.5 / (WS * WS)
        else:
            sel[8, h] = 0.5 / (WS * WS)
    return con, had, rope, sel


def _tiles(w, n=None):
    w = np.asarray(w)
    if n is not None and w.shape[1] < n:
        w = np.concatenate([w, np.zeros((w.shape[0], n - w.shape[1]), w.dtype)], 1)
    return w.reshape(-1, P, w.shape[1]).transpose(1, 0, 2).reshape(P, -1)


def _layout(v):
    v = {k: np.asarray(a) for k, a in v.items()}
    q, kv = v["L0_attn_q_kernel"], v["L0_attn_kv_kernel"]
    qkv = np.stack([q[0::2], q[1::2], kv[0], kv[1]], 0)
    qkv = qkv.reshape(4, NKV, DC, P, HD).transpose(3, 2, 1, 0, 4).reshape(P, -1)
    side = lambda name: v[name].transpose(1, 0, 2).reshape(D, EXPERTS * INNER)
    gate = np.concatenate([side("L0_ffn_gate_w"), v["L0_ffn_s_gate_w"]], 1)
    up = np.concatenate([side("L0_ffn_up_w"), v["L0_ffn_s_up_w"]], 1)
    down = np.concatenate([v["L0_ffn_down_w"].reshape(EXPERTS * INNER, D), v["L0_ffn_s_down_w"],
                           np.zeros((HP - HID0, D), np.float32)], 0)
    wall = np.concatenate([
        qkv, v["L0_attn_out_kernel"].transpose(1, 0, 2).reshape(P, NH * D), _tiles(gate, HP), _tiles(up, HP),
        _tiles(down), _tiles(v["L0_ffn_router_w"].T), _tiles(v["L1_attn_W_attn"]), _tiles(v["L1_attn_W_proj"]),
        _tiles(v["L1_ffn_W1"].T), _tiles(v["L1_ffn_W3"].T)], 1)
    w2t = _tiles(v["L1_ffn_W2"].T)
    shared = np.zeros((2, (J0 - JB) * P), np.float32)
    shared[0, :SHARED] = v["L0_ffn_s_gate_b"]
    shared[1, :SHARED] = v["L0_ffn_s_up_b"]
    brow = np.concatenate([shared.reshape(-1), v["L0_ffn_s_down_b"], v["L1_attn_b_attn"], v["L1_attn_b_proj"]])
    qs, ks = v["L0_attn_q_norm_scale"], v["L0_attn_k_norm_scale"]
    turned = lambda s: np.concatenate([s[HD // 2:], s[:HD // 2]])
    nsc = np.stack([np.stack([qs, qs, ks]), np.stack([turned(qs), turned(qs), turned(ks)])])
    per_layer = lambda a, b: np.stack([_tiles(a).reshape(P, DC, -1), _tiles(b).reshape(P, DC, -1)], 1)
    ct = per_layer(v["L0_c"].T, v["L1_c"].T)
    wmod = per_layer(v["L0_wmod"], v["L1_wmod"])
    con, had, rope, sel = _constants()
    return {"x": v["L0_attn_x"], "wall": wall, "w2t": w2t, "brow": brow, "con": con, "had": had, "rope": rope,
            "nsc": nsc, "sel": sel, "ct": ct, "wmod": wmod}


def kernel(**inputs):
    import concourse.bacc as _bacc
    from concourse.bass_utils import run_bass_kernel_spmd as _run

    assert JB * P == EXPERTS * INNER
    nc = _bacc.Bacc("TRN2", target_bir_lowering=False, num_devices=1)
    arrays, args = {}, []
    for name, a in _layout(inputs).items():
        a = np.ascontiguousarray(a)
        arrays[f"in_{name}_dram"] = a
        args.append(nc.dram_tensor(f"in_{name}_dram", a.shape, mybir.dt.from_np(a.dtype), kind="ExternalInput").ap())
    out = nc.dram_tensor("out_dram", (B, T, D), F32, kind="ExternalOutput").ap()
    gates = nc.dram_tensor("gates_dram", (B, 4 * D), F32, kind="Internal").ap()
    build(nc, *args, out, gates)
    r = _run(nc, [arrays], core_ids=[0])
    return r.results[0]["out_dram"]
```

```python
from contextlib import ExitStack

import numpy as np

import concourse.bass as bass
from concourse import mybir

F32 = mybir.dt.float32
F16 = mybir.dt.float16
I32 = mybir.dt.int32
ALU = mybir.AluOpType
ACT = mybir.ActivationFunctionType
AX = mybir.AxisListType

P = 128
B, T, D = 16, 256, 256
TT = T // P
DC = D // P
NH, NKV, HD = 16, 8, 128
WINDOW = 128
ATT_SCALE = 0.08838834764831845
EXPERTS, INNER, SHARED = 8, 176, 352
HID0 = EXPERTS * INNER + SHARED
J0 = -(-HID0 // P)
HP = J0 * P
JB = (EXPERTS * INNER) // P
H1, HD1 = 32, 8
HID1 = 1024
J1 = HID1 // P
WS = 64.0
NEG = -1e30

COLS = {}
_at = 0
for _name, _n in (("qkv", DC * NKV * 512), ("o", NH * D), ("g", DC * HP), ("u", DC * HP), ("d", J0 * D),
                  ("r", DC * EXPERTS), ("a1", DC * 3 * D), ("p1", DC * D), ("w1", DC * HID1), ("w3", DC * HID1)):
    COLS[_name] = _at
    _at += _n
NW = _at
COLS["w2"] = NW
NW2 = NW + J1 * D
CHUNK = next(n for n in range(1500, 0, -1) if NW % n == 0 and n % 4 == 0)
NCHUNK = NW // CHUNK

BG, BU = 0, (J0 - JB) * P
BD = 2 * BU
BA = BD + D
BP = BA + 3 * D
NB = BP + D

K_ID, K_M0, K_M1, K_HM, K_IO, K_BS, K_EPS = 0, 128, 512, 896, 900, 908, 910
NC = 912

AFTER_AT0 = {1: [("lnc", 0, 1)], 11: [("res0", 0), ("lna", 1, 0)], 12: [("lnb", 1, 0)],
             13: [("lnc", 1, 0)], 14: [("rt", 0)], 16: [("ct", 0)], 17: [("ff0", 0)], 18: [("ff0", 1)],
             19: [("res0", 1), ("lna", 1, 1)]}
AFTER_FF0 = {2: [("lnb", 1, 1)], 4: [("lnc", 1, 1)], 6: [("rt", 1)], 9: [("ct", 1)],
             15: [("resf", 0, 0), ("lna", 2, 0)], 16: [("lnb", 2, 0)], 18: [("lnc", 2, 0)], 20: [("q1", 0)],
             22: [("k1", 0)], 24: [("v1", 0)], 25: [("qm", 0)], 27: [("at1", 0)], 28: [("at1", 1)],
             29: [("resf", 0, 1), ("lna", 2, 1)]}
AFTER_AT1 = {2: [("lnb", 2, 1)], 3: [("lnc", 2, 1)], 4: [("k1", 1)], 5: [("v1", 1)], 6: [("q1", 1)],
             7: [("qm", 1)], 9: [("pvr", 0)], 10: [("at", 0)], 11: [("pj", 0), ("lna", 3, 0)],
             12: [("lnb", 3, 0)], 13: [("lnc", 3, 0)], 16: [("ff1", 0)], 17: [("pvr", 1)]}
AFTER_FF1 = {1: [("at", 1)], 2: [("pj", 1), ("lna", 3, 1)], 3: [("lnb", 3, 1)], 4: [("lnc", 3, 1)],
             9: [("resf", 1, 0)], 17: [("resf", 1, 1)]}
ORDER = [("mc", 0), ("mc", 1), ("lna", 0, 0), ("lnb", 0, 0), ("lnc", 0, 0), ("lna", 0, 1), ("lnb", 0, 1)]
for _u in range(20):
    ORDER += [("at0", _u)] + AFTER_AT0.get(_u, [])
for _v in range(2, 2 * J0 + 2):
    ORDER += [("ff0", _v)] + AFTER_FF0.get(_v, [])
for _w in range(2, 18):
    ORDER += [("at1", _w)] + AFTER_AT1.get(_w, [])
for _v in range(1, 2 * J1 + 2):
    ORDER += [("ff1", _v)] + AFTER_FF1.get(_v, [])

MISC, MISC_HI = {}, {}
_hi = 0
for _item in ORDER:
    _uses = []
    if _item[0] == "at0" and 1 <= _item[1] <= 16:
        _uses = [("t1", _item[1] - 1, _t) for _t in range(TT)]
    elif _item[0] in ("lnc", "rt", "ct", "q1", "k1", "v1", "at", "pj"):
        _uses = [_item]
    for _k in _uses:
        MISC[_k] = len(MISC) + 1
        if _k[0] in ("t1", "q1", "k1", "v1", "at"):
            _hi += 1
            MISC_HI[_k] = _hi
NPAIR = B // 2
U0 = 2 * NKV
W1G = 16
CHAIN = 1100


class Signal:

    def __init__(self, handle, per, unit=1):
        self.handle, self.per, self.unit = handle, per, unit

    def count(self, i, n):
        return i * (self.per * self.unit) + (self.per + n) * self.unit


def build(nc, x_in, wall, w2t, brow, cf, hadm, rope, nsc, sel_in, ct_in, wmod, out, gates_dram):
    ctx = ExitStack()
    with ctx:
        def sb(name, shape, dt):
            return ctx.enter_context(nc.sbuf_tensor(name, shape, dt))

        def sem(name):
            return ctx.enter_context(nc.semaphore(name))

        signals = []

        def signal(name, per, unit=1):
            signals.append(Signal(sem(name), per, unit))
            return signals[-1]

        whi = sb("whi", [P, NW2], F16)
        wlo = sb("wlo", [P, NW2], F16)
        brows = sb("brows", [2, NB], F16)
        sel = sb("sel", [17, HP], F16)
        ones = sb("ones", [2, T], F16)
        con = sb("con", [P, NC], F32)
        ropec = sb("ropec", [P, TT, 3, HD], F32)
        ropes = sb("ropes", [P, TT, 3, HD], F32)
        modt = sb("modt", [P, B, 16], F32)
        mcol = sb("mcol", [P, 2, 16], F32)
        xin = sb("xin", [P, 2, TT, D], F32)
        xs = sb("xs", [P, 2, TT, D], F32)
        gate = sb("gate", [P, 2, 2, D], F32)
        hth = sb("hth", [P, 2, DC, T], F16)
        htl = sb("htl", [P, 2, DC, T], F16)
        hf = sb("hf", [P, 2 * T], F32)
        xn = sb("xn", [P, TT, D], F32)
        vh0 = sb("vh0", [P, 4, TT, HD], F16)
        vl0 = sb("vl0", [P, 4, TT, HD], F16)
        k1h = sb("k1h", [P, 2, DC, T], F16)
        k1l = sb("k1l", [P, 2, DC, T], F16)
        v1h = sb("v1h", [P, 2, TT, D], F16)
        v1l = sb("v1l", [P, 2, TT, D], F16)
        q1h = sb("q1h", [P, DC * T], F16)
        q1l = sb("q1l", [P, DC * T], F16)
        qmh = sb("qmh", [P, 4, DC * T], F16)
        qml = sb("qml", [P, 4, DC * T], F16)
        ctt = sb("ctt", [17, 2, T], F16)
        small = sb("small", [P, 512], F32)
        NARENA = 24 * 256
        arena = sb("arena", [P, NARENA], F32)
        farena = sb("farena", [P, 2048], F32)

        spot = [0]

        def small_at(n):
            spot[0] += n
            assert spot[0] <= 512
            return small[:, spot[0] - n:spot[0]]

        st6 = small_at(TT * 6).rearrange("p (t k) -> p t k", t=TT)
        mv = small_at(TT * 2).rearrange("p (t k) -> p t k", t=TT)
        lv = small_at(TT)
        lr = small_at(2 * TT)
        half = small_at(8)
        ss = small_at(6)
        ms = small_at(6)
        r0 = small_at(12).rearrange("p (k n) -> p k n", k=2)
        rs0 = small_at(24).rearrange("p (k n) -> p k n", k=4)
        mx0 = small_at(8).rearrange("p (k n) -> p k n", k=2)
        nb0 = small_at(8).rearrange("p (k n) -> p k n", k=2)
        sm0 = small_at(8).rearrange("p (k n) -> p k n", k=2)
        ri0 = small_at(8).rearrange("p (k n) -> p k n", k=2)
        rt_l = small_at(16).rearrange("p (t e) -> p t e", t=TT)
        rt_e = small_at(16).rearrange("p (t e) -> p t e", t=TT)
        rt_a = small_at(16).rearrange("p (t e) -> p t e", t=TT)
        rt_k = small_at(16).rearrange("p (t e) -> p t e", t=TT)
        rt_k2 = small_at(16).rearrange("p (t e) -> p t e", t=TT)
        rt_m = small_at(8).rearrange("p (k t) -> p k t", t=TT)
        c17 = small_at(34).rearrange("p (t e) -> p t e", t=TT)
        mx1 = small_at(16).rearrange("p (k n) -> p k n", k=2)
        nb1 = small_at(16).rearrange("p (k n) -> p k n", k=2)
        sum1 = small_at(2 * 64).rearrange("p (s t h) -> p s t h", s=2, t=TT)
        ri1 = small_at(64).rearrange("p (t h) -> p t h", t=TT)
        ch16 = small_at(8).bitcast(F16).rearrange("p (t e) -> p t e", t=TT)

        def carve(pool_, spots, at=0):
            found = []
            for words, dt in spots:
                a = pool_[:, at:at + words]
                found.append(a if dt == F32 else a.bitcast(F16))
                at += words
            assert at <= pool_.shape[1], at
            return found

        ra, rb, qkh, qkl, smx, pth, ptl, ench, encl = carve(arena,
            [(768, F32), (768, F32), (384, F16), (384, F16), (2 * 768, F32), (384, F16), (384, F16),
             (256, F16), (256, F16)])
        ra = ra.rearrange("p (t k h) -> p t k h", t=TT, k=3)
        rb = rb.rearrange("p (t k h) -> p t k h", t=TT, k=3)
        qkh = qkh.rearrange("p (k n) -> p k n", k=3)
        qkl = qkl.rearrange("p (k n) -> p k n", k=3)
        smx = smx.rearrange("p (y k n) -> p y k n", y=2, k=2)
        pth = pth.rearrange("p (k n) -> p k n", k=6)
        ptl = ptl.rearrange("p (k n) -> p k n", k=6)
        ench = ench.rearrange("p (t k n) -> p t k n", t=TT, k=2)
        encl = encl.rearrange("p (t k n) -> p t k n", t=TT, k=2)
        th, fa, fh, fl = carve(farena, [(2 * T, F32), (3 * T, F32), (3 * T // 2, F16), (3 * T // 2, F16)])
        th = th.rearrange("p (k n) -> p k n", k=2)
        fa = fa.rearrange("p (k n) -> p k n", k=3)
        fh = fh.rearrange("p (k n) -> p k n", k=3)
        fl = fl.rearrange("p (k n) -> p k n", k=3)
        s1, p1h, p1l = carve(arena, [(2 * 4 * 384, F32), (2 * 768, F16), (2 * 768, F16)])
        s1 = s1.rearrange("p (b j n) -> p b j n", b=2, j=4)
        p1h = p1h.rearrange("p (y k j n) -> p y k j n", y=2, k=3, j=4)
        p1l = p1l.rearrange("p (y k j n) -> p y k j n", y=2, k=3, j=4)

        ident = con[:, K_ID:K_ID + 128]
        mask0 = con[:, K_M0:K_M0 + 384]
        bias1 = con[:, K_M1:K_M1 + 384]
        iota = con[:, K_IO:K_IO + 8]

        bank = [ctx.enter_context(nc.psum_tensor(f"bank{k}", [P, 512], F32)) for k in range(8)]
        misc = bank[2]

        def w_of(name, at, n):
            a = COLS[name] + at
            return whi[:, a:a + n], wlo[:, a:a + n]

        wm = whi[:, 0:2 * 2 * DC * 1536].bitcast(F32).rearrange("p (l c n) -> p l c n", l=2, c=DC)
        ha = wlo[:, 0:4096].bitcast(F32)
        hb = wlo[:, 4096:8192].bitcast(F32)
        had = wlo[:, 8192:8448].bitcast(F32)
        rcos = wlo[:, 8448:8960].bitcast(F32).rearrange("p (t n) -> p t n", t=TT)
        rsin = wlo[:, 8960:9472].bitcast(F32).rearrange("p (t n) -> p t n", t=TT)
        nsn = wlo[:, 9472:10240].bitcast(F32).rearrange("p (k n) -> p k n", k=3)
        nsw = wlo[:, 10240:11008].bitcast(F32).rearrange("p (k n) -> p k n", k=3)
        braw = wlo[0:2, 11008:11008 + 2 * NB].bitcast(F32)
        sc = wlo[:, 16384:16512].bitcast(F32).rearrange("p (l c n) -> p l c n", l=2, c=DC)
        st = wlo[:, 16512:16640].bitcast(F32).rearrange("p (l c n) -> p l c n", l=2, c=DC)
        gsb = wlo[0:B, 16640:16640 + 2 * 4 * D].bitcast(F32)
        gtmp = wlo[0:B, 18688:18688 + 2 * 4 * D].bitcast(F32)
        bhi = wlo[0:2, 20736:20736 + NB]
        blo = wlo[0:2, 20736 + NB:20736 + 2 * NB]

        ld_con = sem("ld_con")
        ld_c = sem("ld_c")
        ld_wm = sem("ld_wm")
        ld_w2 = sem("ld_w2")
        ld_rope = sem("ld_rope")
        ld_b = sem("ld_b")
        ld_sel = sem("ld_sel")
        set_tanh = sem("set_tanh")
        set_v = sem("set_v")
        set_mm = sem("set_mm")
        set_had = sem("set_had")
        set_hi = sem("set_hi")
        st_gates = sem("st_gates")
        had_step = sem("had_step")

        blk = nc.Block()
        with blk as block:
            @block.sync
            def _(sp):
                sp.dma_start(sc[:, :, :, :], ct_in).then_inc(ld_c, 16)
                sp.dma_start(wm[:, :, :, :], wmod).then_inc(ld_wm, 16)
                sp.dma_start(ha, w2t).then_inc(ld_w2, 16)
                sp.dma_start(had, hadm).then_inc(ld_w2, 16)
                sp.dma_start(con[:, :], cf).then_inc(ld_con, 16)
                sp.dma_start(rcos, rope[:, 0]).then_inc(ld_rope, 16)
                sp.dma_start(rsin, rope[:, 1]).then_inc(ld_rope, 16)
                sp.dma_start(nsn, nsc[0].partition_broadcast(P)).then_inc(ld_rope, 16)
                sp.dma_start(nsw, nsc[1].partition_broadcast(P)).then_inc(ld_rope, 16)
                sp.dma_start(braw, brow.partition_broadcast(2)).then_inc(ld_b, 16)
                sp.dma_start(sel[:, :], sel_in).then_inc(ld_sel, 16)
                sp.wait_ge(set_v, 16)
                sp.dma_start(gates_dram, gsb).then_inc(st_gates, 16)
                sp.wait_ge(st_gates, 16)
                sp.wait_ge(ld_con, 16)
                sp.wait_ge(ld_sel, 16)

            @block.scalar
            def _(act):
                act.wait_ge(ld_c, 16)
                nc.scalar.activation(st[:, :, :, :], sc[:, :, :, :], ACT.Tanh, scale=0.5).then_inc(set_tanh, 1)
                for q in range(4):
                    act.wait_ge(set_had, q + 1)
                    nc.scalar.activation(whi[:, NW + q * 512:NW + (q + 1) * 512], bank[4 + q][:, :], ACT.Copy,
                                         scale=WS / 32.0).then_inc(set_hi, 1)

            @block.tensor
            def _(pe):
                pe.wait_ge(set_v, 2)
                pe.wait_ge(ld_wm, 16)
                for l in range(2):
                    for k, part in enumerate((1, 0, 4, 3)):
                        for c2 in range(DC):
                            n = l * 8 + k * 2 + c2
                            for c in range(DC):
                                last = nc.tensor.matmul(bank[0][:, n * B:(n + 1) * B],
                                                        wm[:, l, c, part * D + c2 * P:part * D + (c2 + 1) * P],
                                                        st[:, l, c, :], start=(c == 0), stop=(c == DC - 1))
                last.then_inc(set_mm, 1)
                for l in range(2):
                    for k, part in enumerate((2, 5)):
                        for c in range(DC):
                            last = nc.tensor.matmul(bank[1 + l][0:B, k * D:(k + 1) * D], st[:, l, c, :],
                                                    wm[:, l, c, part * D:(part + 1) * D],
                                                    start=(c == 0), stop=(c == DC - 1))
                last.then_inc(set_mm, 1)
                pe.wait_ge(set_v, 18)
                pe.wait_ge(ld_w2, 32)
                for q in range(4):
                    nc.tensor.matmul(bank[4 + q][:, :], had, hb[:, q * 512:(q + 1) * 512],
                                     start=True, stop=True).then_inc(set_had, 1)

            @block.gpsimd
            def _(pool):
                pool.memset(half, -0.5)
                pool.memset(ones[:, :], 1.0)
                pool.memset(c17[:, :, 8:9], 1.0)

            @block.vector
            def _(dve):
                n = [0]

                def link(ins):
                    n[0] += 1
                    ins.then_inc(set_v, 1)
                    dve.wait_ge(set_v, n[0])

                dve.wait_ge(set_tanh, 1)
                link(nc.vector.tensor_scalar(st[:, :, :, :], st[:, :, :, :], 1.0, 0.5, ALU.add, ALU.mult))
                link(nc.vector.tensor_tensor(st[:, :, :, :], st[:, :, :, :], sc[:, :, :, :], ALU.mult))
                dve.wait_ge(set_mm, 1)
                src = bank[0][:, 0:16 * B].rearrange("p (n b) -> p b n", b=B)
                link(nc.vector.tensor_copy(modt[:, :, :], src))
                for l in range(2):
                    for k in (0, 2):
                        a = l * 8 + k * 2
                        link(nc.vector.tensor_scalar(modt[:, :, a:a + 2], modt[:, :, a:a + 2], 1.0, None, ALU.add))
                dve.wait_ge(set_mm, 2)
                for l in range(2):
                    g = bank[1 + l][0:B, :]
                    a, b = gsb[:, l * 512:(l + 1) * 512], gtmp[:, l * 512:(l + 1) * 512]
                    link(nc.vector.tensor_scalar(a, g, 0.0, 2.0 / WS, ALU.is_ge, ALU.mult))
                    link(nc.vector.tensor_scalar(a, a, -1.0 / WS, None, ALU.add))
                    link(nc.vector.tensor_scalar(b, g, -1.0, None, ALU.mult))
                    link(nc.vector.tensor_tensor(b, b, g, ALU.max))
                link(nc.vector.scalar_tensor_tensor(out=gsb, in0=gtmp, scalar=0.25, in1=gsb,
                                                    op0=ALU.max, op1=ALU.mult))
                assert n[0] == 16, n[0]
                dve.wait_ge(ld_w2, 32)
                bufs = [(ha, hb), (hb, ha), (ha, hb)]
                for k, (src, dst) in enumerate(bufs):
                    v = [z.rearrange("p (o two i) -> p o two i", two=2, i=D << k) for z in (src, dst)]
                    ins = nc.vector.tensor_tensor(v[1][:, :, 0, :], v[0][:, :, 0, :], v[0][:, :, 1, :], ALU.add)
                    ins2 = nc.vector.tensor_tensor(v[1][:, :, 1, :], v[0][:, :, 0, :], v[0][:, :, 1, :], ALU.subtract)
                    if k < 2:
                        ins2.then_inc(had_step, 1)
                        dve.wait_ge(had_step, k + 1)
                        continue
                    ins2.then_inc(set_v, 2)
                    n[0] += 2
                dve.wait_ge(ld_rope, 64)
                for k in range(3):
                    for t in range(TT):
                        nc.vector.tensor_tensor(ropec[:, t, k, :], rcos[:, t, :], nsn[:, k, :], ALU.mult)
                        nc.vector.tensor_tensor(ropes[:, t, k, :], rsin[:, t, :], nsw[:, k, :], ALU.mult)
                dve.wait_ge(ld_b, 16)
                dve.wait_ge(ld_con, 16)
                link(nc.vector.tensor_scalar(bhi, braw, WS, None, ALU.mult))
                link(nc.vector.scalar_tensor_tensor(out=blo, in0=braw, scalar=WS, in1=bhi,
                                                    op0=ALU.mult, op1=ALU.subtract))
                link(nc.vector.tensor_scalar(bhi, bhi, con[0:2, K_BS:K_BS + 1], None, ALU.mult))
                link(nc.vector.scalar_tensor_tensor(out=brows[:, :], in0=blo, scalar=con[0:2, K_BS + 1:K_BS + 2],
                                                    in1=bhi, op0=ALU.mult, op1=ALU.add))
                for q in range(4):
                    dve.wait_ge(set_hi, q + 1)
                    a = slice(NW + q * 512, NW + (q + 1) * 512)
                    nc.vector.scalar_tensor_tensor(out=wlo[:, a], in0=bank[4 + q][:, :], scalar=WS / 32.0,
                                                   in1=whi[:, a], op0=ALU.mult, op1=ALU.subtract)

        RING = 3
        stage = [arena[:, k * CHUNK:(k + 1) * CHUNK] for k in range(RING)]
        assert RING * CHUNK <= NARENA
        ld_stage = [sem(f"ld_stage{k}") for k in range(RING)]
        w_hi = sem("w_hi")
        w_lo = sem("w_lo")

        ld_x = [signal(f"ld_x{s}", 1, 16) for s in range(2)]
        ld_g = [signal(f"ld_g{s}", 2, 16) for s in range(2)]
        st_x = [signal(f"st_x{s}", 1, 16) for s in range(2)]
        ln_stats = signal("ln_stats", 8)
        ln_rstd = signal("ln_rstd", 8)
        ln_norm = signal("ln_norm", 8)
        h_hi = signal("h_hi", 8)
        h_lo = signal("h_lo", 8)
        misc_mm = signal("misc_mm", len(MISC))
        misc_hi = signal("misc_hi", len(MISC_HI))
        misc_free = signal("misc_free", len(MISC))
        qkv_mm = signal("qkv_mm", 2 * U0)
        qkv_act = signal("qkv_act", 2 * U0)
        rope_mul = signal("rope_mul", 2 * U0)
        rope_sum = signal("rope_sum", 2 * U0)
        qk_rstd = signal("qk_rstd", 2 * U0)
        k_norm = signal("k_norm", 2 * U0)
        s_mm = signal("s_mm", 2 * U0)
        s_max = signal("s_max", 4 * U0)
        s_shift = signal("s_shift", U0)
        s_exp = signal("s_exp", 4 * U0)
        p_norm = signal("p_norm", 4 * U0)
        pt_mm = signal("pt_mm", 2 * U0)
        pt_hi = signal("pt_hi", 2 * U0)
        pt_lo = signal("pt_lo", 2 * U0)
        enc_mm = signal("enc_mm", U0)
        enc_hi = signal("enc_hi", U0)
        enc_lo = signal("enc_lo", U0)
        o_mm = signal("o_mm", 8)
        o_read = signal("o_read", 8)
        NGU = 2 * J0 + 2 * J1
        gu_mm = signal("gu_mm", NGU)
        gu_tanh = signal("gu_tanh", NGU)
        gu_read = signal("gu_read", NGU)
        ce_mm = signal("ce_mm", 2 * J0)
        ce_read = signal("ce_read", 2 * J0)
        hid_hi = signal("hid_hi", NGU)
        hid_lo = signal("hid_lo", NGU)
        rt_exp = signal("rt_exp", 2)
        rt_sub = signal("rt_sub", 2)
        c_ready = signal("c_ready", 2)
        qm_ready = signal("qm_ready", 2)
        a_mm = signal("a_mm", 3 * W1G)
        a_max = signal("a_max", 8 * W1G)
        a_shift = signal("a_shift", 2 * W1G)
        a_exp = signal("a_exp", 8 * W1G)
        at_mm = signal("at_mm", 3 * W1G)
        at_hi = signal("at_hi", 3 * W1G)
        at_lo = signal("at_lo", 3 * W1G)
        v_chain = signal("v_chain", CHAIN)
        g_chain = signal("g_chain", 4 * U0 + 8)

        passed_pool = sem("passed_pool")
        passed_dve = sem("passed_dve")

        with nc.Block() as block:
            @block.sync
            def _(sp):
                for n in range(NCHUNK):
                    if n >= RING:
                        sp.wait_ge(w_lo, n - RING + 1)
                    sp.dma_start(stage[n % RING], wall[:, n * CHUNK:(n + 1) * CHUNK]).then_inc(ld_stage[n % RING], 16)
                for z in signals:
                    sp.sem_inc(z.handle, z.per * z.unit)

            @block.scalar
            def _(act):
                for n in range(NCHUNK):
                    act.wait_ge(ld_stage[n % RING], 16 * (n // RING + 1))
                    nc.scalar.activation(whi[:, n * CHUNK:(n + 1) * CHUNK], stage[n % RING], ACT.Copy,
                                         scale=WS).then_inc(w_hi, 1)

            @block.vector
            def _(dve):
                for n in range(NCHUNK):
                    dve.wait_ge(w_hi, n + 1)
                    nc.vector.scalar_tensor_tensor(out=wlo[:, n * CHUNK:(n + 1) * CHUNK], in0=stage[n % RING],
                                                   scalar=WS, in1=whi[:, n * CHUNK:(n + 1) * CHUNK],
                                                   op0=ALU.mult, op1=ALU.subtract).then_inc(w_lo, 1)

        def n_ln(k, s):
            return 2 * k + s + 1

        def n_o(stage_, s):
            return 2 * stage_ + s + 1

        def n_gu(f, v):
            return (2 * J0 if f else 0) + v + 1

        def ff_dims(f):
            return (J1 if f else J0), ("w1" if f else "g"), ("w3" if f else "u"), ("w2" if f else "d")

        o_bank = {(1, 0): 6, (1, 1): 7, (3, 0): 6, (3, 1): 7}

        with nc.Block() as block:
            @block.sync
            def _(sp):
                with sp.Fori(0, NPAIR) as i:
                    for s in range(2):
                        sp.wait_ge(o_read.handle, o_read.count(i, n_o(0, s) - 8))
                        sp.dma_start(xin[:, s], x_in[2 * i + s].rearrange("(t p) d -> p t d", p=P)).then_inc(ld_x[s].handle, 16)
                    for l in range(2):
                        for s in range(2):
                            if l == 0:
                                sp.wait_ge(o_read.handle, o_read.count(i, n_o(3, s) - 8))
                            else:
                                sp.wait_ge(o_read.handle, o_read.count(i, n_o(1, s)))
                            sp.dma_start(gate[:, s], gates_dram[2 * i + s, l * 512:(l + 1) * 512]
                                         .rearrange("(k n) -> k n", k=2).partition_broadcast(P)).then_inc(ld_g[s].handle, 16)

            @block.tensor
            def _(pe):
                def mm3(dst, lhs, rhs, start, stop, skip=False):
                    nc.tensor.matmul(dst, lhs[0], rhs[0], start=start, stop=False, skip_group_check=skip)
                    nc.tensor.matmul(dst, lhs[0], rhs[1], start=False, stop=False, skip_group_check=skip)
                    return nc.tensor.matmul(dst, lhs[1], rhs[0], start=False, stop=stop, skip_group_check=skip)

                with pe.Fori(0, NPAIR) as i:
                    def wait(z, n):
                        pe.wait_ge(z.handle, z.count(i, n))

                    def misc_begin(key):
                        wait(misc_free, MISC[key] - 1)

                    def transposes4(src):
                        for c in range(DC):
                            for t in range(TT):
                                last = nc.tensor.transpose(misc[:, c * T + t * P:c * T + (t + 1) * P],
                                                           src[:, t, c * P:(c + 1) * P], ident)
                        last.then_inc(misc_mm.handle, 1)

                    def h_of(s, c, t=None):
                        if t is None:
                            return hth[:, s, c, :], htl[:, s, c, :]
                        return hth[:, s, c, t * P:(t + 1) * P], htl[:, s, c, t * P:(t + 1) * P]

                    def qk_turn(e, t):
                        misc_begin(("t1", e, t))
                        wait(rope_sum, 2 * e + t + 1)
                        wait(k_norm, 2 * e + t + 1)
                        for k in range(3):
                            last = nc.tensor.transpose(misc[:, k * P:(k + 1) * P], ra[:, t, k, :], ident)
                        last.then_inc(misc_mm.handle, 1)

                    def qkv(e, t):
                        s, g = divmod(e, NKV)
                        if g == 0 and t == 0:
                            wait(h_lo, n_ln(0, s))
                        wait(rope_mul, 2 * (e - 1) + t + 1)
                        for c in range(DC):
                            last = mm3(bank[t][:, :], h_of(s, c, t), w_of("qkv", c * 4096 + g * 512, 512),
                                       c == 0, c == DC - 1)
                        last.then_inc(qkv_mm.handle, 1)

                    def p_turn(e, b):
                        y = e % 2
                        if b == 0:
                            wait(p_norm, 4 * (e + 1))
                        wait(pt_lo, 2 * e + b)
                        for kt in range(b + 1):
                            for k in range(2):
                                a = (b + kt) * P
                                last = nc.tensor.transpose(bank[5][:, (2 * kt + k) * P:(2 * kt + k + 1) * P],
                                                           smx[:, y, k, a:a + P], ident)
                        last.then_inc(pt_mm.handle, 1)

                    def scores(e):
                        wait(misc_free, MISC[("t1", e, 1)])
                        wait(s_max, 4 * e)
                        for k in range(2):
                            last = mm3(bank[3][:, k * P:(k + 1) * P], (qkh[:, k, 0:P], qkl[:, k, 0:P]),
                                       (qkh[:, 2, 0:P], qkl[:, 2, 0:P]), True, True)
                        last.then_inc(s_mm.handle, 1)
                        for k in range(2):
                            last = mm3(bank[4][:, k * T:(k + 1) * T], (qkh[:, k, P:T], qkl[:, k, P:T]),
                                       (qkh[:, 2, :], qkl[:, 2, :]), True, True)
                        last.then_inc(s_mm.handle, 1)

                    def project(e):
                        s, g = divmod(e, NKV)
                        wait(enc_lo, e + 1)
                        if g == 0:
                            wait(o_read, n_o(3, 1) - 8 if s == 0 else n_o(0, 0))
                        for k in range(2):
                            for t in range(TT):
                                first = g == 0 and k == 0 and t == 0
                                last = mm3(bank[7][:, t * D:(t + 1) * D], (ench[:, t, k, :], encl[:, t, k, :]),
                                           w_of("o", (2 * g + k) * D, D), first, g == NKV - 1 and k == 1, skip=True)
                        if g == NKV - 1:
                            last.then_inc(o_mm.handle, 1)

                    def encode(e):
                        wait(pt_lo, 2 * (e + 1))
                        if e == 0:
                            wait(o_read, n_o(3, 0) - 8)
                        v = e % 4
                        mm3(bank[6][:, 0:T], (vh0[:, v, 0, :], vl0[:, v, 0, :]),
                            (pth[:, 0:2, :], ptl[:, 0:2, :]), True, True)
                        mm3(bank[6][:, T:2 * T], (vh0[:, v, 0, :], vl0[:, v, 0, :]),
                            (pth[:, 2:4, :], ptl[:, 2:4, :]), True, False)
                        last = mm3(bank[6][:, T:2 * T], (vh0[:, v, 1, :], vl0[:, v, 1, :]),
                                   (pth[:, 4:6, :], ptl[:, 4:6, :]), False, True)
                        last.then_inc(enc_mm.handle, 1)

                    def at0(u):
                        if 0 <= u - 3 < U0:
                            p_turn(u - 3, 0)
                        if 0 <= u - 2 < U0:
                            scores(u - 2)
                        if 0 <= u - 3 < U0:
                            p_turn(u - 3, 1)
                        if 0 <= u - 1 < U0:
                            qk_turn(u - 1, 0)
                        if u < U0:
                            qkv(u, 0)
                        if 0 <= u - 4 < U0:
                            project(u - 4)
                        if 0 <= u - 1 < U0:
                            qk_turn(u - 1, 1)
                        if u < U0:
                            qkv(u, 1)
                        if 0 <= u - 3 < U0:
                            encode(u - 3)

                    def ff(f, v):
                        J, wg, wu, wd = ff_dims(f)
                        stage_ = 3 if f else 1
                        if v < 2 * J:
                            s, j = divmod(v, J)
                            n = n_gu(f, v)
                            if j == 0:
                                wait(h_lo, n_ln(3 if f else 1, s))
                            if not f and v < 2:
                                wait(rope_mul, 2 * U0)
                            elif f and v < 2:
                                wait(a_max, 8 * W1G)
                            else:
                                wait(gu_read, n - 2)
                            bk = bank[(n - 1) % 2]
                            bias = not f and j >= JB
                            for k, name in enumerate((wg, wu)):
                                for c in range(DC):
                                    last = mm3(bk[:, k * T:(k + 1) * T],
                                               w_of(name, c * J * P + j * P, P), h_of(s, c), c == 0,
                                               c == DC - 1 and not bias)
                                if bias:
                                    a = (BG, BU)[k] + (j - JB) * P
                                    last = nc.tensor.matmul(bk[:, k * T:(k + 1) * T], brows[:, a:a + P], ones[:, :],
                                                            start=False, stop=True)
                            last.then_inc(gu_mm.handle, 1)
                            if not f:
                                if j == 0:
                                    wait(misc_free, MISC[("ct", s)])
                                if v < 2:
                                    wait(s_max, 4 * U0)
                                else:
                                    wait(ce_read, v - 1)
                                nc.tensor.matmul(bank[3 + v % 2][:, 0:T], sel[:, j * P:(j + 1) * P], ctt[:, s, :],
                                                 start=True, stop=True).then_inc(ce_mm.handle, 1)
                        if v >= 2:
                            s, j = divmod(v - 2, J)
                            n = n_gu(f, v - 2)
                            wait(hid_lo, n)
                            ob = bank[o_bank[(stage_, s)]]
                            if j == 0:
                                if s == 0:
                                    wait(*((at_lo, 3 * W1G) if f else (enc_lo, U0)))
                                else:
                                    wait(o_read, n_o(stage_ - 1, 1))
                            z = (n - 1) % 3
                            for t in range(TT):
                                last = mm3(ob[:, t * D:(t + 1) * D],
                                           (fh[:, z, t * P:(t + 1) * P], fl[:, z, t * P:(t + 1) * P]),
                                           w_of(wd, j * D, D), j == 0 and t == 0, f == 1 and j == J - 1, skip=True)
                                if not f and j == J - 1:
                                    last = nc.tensor.matmul(ob[:, t * D:(t + 1) * D], ones[:, 0:P], brows[:, BD:BD + D],
                                                            start=False, stop=True, skip_group_check=True)
                            if j == J - 1:
                                last.then_inc(o_mm.handle, 1)

                    def scores1(w):
                        s, gr = divmod(w, 8)
                        c, g = divmod(gr, 4)
                        if gr == 0:
                            wait(qm_ready, s + 1)
                            wait(misc_free, MISC[("k1", s)])
                        if w == 0:
                            wait(gu_read, 2 * J0)
                            wait(ce_read, 2 * J0)
                        wait(a_max, 8 * w)
                        rows = slice(32 * g, 32 * g + 32)
                        for j in range(4):
                            q = slice(c * T, c * T + P)
                            last = mm3(bank[0][:, j * P:(j + 1) * P], (qmh[rows, j, q], qml[rows, j, q]),
                                       (k1h[rows, s, c, 0:P], k1l[rows, s, c, 0:P]), True, True)
                        last.then_inc(a_mm.handle, 1)
                        for j in range(4):
                            q = slice(c * T + P, (c + 1) * T)
                            last = mm3(bank[(1, 3)[j // 2]][:, j % 2 * T:(j % 2 + 1) * T],
                                       (qmh[rows, j, q], qml[rows, j, q]),
                                       (k1h[rows, s, c, :], k1l[rows, s, c, :]), True, True)
                            if j % 2:
                                last.then_inc(a_mm.handle, 1)

                    def p_turn1(w):
                        y = w % 2
                        for b in range(3):
                            wait(a_exp, 8 * w + (4 if b == 0 else 8))
                            wait(at_lo, 3 * (w - 1) + b + 1)
                            if w == 0 and b == 2:
                                wait(o_read, n_o(1, 0))
                            for j in range(4):
                                last = nc.tensor.transpose(bank[4 + b][:, j * P:(j + 1) * P],
                                                           s1[:, y, j, b * P:(b + 1) * P], ident)
                            last.then_inc(at_mm.handle, 1)

                    def attend1(w):
                        s, gr = divmod(w, 8)
                        y = w % 2
                        wait(at_lo, 3 * (w + 1))
                        if gr == 0:
                            wait(misc_free, MISC[("v1", s)])
                            wait(o_read, n_o(1, 1) if s == 0 else n_o(2, 0))
                        for j in range(4):
                            d = (4 * gr + j) * HD1
                            for t in range(TT):
                                for kt in range(t + 1):
                                    b = t + kt
                                    last = mm3(bank[7][:, t * D + d:t * D + d + HD1],
                                               (p1h[:, y, b, j, :], p1l[:, y, b, j, :]),
                                               (v1h[:, s, kt, d:d + HD1], v1l[:, s, kt, d:d + HD1]),
                                               gr == 0 and j == 0 and t == 0, kt == t, skip=True)
                        if gr == 7:
                            last.then_inc(o_mm.handle, 1)

                    def at1(w):
                        if w < W1G:
                            scores1(w)
                        if 0 <= w - 1 < W1G:
                            p_turn1(w - 1)
                        if 0 <= w - 2:
                            attend1(w - 2)

                    for item in ORDER:
                        kind = item[0]
                        if kind == "at0":
                            at0(item[1])
                        elif kind in ("ff0", "ff1"):
                            ff(int(kind == "ff1"), item[1])
                        elif kind == "at1":
                            at1(item[1])
                        elif kind == "lnc":
                            misc_begin(item)
                            wait(ln_norm, n_ln(item[1], item[2]))
                            transposes4(xn)
                        elif kind == "rt":
                            misc_begin(item)
                            s = item[1]
                            wait(h_lo, n_ln(1, s))
                            for t in range(TT):
                                for c in range(DC):
                                    last = mm3(misc[:, t * EXPERTS:(t + 1) * EXPERTS], h_of(s, c, t),
                                               w_of("r", c * EXPERTS, EXPERTS), c == 0, c == DC - 1)
                            last.then_inc(misc_mm.handle, 1)
                        elif kind == "ct":
                            misc_begin(item)
                            wait(c_ready, item[1] + 1)
                            for t in range(TT):
                                last = nc.tensor.transpose(misc[0:17, t * P:(t + 1) * P], c17[:, t, :], ident)
                            last.then_inc(misc_mm.handle, 1)
                        elif kind in ("q1", "k1"):
                            misc_begin(item)
                            s = item[1]
                            wait(h_lo, n_ln(2, s))
                            a = 0 if kind == "q1" else D
                            for c2 in range(DC):
                                for c in range(DC):
                                    mm3(misc[:, c2 * T:(c2 + 1) * T], w_of("a1", c * 3 * D + a + c2 * P, P),
                                        h_of(s, c), c == 0, False)
                                b = BA + a + c2 * P
                                last = nc.tensor.matmul(misc[:, c2 * T:(c2 + 1) * T], brows[:, b:b + P], ones[:, :],
                                                        start=False, stop=True)
                            last.then_inc(misc_mm.handle, 1)
                        elif kind == "v1":
                            misc_begin(item)
                            s = item[1]
                            wait(h_lo, n_ln(2, s))
                            for t in range(TT):
                                for c in range(DC):
                                    mm3(misc[:, t * D:(t + 1) * D], h_of(s, c, t),
                                        w_of("a1", c * 3 * D + 2 * D, D), c == 0, False)
                                last = nc.tensor.matmul(misc[:, t * D:(t + 1) * D], ones[:, 0:P],
                                                        brows[:, BA + 2 * D:BA + 3 * D], start=False, stop=True)
                            last.then_inc(misc_mm.handle, 1)
                        elif kind == "at":
                            misc_begin(item)
                            wait(o_read, n_o(2, item[1]))
                            transposes4(xn)
                        elif kind == "pj":
                            misc_begin(item)
                            wait(misc_free, MISC[("at", item[1])])
                            for t in range(TT):
                                for c in range(DC):
                                    q = slice(c * T + t * P, c * T + (t + 1) * P)
                                    mm3(misc[:, t * D:(t + 1) * D], (q1h[:, q], q1l[:, q]), w_of("p1", c * D, D),
                                        c == 0, False)
                                last = nc.tensor.matmul(misc[:, t * D:(t + 1) * D], ones[:, 0:P],
                                                        brows[:, BP:BP + D], start=False, stop=True)
                            last.then_inc(misc_mm.handle, 1)

            @block.scalar
            def _(act):
                with act.Fori(0, NPAIR) as i:
                    def wait(z, n):
                        act.wait_ge(z.handle, z.count(i, n))

                    def copy_hi(dst, src, key, scale):
                        wait(misc_mm, MISC[key])
                        nc.scalar.activation(dst, src, ACT.Copy, scale=scale).then_inc(misc_hi.handle, 1)

                    def qk_hi(e, t):
                        copy_hi(qkh[:, :, t * P:(t + 1) * P], misc[:, 0:3 * P].rearrange("p (k n) -> p k n", k=3),
                                ("t1", e, t), 1.0 / WS)

                    def p_hi(e, b):
                        lo, hi = ((0, 2), (2, 6))[b]
                        wait(pt_mm, 2 * e + b + 1)
                        nc.scalar.activation(pth[:, lo:hi, :], bank[5][:, 0:(hi - lo) * P]
                                             .rearrange("p (k n) -> p k n", n=P), ACT.Copy).then_inc(pt_hi.handle, 1)

                    def stats(e, t):
                        wait(qkv_mm, 2 * e + t + 1)
                        nc.scalar.activation(vh0[:, e % 4, t, :], bank[t][:, 3 * P:4 * P], ACT.Copy, scale=1.0 / WS)
                        for k in range(3):
                            last = nc.scalar.activation(rb[:, t, k, :], bank[t][:, k * P:(k + 1) * P], ACT.Square,
                                                        accum_out=ss[:, 3 * t + k:3 * t + k + 1])
                        last.then_inc(qkv_act.handle, 1)

                    def exps(e, t):
                        y = e % 2
                        if t == 0:
                            wait(s_shift, e + 1)
                        for k in range(2):
                            a = smx[:, y, k, t * P:t * P + (t + 1) * P]
                            nc.scalar.activation(a, a, ACT.Exp, bias=nb0[:, y, 2 * t + k:2 * t + k + 1],
                                                 scale=rs0[:, e % 4, 3 * t + k:3 * t + k + 1],
                                                 accum_out=sm0[:, y, 2 * t + k:2 * t + k + 1]).then_inc(s_exp.handle, 1)

                    def exps1(w, t):
                        s, gr = divmod(w, 8)
                        y = w % 2
                        wait(a_shift, 2 * w + t + 1)
                        for j in range(4):
                            a = s1[:, y, j, t * P:t * P + (t + 1) * P]
                            nc.scalar.activation(a, a, ACT.Exp, bias=nb1[:, y, 4 * t + j:4 * t + j + 1],
                                                 accum_out=sum1[:, s, t, 4 * gr + j:4 * gr + j + 1])\
                                .then_inc(a_exp.handle, 1)

                    for item in ORDER:
                        kind = item[0]
                        if kind == "at0":
                            u = item[1]
                            if 0 <= u - 3 < U0:
                                p_hi(u - 3, 0)
                                p_hi(u - 3, 1)
                            if 0 <= u - 1 < U0:
                                qk_hi(u - 1, 0)
                            if 0 <= u - 2 < U0:
                                exps(u - 2, 0)
                            if u < U0:
                                stats(u, 0)
                            if 0 <= u - 2 < U0:
                                exps(u - 2, 1)
                            if 0 <= u - 1 < U0:
                                qk_hi(u - 1, 1)
                            if u < U0:
                                stats(u, 1)
                            if 0 <= u - 3 < U0:
                                wait(enc_mm, u - 2)
                                nc.scalar.activation(ench[:, :, :, :].rearrange("p t k n -> p (t k n)"), bank[6][:, :],
                                                     ACT.Copy).then_inc(enc_hi.handle, 1)
                        elif kind in ("ff0", "ff1"):
                            f, v = int(kind == "ff1"), item[1]
                            J = ff_dims(f)[0]
                            if v < 2 * J:
                                n = n_gu(f, v)
                                wait(gu_mm, n)
                                nc.scalar.activation(th[:, (n - 1) % 2, :], bank[(n - 1) % 2][:, 0:T], ACT.Tanh,
                                                     scale=0.5 / WS).then_inc(gu_tanh.handle, 1)
                            if 1 <= v <= 2 * J:
                                n = n_gu(f, v - 1)
                                z = (n - 1) % 3
                                if f:
                                    wait(gu_read, n)
                                else:
                                    wait(ce_read, v)
                                nc.scalar.activation(fh[:, z, :], fa[:, z, :], ACT.Copy).then_inc(hid_hi.handle, 1)
                        elif kind == "at1":
                            w = item[1]
                            if w < W1G:
                                exps1(w, 0)
                            if 0 <= w - 1 < W1G:
                                for b in range(3):
                                    wait(at_mm, 3 * (w - 1) + b + 1)
                                    nc.scalar.activation(p1h[:, (w - 1) % 2, b, :, :].rearrange("p j n -> p (j n)"),
                                                         bank[4 + b][:, :], ACT.Copy).then_inc(at_hi.handle, 1)
                            if w < W1G:
                                exps1(w, 1)
                        elif kind == "lnc":
                            k, s = item[1:]
                            wait(misc_free, MISC[item])
                            nc.scalar.activation(hth[:, s].rearrange("p c n -> p (c n)"), hf[:, :],
                                                 ACT.Copy).then_inc(h_hi.handle, 1)
                        elif kind == "rt":
                            wait(rt_sub, item[1] + 1)
                            nc.scalar.activation(rt_e, rt_a, ACT.Exp).then_inc(rt_exp.handle, 1)
                        elif kind == "q1":
                            copy_hi(q1h[:, :], misc[:, :], item, 1.0 / WS)
                        elif kind == "k1":
                            copy_hi(k1h[:, item[1]].rearrange("p c n -> p (c n)"), misc[:, :], item, 1.0 / WS)
                        elif kind == "v1":
                            copy_hi(v1h[:, item[1]].rearrange("p c n -> p (c n)"), misc[:, :], item, 1.0 / WS)
                        elif kind == "at":
                            copy_hi(q1h[:, :], misc[:, :], item, 1.0)
                        elif kind == "resf" and item[1] == 1:
                            s = item[2]
                            wait(o_read, n_o(3, s))
                            act.dma_start(out[2 * i + s].rearrange("(t p) d -> p t d", p=P), xs[:, s])\
                               .then_inc(st_x[s].handle, 16)
                for s in range(2):
                    act.wait_ge(st_x[s].handle, 16 * (NPAIR + 1))

            @block.gpsimd
            def _(pool):
                with pool.Fori(0, NPAIR) as i:
                    chained = [0]

                    def wait(z, n):
                        pool.wait_ge(z.handle, z.count(i, n))

                    def link(ins):
                        chained[0] += 1
                        ins.then_inc(g_chain.handle, 1)
                        wait(g_chain, chained[0])

                    for item in ORDER:
                        kind = item[0]
                        if kind == "lna":
                            wait(ln_stats, n_ln(item[1], item[2]))
                            pool.sem_inc(passed_pool, 1)
                            link(nc.gpsimd.tensor_scalar(lv, mv[:, :, 1], 1e-5, None, ALU.add))
                            nc.gpsimd.tensor_tensor(lr[:, 0:TT], lv, half[:, 0:TT], ALU.pow).then_inc(ln_rstd.handle, 1)
                        elif kind == "at0" and item[1] < U0:
                            u = item[1]
                            for t in range(TT):
                                k3 = slice(3 * t, 3 * t + 3)
                                wait(qkv_act, 2 * u + t + 1)
                                pool.sem_inc(passed_pool, 1)
                                link(nc.gpsimd.tensor_scalar(ms[:, k3], ss[:, k3], 1.0 / (HD * WS * WS), 1e-6,
                                                             ALU.mult, ALU.add))
                                link(nc.gpsimd.tensor_tensor(r0[:, u % 2, k3], ms[:, k3], half[:, 0:3], ALU.pow))
                                pool.sem_inc(passed_pool, 1)
                                nc.gpsimd.tensor_scalar(rs0[:, u % 4, k3], r0[:, u % 2, k3], ATT_SCALE, None, ALU.mult)\
                                    .then_inc(qk_rstd.handle, 1)
                                wait(rope_mul, 2 * u + t + 1)
                                a, b = (z[:, t].rearrange("p k h -> p (k h)") for z in (ra, rb))
                                nc.gpsimd.tensor_tensor(a, a, b, ALU.add).then_inc(rope_sum.handle, 1)
                                wait(rope_sum, 2 * u + t + 1)
                                pool.sem_inc(passed_pool, 1)
                                nc.gpsimd.tensor_scalar(ra[:, t, 2, :], ra[:, t, 2, :],
                                                        r0[:, u % 2, 3 * t + 2:3 * t + 3], None,
                                                        ALU.mult).then_inc(k_norm.handle, 1)
                        elif kind in ("ff0", "ff1"):
                            f, v = int(kind == "ff1"), item[1]
                            J = ff_dims(f)[0]
                            if 1 <= v <= 2 * J:
                                n = n_gu(f, v - 1)
                                z = (n - 1) % 3
                                wait(hid_hi, n)
                                nc.gpsimd.tensor_tensor(fl[:, z, :], fa[:, z, :], fh[:, z, :], ALU.subtract)\
                                    .then_inc(hid_lo.handle, 1)
                    assert chained[0] == g_chain.per, chained[0]

            @block.vector
            def _(dve):
                with dve.Fori(0, NPAIR) as i:
                    chained = [0]

                    def wait(z, n):
                        dve.wait_ge(z.handle, z.count(i, n))

                    def link(ins):
                        chained[0] += 1
                        ins.then_inc(v_chain.handle, 1)
                        wait(v_chain, chained[0])

                    def split_lo(dst, src, hi, key, scale):
                        wait(misc_hi, MISC_HI[key])
                        nc.vector.scalar_tensor_tensor(out=dst, in0=src, scalar=scale, in1=hi, op0=ALU.mult,
                                                       op1=ALU.subtract).then_inc(misc_free.handle, 1)

                    def residual(ps, s, k, into, base):
                        tmp = hf[:, :].rearrange("p (t d) -> p t d", t=TT)
                        g = gate[:, s, k:k + 1, :].to_broadcast([P, TT, D])
                        n = nc.vector.tensor_tensor(tmp, ps[:, :].rearrange("p (t d) -> p t d", t=TT), g, ALU.mult)
                        return n, lambda: nc.vector.tensor_tensor(into, tmp, base, ALU.add)

                    def qk_lo(e, t):
                        c = slice(t * P, (t + 1) * P)
                        split_lo(qkl[:, :, c], misc[:, 0:3 * P].rearrange("p (k n) -> p k n", k=3),
                                 qkh[:, :, c], ("t1", e, t), 1.0 / WS)

                    def p_lo(e, b):
                        lo, hi = ((0, 2), (2, 6))[b]
                        wait(pt_hi, 2 * e + b + 1)
                        nc.vector.tensor_tensor(ptl[:, lo:hi, :], bank[5][:, 0:(hi - lo) * P]
                                                .rearrange("p (k n) -> p k n", n=P), pth[:, lo:hi, :],
                                                ALU.subtract).then_inc(pt_lo.handle, 1)

                    def rope_products(e, t):
                        wait(qkv_act, 2 * e + t + 1)
                        nc.vector.scalar_tensor_tensor(out=vl0[:, e % 4, t, :], in0=bank[t][:, 3 * P:4 * P],
                                                       scalar=1.0 / WS, in1=vh0[:, e % 4, t, :],
                                                       op0=ALU.mult, op1=ALU.subtract)
                        src = bank[t][:, 0:3 * P].rearrange("p (k h) -> p k h", k=3)
                        nc.vector.tensor_tensor(ra[:, t], src, ropec[:, t], ALU.mult)
                        hh = HD // 2
                        nc.vector.tensor_tensor(rb[:, t, :, 0:hh], src[:, :, hh:HD], ropes[:, t, :, 0:hh], ALU.mult)
                        nc.vector.tensor_tensor(rb[:, t, :, hh:HD], src[:, :, 0:hh], ropes[:, t, :, hh:HD], ALU.mult)\
                            .then_inc(rope_mul.handle, 1)

                    def mask_max(e):
                        y = e % 2
                        for t in range(TT):
                            wait(s_mm, 2 * e + t + 1)
                            dve.sem_inc(passed_dve, 1)
                            n = (t + 1) * P
                            for k in range(2):
                                nc.vector.tensor_tensor_reduce(
                                    out=smx[:, y, k, t * P:t * P + n], in0=bank[3 + t][:, k * n:(k + 1) * n],
                                    in1=mask0[:, t * P:t * P + n], scale=1.0, scalar=-3e38, op0=ALU.add,
                                    op1=ALU.max, accum_out=mx0[:, y, 2 * t + k:2 * t + k + 1]).then_inc(s_max.handle, 1)
                        wait(s_max, 4 * (e + 1))
                        wait(qk_rstd, 2 * (e + 1))
                        nc.vector.scalar_tensor_tensor(
                            out=nb0[:, y, :].rearrange("p (t k) -> p t k", t=TT),
                            in0=mx0[:, y, :].rearrange("p (t k) -> p t k", t=TT), scalar=-1.0,
                            in1=rs0[:, e % 4, :].rearrange("p (t k) -> p t k", t=TT)[:, :, 0:2],
                            op0=ALU.mult, op1=ALU.mult).then_inc(s_shift.handle, 1)

                    def normalise(e):
                        y = e % 2
                        wait(s_exp, 4 * (e + 1))
                        link(nc.vector.reciprocal(ri0[:, y, :], sm0[:, y, :]))
                        for t in range(TT):
                            for k in range(2):
                                a = smx[:, y, k, t * P:t * P + (t + 1) * P]
                                nc.vector.tensor_scalar(a, a, ri0[:, y, 2 * t + k:2 * t + k + 1], None,
                                                        ALU.mult).then_inc(p_norm.handle, 1)

                    def at0(u):
                        if 0 <= u - 3 < U0:
                            p_lo(u - 3, 0)
                        if 0 <= u - 2 < U0:
                            mask_max(u - 2)
                        if 0 <= u - 3 < U0:
                            p_lo(u - 3, 1)
                        if 0 <= u - 1 < U0:
                            qk_lo(u - 1, 0)
                        if u < U0:
                            rope_products(u, 0)
                        if 0 <= u - 2 < U0:
                            normalise(u - 2)
                        if 0 <= u - 1 < U0:
                            qk_lo(u - 1, 1)
                        if u < U0:
                            rope_products(u, 1)
                        if 0 <= u - 3 < U0:
                            wait(enc_hi, u - 2)
                            nc.vector.tensor_tensor(encl[:, :, :, :].rearrange("p t k n -> p (t k n)"), bank[6][:, :],
                                                    ench[:, :, :, :].rearrange("p t k n -> p (t k n)"),
                                                    ALU.subtract).then_inc(enc_lo.handle, 1)

                    def ff(f, v):
                        J = ff_dims(f)[0]
                        if v >= 2 * J:
                            return
                        n = n_gu(f, v)
                        z, bk = (n - 1) % 3, bank[(n - 1) % 2]
                        wait(gu_tanh, n)
                        link(nc.vector.scalar_tensor_tensor(out=fa[:, z, :], in0=th[:, (n - 1) % 2, :], scalar=1.0,
                                                            in1=bk[:, 0:T], op0=ALU.add, op1=ALU.mult))
                        nc.vector.scalar_tensor_tensor(out=fa[:, z, :], in0=fa[:, z, :],
                                                       scalar=0.5 / (WS * WS) if f else 1.0, in1=bk[:, T:2 * T],
                                                       op0=ALU.mult, op1=ALU.mult).then_inc(gu_read.handle, 1)
                        if not f:
                            wait(gu_read, n)
                            wait(ce_mm, v + 1)
                            nc.vector.tensor_tensor(fa[:, z, :], fa[:, z, :], bank[3 + v % 2][:, 0:T], ALU.mult)\
                                .then_inc(ce_read.handle, 1)

                    def at1(w):
                        if w < W1G:
                            y = w % 2
                            for t in range(TT):
                                n = (t + 1) * P
                                for j in range(4):
                                    if t == 0 and j == 0:
                                        wait(a_mm, 3 * w + 1)
                                    if t == 1 and j % 2 == 0:
                                        wait(a_mm, 3 * w + 2 + j // 2)
                                    dve.sem_inc(passed_dve, 1)
                                    src = bank[0][:, j * P:(j + 1) * P] if t == 0 else \
                                        bank[(1, 3)[j // 2]][:, j % 2 * T:(j % 2 + 1) * T]
                                    nc.vector.tensor_tensor_reduce(
                                        out=s1[:, y, j, t * P:t * P + n], in0=src, in1=bias1[:, t * P:t * P + n],
                                        scale=1.0, scalar=-3e38, op0=ALU.add, op1=ALU.max,
                                        accum_out=mx1[:, y, 4 * t + j:4 * t + j + 1]).then_inc(a_max.handle, 1)
                                wait(a_max, 8 * w + 4 * (t + 1))
                                nc.vector.tensor_scalar(nb1[:, y, 4 * t:4 * t + 4], mx1[:, y, 4 * t:4 * t + 4], -1.0,
                                                        None, ALU.mult).then_inc(a_shift.handle, 1)
                        if 1 <= w <= W1G:
                            for b in range(3):
                                wait(at_hi, 3 * (w - 1) + b + 1)
                                z = (w - 1) % 2
                                nc.vector.tensor_tensor(p1l[:, z, b, :, :].rearrange("p j n -> p (j n)"),
                                                        bank[4 + b][:, :],
                                                        p1h[:, z, b, :, :].rearrange("p j n -> p (j n)"),
                                                        ALU.subtract).then_inc(at_lo.handle, 1)

                    def route(s):
                        nc.vector.tensor_scalar(rt_l, misc[:, 0:TT * EXPERTS].rearrange("p (t e) -> p t e", t=TT),
                                                1.0 / WS, None, ALU.mult).then_inc(misc_free.handle, 1)
                        wait(misc_free, MISC[("rt", s)])
                        bc = lambda k: rt_m[:, k, :].unsqueeze(2).to_broadcast([P, TT, EXPERTS])
                        io = iota.unsqueeze(1).to_broadcast([P, TT, EXPERTS])
                        link(nc.vector.tensor_reduce(rt_m[:, 0, :], rt_l, AX.X, ALU.max))
                        nc.vector.tensor_tensor(rt_a, rt_l, bc(0), ALU.subtract).then_inc(rt_sub.handle, 1)
                        wait(rt_sub, s + 1)

                        def pick(src, k, kept):
                            link(nc.vector.tensor_tensor(kept, src, bc(k), ALU.is_ge))
                            link(nc.vector.tensor_tensor(kept, kept, io, ALU.mult))
                            link(nc.vector.tensor_reduce(rt_m[:, 2, :], kept, AX.X, ALU.max))
                            link(nc.vector.tensor_tensor(kept, io, bc(2), ALU.is_equal))

                        pick(rt_l, 0, rt_k)
                        link(nc.vector.scalar_tensor_tensor(out=rt_l, in0=rt_k, scalar=-3e38, in1=rt_l,
                                                            op0=ALU.mult, op1=ALU.add))
                        link(nc.vector.tensor_reduce(rt_m[:, 1, :], rt_l, AX.X, ALU.max))
                        pick(rt_l, 1, rt_k2)
                        link(nc.vector.tensor_tensor(rt_k, rt_k, rt_k2, ALU.add))
                        wait(rt_exp, s + 1)
                        link(nc.vector.tensor_tensor(rt_e, rt_e, rt_k, ALU.mult))
                        link(nc.vector.tensor_reduce(rt_m[:, 3, :], rt_e, AX.X, ALU.add))
                        link(nc.vector.reciprocal(rt_m[:, 3, :], rt_m[:, 3, :]))
                        link(nc.vector.tensor_tensor(rt_e, rt_e, bc(3), ALU.mult))
                        link(nc.vector.tensor_copy(ch16, rt_e))
                        link(nc.vector.tensor_copy(c17[:, :, 0:8], ch16))
                        nc.vector.tensor_tensor(c17[:, :, 9:17], rt_e, ch16, ALU.subtract).then_inc(c_ready.handle, 1)

                    for item in ORDER:
                        kind = item[0]
                        if kind == "at0":
                            at0(item[1])
                        elif kind in ("ff0", "ff1"):
                            ff(int(kind == "ff1"), item[1])
                        elif kind == "at1":
                            at1(item[1])
                        elif kind == "mc":
                            link(nc.vector.tensor_copy(mcol[:, item[1], :], modt[:, 2 * i + item[1], :]))
                        elif kind == "lna":
                            k, s = item[1:]
                            if k == 0:
                                wait(ld_x[s], 1)
                            src = xin if k == 0 else xs
                            for t in range(TT):
                                ins = nc.vector.bn_stats(st6[:, t, :], src[:, s, t, :])
                            link(ins)
                            dve.sem_inc(passed_dve, 1)
                            for t in range(TT):
                                ins = nc.vector.bn_aggr(mv[:, t, :], st6[:, t, :])
                            ins.then_inc(ln_stats.handle, 1)
                        elif kind == "lnb":
                            k, s = item[1:]
                            src = xin if k == 0 else xs
                            wait(ln_rstd, n_ln(k, s))
                            for t in range(TT):
                                ins = nc.vector.tensor_scalar(xn[:, t, :], src[:, s, t, :], mv[:, t, 0:1],
                                                              lr[:, t:t + 1], ALU.subtract, ALU.mult)
                            ins.then_inc(ln_norm.handle, 1)
                        elif kind == "lnc":
                            k, s = item[1:]
                            wait(misc_mm, MISC[item])
                            for c in range(DC):
                                a = 4 * k + c
                                ins = nc.vector.tensor_scalar(hf[:, c * T:(c + 1) * T], misc[:, c * T:(c + 1) * T],
                                                              mcol[:, s, a:a + 1], mcol[:, s, a + 2:a + 3],
                                                              ALU.mult, ALU.add)
                            ins.then_inc(misc_free.handle, 1)
                            wait(misc_free, MISC[item])
                            wait(h_hi, n_ln(k, s))
                            nc.vector.tensor_tensor(htl[:, s].rearrange("p c n -> p (c n)"), hf[:, :],
                                                    hth[:, s].rearrange("p c n -> p (c n)"), ALU.subtract)\
                                .then_inc(h_lo.handle, 1)
                        elif kind == "rt":
                            wait(misc_mm, MISC[item])
                            route(item[1])
                        elif kind == "ct":
                            wait(misc_mm, MISC[item])
                            nc.vector.tensor_copy(ctt[:, item[1], :], misc[0:17, 0:T]).then_inc(misc_free.handle, 1)
                        elif kind == "res0":
                            s = item[1]
                            wait(o_mm, n_o(0, s))
                            wait(ld_g[s], 1)
                            wait(st_x[s], 0)
                            ins, add = residual(bank[7], s, 0, xs[:, s], xin[:, s])
                            link(ins)
                            add().then_inc(o_read.handle, 1)
                            wait(o_read, n_o(0, s))
                        elif kind == "resf":
                            f, s = item[1:]
                            stage_ = 3 if f else 1
                            wait(o_mm, n_o(stage_, s))
                            ins, add = residual(bank[o_bank[(stage_, s)]], s, 1, xs[:, s], xs[:, s])
                            link(ins)
                            add().then_inc(o_read.handle, 1)
                            wait(o_read, n_o(stage_, s))
                        elif kind == "q1":
                            split_lo(q1l[:, :], misc[:, :], q1h[:, :], item, 1.0 / WS)
                            wait(misc_free, MISC[item])
                        elif kind == "k1":
                            s = item[1]
                            split_lo(k1l[:, s].rearrange("p c n -> p (c n)"), misc[:, :],
                                     k1h[:, s].rearrange("p c n -> p (c n)"), item, 1.0 / WS)
                        elif kind == "v1":
                            s = item[1]
                            split_lo(v1l[:, s].rearrange("p c n -> p (c n)"), misc[:, :],
                                     v1h[:, s].rearrange("p c n -> p (c n)"), item, 1.0 / WS)
                        elif kind == "qm":
                            s = item[1]
                            wait(a_mm, 24 * s)
                            for j in range(4):
                                for src, dst in ((q1h, qmh), (q1l, qml)):
                                    ins = nc.vector.tensor_scalar(dst[:, j, :], src[:, :], con[:, K_HM + j:K_HM + j + 1],
                                                                  None, ALU.mult)
                            ins.then_inc(qm_ready.handle, 1)
                        elif kind == "pvr":
                            s = item[1]
                            link(nc.vector.reciprocal(ri1, sum1[:, s]))
                            wait(o_mm, n_o(2, s))
                            rb1 = ri1.rearrange("p t h -> p (t h)").unsqueeze(2).to_broadcast([P, TT * H1, HD1])
                            nc.vector.tensor_tensor(xn[:, :, :].rearrange("p t (h e) -> p (t h) e", e=HD1),
                                                    bank[7][:, :].rearrange("p (n e) -> p n e", e=HD1), rb1,
                                                    ALU.mult).then_inc(o_read.handle, 1)
                        elif kind == "at":
                            split_lo(q1l[:, :], misc[:, :], q1h[:, :], item, 1.0)
                        elif kind == "pj":
                            s = item[1]
                            wait(misc_mm, MISC[item])
                            wait(ld_g[s], 2)
                            ins, add = residual(misc, s, 0, xs[:, s], xs[:, s])
                            link(ins)
                            add().then_inc(misc_free.handle, 1)
                            wait(misc_free, MISC[item])
                    assert chained[0] <= CHAIN, chained[0]
                    dve.sem_inc(v_chain.handle, CHAIN - chained[0])


def _constants():
    rows = np.arange(P)[:, None]
    con = np.zeros((P, NC), np.float32)
    con[:, K_ID:K_ID + P] = np.eye(P)
    ramp = 2.0 ** (-8.0 / H1)
    for t in range(TT):
        keys = np.arange((t + 1) * P)[None, :]
        q = t * P + rows
        seen = keys <= q
        a, b = t * P, t * P + (t + 1) * P
        con[:, K_M0 + a:K_M0 + b] = np.where(seen & (q - keys < WINDOW), 0.0, NEG)
        con[:, K_M1 + a:K_M1 + b] = np.where(seen, (keys - q) * ramp, NEG)
    for j in range(4):
        con[:, K_HM + j] = (np.arange(P) % 32 // HD1 == j) * (HD1 ** -0.5)
    con[:, K_IO:K_IO + EXPERTS] = np.arange(EXPERTS, 0, -1)
    con[0, K_BS] = 1.0
    con[1, K_BS + 1] = 1.0
    bits = np.arange(P)[:, None] & np.arange(P)[None, :]
    ones = np.array([[bin(v).count("1") % 2 for v in row] for row in bits])
    had = (1.0 - 2.0 * ones).astype(np.float32)
    frac = np.arange(0, HD, 2, dtype=np.float32) / np.float32(HD)
    turn = np.arange(T, dtype=np.float32)[:, None] / (np.float32(10000.0) ** frac)
    cos, sin = np.cos(turn).astype(np.float32), np.sin(turn).astype(np.float32)
    rope = np.stack([np.concatenate([cos, cos], 1), np.concatenate([-sin, sin], 1)])
    rope = np.ascontiguousarray(rope.reshape(2, TT, P, HD).transpose(2, 0, 1, 3))
    sel = np.zeros((17, HP), np.float16)
    for h in range(HID0):
        e = h // INNER
        if e < EXPERTS:
            sel[e, h] = sel[9 + e, h] = 0.5 / (WS * WS)
        else:
            sel[8, h] = 0.5 / (WS * WS)
    return con, had, rope, sel


def _tiles(w, n=None):
    w = np.asarray(w)
    if n is not None and w.shape[1] < n:
        w = np.concatenate([w, np.zeros((w.shape[0], n - w.shape[1]), w.dtype)], 1)
    return w.reshape(-1, P, w.shape[1]).transpose(1, 0, 2).reshape(P, -1)


def _layout(v):
    v = {k: np.asarray(a) for k, a in v.items()}
    q, kv = v["L0_attn_q_kernel"], v["L0_attn_kv_kernel"]
    qkv = np.stack([q[0::2], q[1::2], kv[0], kv[1]], 0)
    qkv = qkv.reshape(4, NKV, DC, P, HD).transpose(3, 2, 1, 0, 4).reshape(P, -1)
    side = lambda name: v[name].transpose(1, 0, 2).reshape(D, EXPERTS * INNER)
    gate = np.concatenate([side("L0_ffn_gate_w"), v["L0_ffn_s_gate_w"]], 1)
    up = np.concatenate([side("L0_ffn_up_w"), v["L0_ffn_s_up_w"]], 1)
    down = np.concatenate([v["L0_ffn_down_w"].reshape(EXPERTS * INNER, D), v["L0_ffn_s_down_w"],
                           np.zeros((HP - HID0, D), np.float32)], 0)
    wall = np.concatenate([
        qkv, v["L0_attn_out_kernel"].transpose(1, 0, 2).reshape(P, NH * D), _tiles(gate, HP), _tiles(up, HP),
        _tiles(down), _tiles(v["L0_ffn_router_w"].T), _tiles(v["L1_attn_W_attn"]), _tiles(v["L1_attn_W_proj"]),
        _tiles(v["L1_ffn_W1"].T), _tiles(v["L1_ffn_W3"].T)], 1)
    w2t = _tiles(v["L1_ffn_W2"].T)
    shared = np.zeros((2, (J0 - JB) * P), np.float32)
    shared[0, :SHARED] = v["L0_ffn_s_gate_b"]
    shared[1, :SHARED] = v["L0_ffn_s_up_b"]
    brow = np.concatenate([shared.reshape(-1), v["L0_ffn_s_down_b"], v["L1_attn_b_attn"], v["L1_attn_b_proj"]])
    qs, ks = v["L0_attn_q_norm_scale"], v["L0_attn_k_norm_scale"]
    turned = lambda s: np.concatenate([s[HD // 2:], s[:HD // 2]])
    nsc = np.stack([np.stack([qs, qs, ks]), np.stack([turned(qs), turned(qs), turned(ks)])])
    per_layer = lambda a, b: np.stack([_tiles(a).reshape(P, DC, -1), _tiles(b).reshape(P, DC, -1)], 1)
    ct = per_layer(v["L0_c"].T, v["L1_c"].T)
    wmod = per_layer(v["L0_wmod"], v["L1_wmod"])
    con, had, rope, sel = _constants()
    return {"x": v["L0_attn_x"], "wall": wall, "w2t": w2t, "brow": brow, "con": con, "had": had, "rope": rope,
            "nsc": nsc, "sel": sel, "ct": ct, "wmod": wmod}


def kernel(**inputs):
    import concourse.bacc as _bacc
    from concourse.bass_utils import run_bass_kernel_spmd as _run

    assert JB * P == EXPERTS * INNER
    nc = _bacc.Bacc("TRN2", target_bir_lowering=False, num_devices=1, dynamic_dma_scratch_size=1024)
    arrays, args = {}, []
    for name, a in _layout(inputs).items():
        a = np.ascontiguousarray(a)
        arrays[f"in_{name}_dram"] = a
        args.append(nc.dram_tensor(f"in_{name}_dram", a.shape, mybir.dt.from_np(a.dtype), kind="ExternalInput").ap())
    out = nc.dram_tensor("out_dram", (B, T, D), F32, kind="ExternalOutput").ap()
    gates = nc.dram_tensor("gates_dram", (B, 4 * D), F32, kind="Internal").ap()
    build(nc, *args, out, gates)
    r = _run(nc, [arrays], core_ids=[0])
    return r.results[0]["out_dram"]
```

```python
from contextlib import ExitStack

import numpy as np

import concourse.bass as bass
from concourse import mybir

F32 = mybir.dt.float32
F16 = mybir.dt.float16
I32 = mybir.dt.int32
ALU = mybir.AluOpType
ACT = mybir.ActivationFunctionType
AX = mybir.AxisListType

P = 128
B, T, D = 16, 256, 256
TT = T // P
DC = D // P
NH, NKV, HD = 16, 8, 128
WINDOW = 128
ATT_SCALE = 0.08838834764831845
EXPERTS, INNER, SHARED = 8, 176, 352
HID0 = EXPERTS * INNER + SHARED
J0 = -(-HID0 // P)
HP = J0 * P
JB = (EXPERTS * INNER) // P
H1, HD1 = 32, 8
HID1 = 1024
J1 = HID1 // P
WS = 64.0
NEG = -1e30

COLS = {}
_at = 0
for _name, _n in (("qkv", DC * NKV * 512), ("o", NH * D), ("g", DC * HP), ("u", DC * HP), ("d", J0 * D),
                  ("r", DC * EXPERTS), ("a1", DC * 3 * D), ("p1", DC * D), ("w1", DC * HID1), ("w3", DC * HID1)):
    COLS[_name] = _at
    _at += _n
NW = _at
COLS["w2"] = NW
NW2 = NW + J1 * D
CHUNK = next(n for n in range(1500, 0, -1) if NW % n == 0 and n % 4 == 0)
NCHUNK = NW // CHUNK

BG, BU = 0, (J0 - JB) * P
BD = 2 * BU
BA = BD + D
BP = BA + 3 * D
NB = BP + D

K_ID, K_M0, K_M1, K_HM, K_IO, K_BS = 0, 128, 512, 896, 900, 908
NC = 912

MID_AT0 = {5: [("lnc", 0, 1)], 13: [("lnc", 1, 0)], 14: [("rt", 0)]}
AFTER_AT0 = {3: [("mc", 1), ("lna", 0, 1)], 4: [("lnb", 0, 1)], 5: [("lnd", 0, 1)],
             11: [("res0", 0), ("lna", 1, 0)], 12: [("lnb", 1, 0)], 13: [("lnd", 1, 0)], 15: [("rt2", 0)],
             16: [("rt3", 0)], 17: [("ct", 0), ("ff0", 0)], 18: [("ff0", 1)], 19: [("res0", 1), ("lna", 1, 1)]}
AFTER_FF0 = {2: [("lnb", 1, 1)], 3: [("lnc", 1, 1), ("lnd", 1, 1)], 6: [("rt", 1)], 7: [("rt2", 1)],
             8: [("rt3", 1)], 10: [("ct", 1)], 15: [("resf", 0, 0), ("lna", 2, 0)], 16: [("lnb", 2, 0)],
             18: [("lnc", 2, 0), ("lnd", 2, 0)], 20: [("q1", 0)], 22: [("k1", 0)], 24: [("v1", 0)],
             25: [("qm", 0, 0), ("qm", 0, 1)], 27: [("at1", 0)], 28: [("at1", 1)],
             29: [("resf", 0, 1), ("lna", 2, 1)]}
AFTER_AT1 = {2: [("lnb", 2, 1)], 3: [("lnc", 2, 1), ("lnd", 2, 1)], 4: [("q1", 1)], 5: [("k1", 1), ("qm", 1, 0)],
             6: [("v1", 1)], 7: [("qm", 1, 1)], 9: [("pvr", 0)], 10: [("at", 0)], 11: [("pj", 0), ("lna", 3, 0)],
             12: [("lnb", 3, 0)], 13: [("lnc", 3, 0), ("lnd", 3, 0)], 16: [("ff1", 0)], 17: [("pvr", 1)]}
AFTER_FF1 = {1: [("at", 1)], 2: [("pj", 1), ("lna", 3, 1)], 3: [("lnb", 3, 1)], 4: [("lnc", 3, 1), ("lnd", 3, 1)],
             6: [("mc", 0), ("lna", 0, 0)], 7: [("lnb", 0, 0)], 9: [("resf", 1, 0)],
             10: [("lnc", 0, 0), ("lnd", 0, 0)], 17: [("resf", 1, 1)]}
MISC_KINDS = ("lnc", "rt", "ct", "q1", "k1", "v1", "at", "pj")
ORDER = []
for _u in range(20):
    ORDER += [("at0", _u)] + AFTER_AT0.get(_u, [])
for _v in range(2, 2 * J0 + 2):
    ORDER += [("ff0", _v)] + AFTER_FF0.get(_v, [])
for _w in range(2, 18):
    ORDER += [("at1", _w)] + AFTER_AT1.get(_w, [])
for _v in range(1, 2 * J1 + 2):
    ORDER += [("ff1", _v)] + AFTER_FF1.get(_v, [])
    if _v == 2 * J1:
        ORDER += [("first",)]

MISC, MISC_HI = {}, {}
_hi = 0
for _item in ORDER:
    _uses = []
    if _item[0] == "at0":
        _uses = [("t1", _item[1] - 1, _t) for _t in range(TT) if 1 <= _item[1] <= 16]
        _uses += [_m for _m in MID_AT0.get(_item[1], []) if _m[0] in MISC_KINDS]
    elif _item[0] in MISC_KINDS:
        _uses = [_item]
    for _k in _uses:
        MISC[_k] = len(MISC) + 1
        if _k[0] in ("t1", "q1", "k1", "v1", "at"):
            _hi += 1
            MISC_HI[_k] = _hi
NPAIR = B // 2
U0 = 2 * NKV
W1G = 16
CHAIN = 1100


class Signal:

    def __init__(self, handle, per, unit=1):
        self.handle, self.per, self.unit = handle, per, unit

    def count(self, i, n):
        return i * (self.per * self.unit) + (self.per + n) * self.unit


def build(nc, x_in, wall, w2t, brow, cf, hadm, rope, nsc, sel_in, ct_in, wmod, out, gates_dram):
    ctx = ExitStack()
    with ctx:
        def sb(name, shape, dt):
            return ctx.enter_context(nc.sbuf_tensor(name, shape, dt))

        def sem(name):
            return ctx.enter_context(nc.semaphore(name))

        signals = []

        def signal(name, per, unit=1):
            signals.append(Signal(sem(name), per, unit))
            return signals[-1]

        whi = sb("whi", [P, NW2], F16)
        wlo = sb("wlo", [P, NW2], F16)
        brows = sb("brows", [2, NB], F16)
        sel = sb("sel", [17, HP], F16)
        ones = sb("ones", [2, T], F16)
        con = sb("con", [P, NC], F32)
        ropec = sb("ropec", [P, TT, 3, HD], F32)
        ropes = sb("ropes", [P, TT, 3, HD], F32)
        modt = sb("modt", [P, B + 1, 16], F32)
        mcol = sb("mcol", [P, 2, 16], F32)
        xin = sb("xin", [P, 2, TT, D], F32)
        xs = sb("xs", [P, 2, TT, D], F32)
        gate = sb("gate", [P, 2, 2, D], F32)
        hth = sb("hth", [P, 2, DC, T], F16)
        htl = sb("htl", [P, 2, DC, T], F16)
        hf = sb("hf", [P, 2 * T], F32)
        xn = sb("xn", [P, TT, D], F32)
        vh0 = sb("vh0", [P, 4, TT, HD], F16)
        vl0 = sb("vl0", [P, 4, TT, HD], F16)
        k1h = sb("k1h", [P, 2, DC, T], F16)
        k1l = sb("k1l", [P, 2, DC, T], F16)
        v1h = sb("v1h", [P, 2, TT, D], F16)
        v1l = sb("v1l", [P, 2, TT, D], F16)
        q1h = sb("q1h", [P, DC * T], F16)
        q1l = sb("q1l", [P, DC * T], F16)
        qmh = sb("qmh", [P, 4, DC * T], F16)
        qml = sb("qml", [P, 4, DC * T], F16)
        ctt = sb("ctt", [17, 2, T], F16)
        small = sb("small", [P, 512], F32)
        NARENA = 24 * 256
        arena = sb("arena", [P, NARENA], F32)
        farena = sb("farena", [P, 2048], F32)

        spot = [0]

        def small_at(n):
            spot[0] += n
            assert spot[0] <= 512
            return small[:, spot[0] - n:spot[0]]

        st6 = small_at(TT * 6).rearrange("p (t k) -> p t k", t=TT)
        mv = small_at(TT * 2).rearrange("p (t k) -> p t k", t=TT)
        lv = small_at(TT)
        lr = small_at(2 * TT)
        half = small_at(8)
        ss = small_at(6)
        ms = small_at(6)
        rs0 = small_at(24).rearrange("p (k n) -> p k n", k=4)
        mx0 = small_at(8).rearrange("p (k n) -> p k n", k=2)
        nb0 = small_at(8).rearrange("p (k n) -> p k n", k=2)
        sm0 = small_at(8).rearrange("p (k n) -> p k n", k=2)
        ri0 = small_at(8).rearrange("p (k n) -> p k n", k=2)
        rt_l = small_at(16).rearrange("p (t e) -> p t e", t=TT)
        rt_e = small_at(16).rearrange("p (t e) -> p t e", t=TT)
        rt_a = small_at(16).rearrange("p (t e) -> p t e", t=TT)
        rt_k = small_at(16).rearrange("p (t e) -> p t e", t=TT)
        rt_k2 = small_at(16).rearrange("p (t e) -> p t e", t=TT)
        rt_m = small_at(8).rearrange("p (k t) -> p k t", t=TT)
        c17 = small_at(34).rearrange("p (t e) -> p t e", t=TT)
        mx1 = small_at(16).rearrange("p (k n) -> p k n", k=2)
        nb1 = small_at(16).rearrange("p (k n) -> p k n", k=2)
        sum1 = small_at(2 * 64).rearrange("p (s t h) -> p s t h", s=2, t=TT)
        ri1 = small_at(64).rearrange("p (t h) -> p t h", t=TT)
        ch16 = small_at(8).bitcast(F16).rearrange("p (t e) -> p t e", t=TT)

        def carve(pool_, spots, at=0):
            found = []
            for words, dt in spots:
                a = pool_[:, at:at + words]
                found.append(a if dt == F32 else a.bitcast(F16))
                at += words
            assert at <= pool_.shape[1], at
            return found

        ra, rb, qkh, qkl, smx, pth, ptl, ench, encl = carve(arena,
            [(768, F32), (768, F32), (768, F16), (768, F16), (2 * 768, F32), (384, F16), (384, F16),
             (256, F16), (256, F16)])
        ra = ra.rearrange("p (t k h) -> p t k h", t=TT, k=3)
        rb = rb.rearrange("p (t k h) -> p t k h", t=TT, k=3)
        qkh = qkh.rearrange("p (y k n) -> p y k n", y=2, k=3)
        qkl = qkl.rearrange("p (y k n) -> p y k n", y=2, k=3)
        smx = smx.rearrange("p (y k n) -> p y k n", y=2, k=2)
        pth = pth.rearrange("p (k n) -> p k n", k=6)
        ptl = ptl.rearrange("p (k n) -> p k n", k=6)
        ench = ench.rearrange("p (t k n) -> p t k n", t=TT, k=2)
        encl = encl.rearrange("p (t k n) -> p t k n", t=TT, k=2)
        th, fa, fh, fl = carve(farena, [(2 * T, F32), (3 * T, F32), (3 * T // 2, F16), (3 * T // 2, F16)])
        th = th.rearrange("p (k n) -> p k n", k=2)
        fa = fa.rearrange("p (k n) -> p k n", k=3)
        fh = fh.rearrange("p (k n) -> p k n", k=3)
        fl = fl.rearrange("p (k n) -> p k n", k=3)
        s1, p1h, p1l = carve(arena, [(2 * 4 * 384, F32), (2 * 768, F16), (2 * 768, F16)])
        s1 = s1.rearrange("p (b j n) -> p b j n", b=2, j=4)
        p1h = p1h.rearrange("p (y k j n) -> p y k j n", y=2, k=3, j=4)
        p1l = p1l.rearrange("p (y k j n) -> p y k j n", y=2, k=3, j=4)

        ident = con[:, K_ID:K_ID + 128]
        mask0 = con[:, K_M0:K_M0 + 384]
        bias1 = con[:, K_M1:K_M1 + 384]
        iota = con[:, K_IO:K_IO + 8]

        bank = [ctx.enter_context(nc.psum_tensor(f"bank{k}", [P, 512], F32)) for k in range(8)]
        misc = bank[2]

        def w_of(name, at, n):
            a = COLS[name] + at
            return whi[:, a:a + n], wlo[:, a:a + n]

        wm = whi[:, 0:2 * 2 * DC * 1536].bitcast(F32).rearrange("p (l c n) -> p l c n", l=2, c=DC)
        ha = wlo[:, 0:4096].bitcast(F32)
        hb = wlo[:, 4096:8192].bitcast(F32)
        had = wlo[:, 8192:8448].bitcast(F32)
        rcos = wlo[:, 8448:8960].bitcast(F32).rearrange("p (t n) -> p t n", t=TT)
        rsin = wlo[:, 8960:9472].bitcast(F32).rearrange("p (t n) -> p t n", t=TT)
        nsn = wlo[:, 9472:10240].bitcast(F32).rearrange("p (k n) -> p k n", k=3)
        nsw = wlo[:, 10240:11008].bitcast(F32).rearrange("p (k n) -> p k n", k=3)
        braw = wlo[0:2, 11008:11008 + 2 * NB].bitcast(F32)
        sc = wlo[:, 16384:16512].bitcast(F32).rearrange("p (l c n) -> p l c n", l=2, c=DC)
        st = wlo[:, 16512:16640].bitcast(F32).rearrange("p (l c n) -> p l c n", l=2, c=DC)
        gsb = wlo[0:B, 16640:16640 + 2 * 4 * D].bitcast(F32)
        gtmp = wlo[0:B, 18688:18688 + 2 * 4 * D].bitcast(F32)
        bhi = wlo[0:2, 20736:20736 + NB]
        blo = wlo[0:2, 20736 + NB:20736 + 2 * NB]

        ld_con = sem("ld_con")
        ld_c = sem("ld_c")
        ld_wm = [sem(f"ld_wm{l}") for l in range(2)]
        ld_w2 = sem("ld_w2")
        ld_rope = sem("ld_rope")
        ld_b = sem("ld_b")
        ld_sel = sem("ld_sel")
        set_tanh = sem("set_tanh")
        set_v = sem("set_v")
        set_mm = sem("set_mm")
        set_had = sem("set_had")
        set_hi = sem("set_hi")
        st_gates = sem("st_gates")
        gates_ready = sem("gates_ready")
        had_step = sem("had_step")

        RING = 5
        stage = [arena[:, k * CHUNK:(k + 1) * CHUNK] for k in range(4)] + [farena[:, 0:CHUNK]]
        assert 4 * CHUNK <= NARENA and CHUNK <= 2048
        ld_stage = [sem(f"ld_stage{k}") for k in range(RING)]

        def load_chunk(sp, n):
            sp.dma_start(stage[n % RING], wall[:, n * CHUNK:(n + 1) * CHUNK]).then_inc(ld_stage[n % RING], 16)

        with nc.Block() as block:
            @block.sync
            def _(sp):
                sp.dma_start(sc[:, :, :, :], ct_in).then_inc(ld_c, 16)
                sp.dma_start(ha, w2t).then_inc(ld_w2, 16)
                sp.dma_start(had, hadm).then_inc(ld_w2, 16)
                for l in range(2):
                    sp.dma_start(wm[:, l], wmod[:, l]).then_inc(ld_wm[l], 16)
                sp.dma_start(con[:, :], cf).then_inc(ld_con, 16)
                sp.dma_start(rcos, rope[:, 0]).then_inc(ld_rope, 16)
                sp.dma_start(rsin, rope[:, 1]).then_inc(ld_rope, 16)
                sp.dma_start(nsn, nsc[0].partition_broadcast(P)).then_inc(ld_rope, 16)
                sp.dma_start(nsw, nsc[1].partition_broadcast(P)).then_inc(ld_rope, 16)
                sp.dma_start(braw, brow.partition_broadcast(2)).then_inc(ld_b, 16)
                sp.dma_start(sel[:, :], sel_in).then_inc(ld_sel, 16)
                for n in range(RING):
                    load_chunk(sp, n)
                sp.wait_ge(gates_ready, 1)
                sp.dma_start(gates_dram, gsb).then_inc(st_gates, 16)
                sp.wait_ge(st_gates, 16)
                sp.wait_ge(ld_con, 16)
                sp.wait_ge(ld_sel, 16)

            @block.scalar
            def _(act):
                act.wait_ge(ld_c, 16)
                nc.scalar.activation(st[:, :, :, :], sc[:, :, :, :], ACT.Tanh, scale=0.5).then_inc(set_tanh, 1)
                for q in range(4):
                    act.wait_ge(set_had, q + 1)
                    nc.scalar.activation(whi[:, NW + q * 512:NW + (q + 1) * 512], bank[4 + q][:, :], ACT.Copy,
                                         scale=WS / 32.0).then_inc(set_hi, 1)

            @block.tensor
            def _(pe):
                pe.wait_ge(had_step, 3)
                pe.wait_ge(ld_w2, 32)
                for q in range(4):
                    nc.tensor.matmul(bank[4 + q][:, :], had, hb[:, q * 512:(q + 1) * 512],
                                     start=True, stop=True).then_inc(set_had, 1)
                pe.wait_ge(set_v, 2)
                for l in range(2):
                    pe.wait_ge(ld_wm[l], 16)
                    for k, part in enumerate((1, 0, 4, 3)):
                        for c2 in range(DC):
                            n = l * 8 + k * 2 + c2
                            for c in range(DC):
                                last = nc.tensor.matmul(bank[0][:, n * B:(n + 1) * B],
                                                        wm[:, l, c, part * D + c2 * P:part * D + (c2 + 1) * P],
                                                        st[:, l, c, :], start=(c == 0), stop=(c == DC - 1))
                last.then_inc(set_mm, 1)
                for l in range(2):
                    for k, part in enumerate((2, 5)):
                        for c in range(DC):
                            last = nc.tensor.matmul(bank[1 + l][0:B, k * D:(k + 1) * D], st[:, l, c, :],
                                                    wm[:, l, c, part * D:(part + 1) * D],
                                                    start=(c == 0), stop=(c == DC - 1))
                last.then_inc(set_mm, 1)

            @block.gpsimd
            def _(pool):
                pool.memset(half, -0.5)
                pool.memset(modt[:, B, :], 0.0)
                pool.memset(ones[:, :], 1.0)
                pool.memset(c17[:, :, 8:9], 1.0)

            @block.vector
            def _(dve):
                n = [0]

                def link(ins):
                    n[0] += 1
                    ins.then_inc(set_v, 1)
                    dve.wait_ge(set_v, n[0])

                dve.wait_ge(ld_w2, 32)
                bufs = [(ha, hb), (hb, ha), (ha, hb)]
                for k, (src, dst) in enumerate(bufs):
                    v = [z.rearrange("p (o two i) -> p o two i", two=2, i=D << k) for z in (src, dst)]
                    ins = nc.vector.tensor_tensor(v[1][:, :, 0, :], v[0][:, :, 0, :], v[0][:, :, 1, :], ALU.add)
                    ins2 = nc.vector.tensor_tensor(v[1][:, :, 1, :], v[0][:, :, 0, :], v[0][:, :, 1, :], ALU.subtract)
                    ins2.then_inc(had_step, 1)
                    if k < 2:
                        dve.wait_ge(had_step, k + 1)
                dve.wait_ge(set_tanh, 1)
                link(nc.vector.tensor_scalar(st[:, :, :, :], st[:, :, :, :], 1.0, 0.5, ALU.add, ALU.mult))
                link(nc.vector.tensor_tensor(st[:, :, :, :], st[:, :, :, :], sc[:, :, :, :], ALU.mult))
                dve.wait_ge(ld_rope, 64)
                for z in (nsn, nsw):
                    link(nc.vector.tensor_scalar(z[:, 0:2, :], z[:, 0:2, :], ATT_SCALE, None, ALU.mult))
                for k in range(3):
                    for t in range(TT):
                        nc.vector.tensor_tensor(ropec[:, t, k, :], rcos[:, t, :], nsn[:, k, :], ALU.mult)
                        nc.vector.tensor_tensor(ropes[:, t, k, :], rsin[:, t, :], nsw[:, k, :], ALU.mult)
                dve.wait_ge(ld_b, 16)
                dve.wait_ge(ld_con, 16)
                link(nc.vector.tensor_scalar(bhi, braw, WS, None, ALU.mult))
                link(nc.vector.scalar_tensor_tensor(out=blo, in0=braw, scalar=WS, in1=bhi,
                                                    op0=ALU.mult, op1=ALU.subtract))
                link(nc.vector.tensor_scalar(bhi, bhi, con[0:2, K_BS:K_BS + 1], None, ALU.mult))
                link(nc.vector.scalar_tensor_tensor(out=brows[:, :], in0=blo, scalar=con[0:2, K_BS + 1:K_BS + 2],
                                                    in1=bhi, op0=ALU.mult, op1=ALU.add))
                for q in range(4):
                    dve.wait_ge(set_hi, q + 1)
                    a = slice(NW + q * 512, NW + (q + 1) * 512)
                    nc.vector.scalar_tensor_tensor(out=wlo[:, a], in0=bank[4 + q][:, :], scalar=WS / 32.0,
                                                   in1=whi[:, a], op0=ALU.mult, op1=ALU.subtract)
                dve.wait_ge(set_mm, 1)
                src = bank[0][:, 0:16 * B].rearrange("p (n b) -> p b n", b=B)
                link(nc.vector.tensor_copy(modt[:, 0:B, :], src))
                for l in range(2):
                    for k in (0, 2):
                        a = l * 8 + k * 2
                        link(nc.vector.tensor_scalar(modt[:, 0:B, a:a + 2], modt[:, 0:B, a:a + 2], 1.0, None, ALU.add))
                dve.wait_ge(set_mm, 2)
                for l in range(2):
                    g = bank[1 + l][0:B, :]
                    a, b = gsb[:, l * 512:(l + 1) * 512], gtmp[:, l * 512:(l + 1) * 512]
                    link(nc.vector.tensor_scalar(a, g, 0.0, 2.0 / WS, ALU.is_ge, ALU.mult))
                    link(nc.vector.tensor_scalar(a, a, -1.0 / WS, None, ALU.add))
                    link(nc.vector.tensor_scalar(b, g, -1.0, None, ALU.mult))
                    link(nc.vector.tensor_tensor(b, b, g, ALU.max))
                nc.vector.scalar_tensor_tensor(out=gsb, in0=gtmp, scalar=0.25, in1=gsb,
                                               op0=ALU.max, op1=ALU.mult).then_inc(gates_ready, 1)

        ld_first = sem("ld_first")
        first_v = sem("first_v")
        first_rstd = sem("first_rstd")
        first_mm = sem("first_mm")
        first_hi = sem("first_hi")
        w_hi = sem("w_hi")
        w_lo = sem("w_lo")

        ld_x = [signal(f"ld_x{s}", 1, 16) for s in range(2)]
        ld_g = [signal(f"ld_g{s}", 2, 16) for s in range(2)]
        st_x = [signal(f"st_x{s}", 1, 16) for s in range(2)]
        ln_stats = signal("ln_stats", 8)
        ln_rstd = signal("ln_rstd", 8)
        ln_norm = signal("ln_norm", 8)
        h_hi = signal("h_hi", 8)
        h_lo = signal("h_lo", 8)
        misc_mm = signal("misc_mm", len(MISC))
        misc_hi = signal("misc_hi", len(MISC_HI))
        misc_free = signal("misc_free", len(MISC))
        qkv_mm = signal("qkv_mm", 2 * U0)
        qkv_act = signal("qkv_act", 2 * U0)
        rope_mul = signal("rope_mul", 2 * U0)
        rope_sum = signal("rope_sum", 2 * U0)
        qk_rstd = signal("qk_rstd", 2 * U0)
        k_norm = signal("k_norm", 2 * U0)
        s_mm = signal("s_mm", 2 * U0)
        s_max = signal("s_max", 4 * U0)
        s_shift = signal("s_shift", U0)
        s_exp = signal("s_exp", 4 * U0)
        p_norm = signal("p_norm", 4 * U0)
        pt_mm = signal("pt_mm", 2 * U0)
        pt_hi = signal("pt_hi", 2 * U0)
        pt_lo = signal("pt_lo", 2 * U0)
        enc_mm = signal("enc_mm", U0)
        enc_hi = signal("enc_hi", U0)
        enc_lo = signal("enc_lo", U0)
        o_mm = signal("o_mm", 8)
        o_read = signal("o_read", 8)
        NGU = 2 * J0 + 2 * J1
        gu_mm = signal("gu_mm", NGU)
        gu_tanh = signal("gu_tanh", NGU)
        gu_read = signal("gu_read", NGU)
        ce_mm = signal("ce_mm", 2 * J0)
        ce_read = signal("ce_read", 2 * J0)
        hid_hi = signal("hid_hi", NGU)
        hid_lo = signal("hid_lo", NGU)
        rt_exp = signal("rt_exp", 2)
        rt_sub = signal("rt_sub", 2)
        c_ready = signal("c_ready", 2)
        qm_ready = signal("qm_ready", 4)
        a_mm = signal("a_mm", 3 * W1G)
        a_max = signal("a_max", 8 * W1G)
        a_shift = signal("a_shift", 2 * W1G)
        a_exp = signal("a_exp", 8 * W1G)
        at_mm = signal("at_mm", 3 * W1G)
        at_hi = signal("at_hi", 3 * W1G)
        at_lo = signal("at_lo", 3 * W1G)
        v_chain = signal("v_chain", CHAIN)
        g_chain = signal("g_chain", 2 * U0 + 8)

        passed_pool = sem("passed_pool")
        passed_dve = sem("passed_dve")

        with nc.Block() as block:
            @block.sync
            def _(sp):
                for s in range(2):
                    sp.dma_start(xin[:, s], x_in[s].rearrange("(t p) d -> p t d", p=P)).then_inc(ld_first, 16)
                for n in range(RING, NCHUNK):
                    sp.wait_ge(w_lo, n - RING + 1)
                    load_chunk(sp, n)
                sp.wait_ge(ld_first, 32)
                for z in signals:
                    sp.sem_inc(z.handle, z.per * z.unit)

            @block.tensor
            def _(pe):
                pe.wait_ge(first_v, 4)
                for c in range(DC):
                    for t in range(TT):
                        last = nc.tensor.transpose(misc[:, c * T + t * P:c * T + (t + 1) * P],
                                                   xn[:, t, c * P:(c + 1) * P], ident)
                last.then_inc(first_mm, 1)

            @block.gpsimd
            def _(pool):
                pool.wait_ge(first_v, 3)
                nc.gpsimd.tensor_tensor(lr[:, 0:TT], lv, half[:, 0:TT], ALU.pow).then_inc(first_rstd, 1)

            @block.scalar
            def _(act):
                for n in range(NCHUNK):
                    act.wait_ge(ld_stage[n % RING], 16 * (n // RING + 1))
                    nc.scalar.activation(whi[:, n * CHUNK:(n + 1) * CHUNK], stage[n % RING], ACT.Copy,
                                         scale=WS).then_inc(w_hi, 1)
                    if n == 8:
                        act.wait_ge(first_v, 5)
                        nc.scalar.activation(hth[:, 0].rearrange("p c n -> p (c n)"), hf[:, :],
                                             ACT.Copy).then_inc(first_hi, 1)

            @block.vector
            def _(dve):
                for n in range(NCHUNK):
                    dve.wait_ge(w_hi, n + 1)
                    nc.vector.scalar_tensor_tensor(out=wlo[:, n * CHUNK:(n + 1) * CHUNK], in0=stage[n % RING],
                                                   scalar=WS, in1=whi[:, n * CHUNK:(n + 1) * CHUNK],
                                                   op0=ALU.mult, op1=ALU.subtract).then_inc(w_lo, 1)
                    if n == 1:
                        dve.wait_ge(ld_first, 32)
                        nc.vector.tensor_copy(mcol[:, 0, :], modt[:, 0, :])
                        for t in range(TT):
                            ins = nc.vector.bn_stats(st6[:, t, :], xin[:, 0, t, :])
                        ins.then_inc(first_v, 1)
                        dve.wait_ge(first_v, 1)
                        for t in range(TT):
                            ins = nc.vector.bn_aggr(mv[:, t, :], st6[:, t, :])
                        ins.then_inc(first_v, 1)
                        dve.wait_ge(first_v, 2)
                        nc.vector.tensor_scalar(lv, mv[:, :, 1], 1e-5, None, ALU.add).then_inc(first_v, 1)
                    if n == 3:
                        dve.wait_ge(first_rstd, 1)
                        for t in range(TT):
                            ins = nc.vector.tensor_scalar(xn[:, t, :], xin[:, 0, t, :], mv[:, t, 0:1],
                                                          lr[:, t:t + 1], ALU.subtract, ALU.mult)
                        ins.then_inc(first_v, 1)
                    if n == 5:
                        dve.wait_ge(first_mm, 1)
                        for c in range(DC):
                            ins = nc.vector.tensor_scalar(hf[:, c * T:(c + 1) * T], misc[:, c * T:(c + 1) * T],
                                                          mcol[:, 0, c:c + 1], mcol[:, 0, c + 2:c + 3],
                                                          ALU.mult, ALU.add)
                        ins.then_inc(first_v, 1)
                    if n == 10:
                        dve.wait_ge(first_hi, 1)
                        nc.vector.tensor_tensor(htl[:, 0].rearrange("p c n -> p (c n)"), hf[:, :],
                                                hth[:, 0].rearrange("p c n -> p (c n)"), ALU.subtract)

        def n_ln(k, s, ahead=False):
            return 8 if ahead else 2 * k + s

        def n_o(stage_, s):
            return 2 * stage_ + s + 1

        def n_gu(f, v):
            return (2 * J0 if f else 0) + v + 1

        def ff_dims(f):
            return (J1 if f else J0), ("w1" if f else "g"), ("w3" if f else "u"), ("w2" if f else "d")

        o_bank = {(1, 0): 6, (1, 1): 7, (3, 0): 6, (3, 1): 7}

        with nc.Block() as block:
            @block.sync
            def _(sp):
                with sp.Fori(0, NPAIR) as i:
                    def load_gates(l, s):
                        sp.wait_ge(o_read.handle, o_read.count(i, n_o(1, s) if l else n_o(3, s) - 8))
                        sp.dma_start(gate[:, s], gates_dram[2 * i + s, l * 512:(l + 1) * 512]
                                     .rearrange("(k n) -> k n", k=2).partition_broadcast(P)).then_inc(ld_g[s].handle, 16)

                    for s in range(2):
                        load_gates(0, s)
                    for s in range(2):
                        sp.wait_ge(o_read.handle, o_read.count(i, n_o(0, s)))
                        sp.dma_start(xin[:, s], x_in[2 * i + 2 + s].rearrange("(t p) d -> p t d", p=P))\
                          .then_inc(ld_x[s].handle, 16)
                    for s in range(2):
                        load_gates(1, s)
                    for s in range(2):
                        sp.wait_ge(o_read.handle, o_read.count(i, n_o(3, s)))
                        sp.dma_start(out[2 * i + s].rearrange("(t p) d -> p t d", p=P), xs[:, s])\
                          .then_inc(st_x[s].handle, 16)
                for s in range(2):
                    sp.wait_ge(st_x[s].handle, 16 * (NPAIR + 1))

            @block.tensor
            def _(pe):
                def mm3(dst, lhs, rhs, start, stop, skip=False):
                    nc.tensor.matmul(dst, lhs[0], rhs[0], start=start, stop=False, skip_group_check=skip)
                    nc.tensor.matmul(dst, lhs[0], rhs[1], start=False, stop=False, skip_group_check=skip)
                    return nc.tensor.matmul(dst, lhs[1], rhs[0], start=False, stop=stop, skip_group_check=skip)

                i = 0
                def wait(z, n):
                    pe.wait_ge(z.handle, z.count(i, n))

                def misc_begin(key):
                    wait(misc_free, MISC[key] - 1)

                def transposes4(src):
                    for c in range(DC):
                        for t in range(TT):
                            last = nc.tensor.transpose(misc[:, c * T + t * P:c * T + (t + 1) * P],
                                                       src[:, t, c * P:(c + 1) * P], ident)
                    last.then_inc(misc_mm.handle, 1)

                def h_of(s, c, t=None):
                    if t is None:
                        return hth[:, s, c, :], htl[:, s, c, :]
                    return hth[:, s, c, t * P:(t + 1) * P], htl[:, s, c, t * P:(t + 1) * P]

                def qk_turn(e, t):
                    misc_begin(("t1", e, t))
                    wait(k_norm, 2 * e + t + 1)
                    for k in range(3):
                        last = nc.tensor.transpose(misc[:, k * P:(k + 1) * P], ra[:, t, k, :], ident)
                    last.then_inc(misc_mm.handle, 1)

                def qkv(e, t):
                    s, g = divmod(e % U0, NKV)
                    if g == 0 and t == 0:
                        wait(h_lo, n_ln(0, s, e == U0))
                    if e % U0 == 0 and t == 0:
                        wait(gu_read, NGU if e else 0)
                    wait(rope_mul, 2 * (e - 1) + t + 1)
                    for c in range(DC):
                        last = mm3(bank[t][:, :], h_of(s, c, t), w_of("qkv", c * 4096 + g * 512, 512),
                                   c == 0, c == DC - 1)
                    last.then_inc(qkv_mm.handle, 1)

                def p_turn(e, b):
                    y = e % 2
                    wait(p_norm, 4 * e + 2 * (b + 1))
                    wait(pt_lo, 2 * e + b)
                    for kt in range(b + 1):
                        for k in range(2):
                            a = (b + kt) * P
                            last = nc.tensor.transpose(bank[5][:, (2 * kt + k) * P:(2 * kt + k + 1) * P],
                                                       smx[:, y, k, a:a + P], ident)
                    last.then_inc(pt_mm.handle, 1)

                def scores(e):
                    wait(misc_free, MISC[("t1", e, 1)])
                    wait(s_max, 4 * e)
                    y = e % 2
                    for k in range(2):
                        last = mm3(bank[3][:, k * P:(k + 1) * P], (qkh[:, y, k, 0:P], qkl[:, y, k, 0:P]),
                                   (qkh[:, y, 2, 0:P], qkl[:, y, 2, 0:P]), True, True)
                    last.then_inc(s_mm.handle, 1)
                    for k in range(2):
                        last = mm3(bank[4][:, k * T:(k + 1) * T], (qkh[:, y, k, P:T], qkl[:, y, k, P:T]),
                                   (qkh[:, y, 2, :], qkl[:, y, 2, :]), True, True)
                    last.then_inc(s_mm.handle, 1)

                def project(e):
                    s, g = divmod(e, NKV)
                    wait(enc_lo, e + 1)
                    if g == 0:
                        wait(o_read, n_o(3, 1) - 8 if s == 0 else n_o(0, 0))
                    for k in range(2):
                        for t in range(TT):
                            first = g == 0 and k == 0 and t == 0
                            last = mm3(bank[7][:, t * D:(t + 1) * D], (ench[:, t, k, :], encl[:, t, k, :]),
                                       w_of("o", (2 * g + k) * D, D), first, g == NKV - 1 and k == 1, skip=True)
                    if g == NKV - 1:
                        last.then_inc(o_mm.handle, 1)

                def encode(e):
                    wait(pt_lo, 2 * (e + 1))
                    if e == 0:
                        wait(o_read, n_o(3, 0) - 8)
                    v = e % 4
                    mm3(bank[6][:, 0:T], (vh0[:, v, 0, :], vl0[:, v, 0, :]),
                        (pth[:, 0:2, :], ptl[:, 0:2, :]), True, True)
                    mm3(bank[6][:, T:2 * T], (vh0[:, v, 0, :], vl0[:, v, 0, :]),
                        (pth[:, 2:4, :], ptl[:, 2:4, :]), True, False)
                    last = mm3(bank[6][:, T:2 * T], (vh0[:, v, 1, :], vl0[:, v, 1, :]),
                               (pth[:, 4:6, :], ptl[:, 4:6, :]), False, True)
                    last.then_inc(enc_mm.handle, 1)

                def at0(u):
                    if 0 <= u - 3 < U0:
                        p_turn(u - 3, 0)
                    if 0 <= u - 2 < U0:
                        scores(u - 2)
                    if 0 <= u - 1 < U0:
                        qk_turn(u - 1, 0)
                    if 0 < u < U0:
                        qkv(u, 0)
                    if 0 <= u - 1 < U0:
                        qk_turn(u - 1, 1)
                    if 0 <= u - 3 < U0:
                        p_turn(u - 3, 1)
                    if 0 < u < U0:
                        qkv(u, 1)
                    if 0 <= u - 4 < U0:
                        project(u - 4)
                    for item in MID_AT0.get(u, []):
                        stage(item)
                    if 0 <= u - 3 < U0:
                        encode(u - 3)

                def ff(f, v):
                    J, wg, wu, wd = ff_dims(f)
                    stage_ = 3 if f else 1
                    if v < 2 * J:
                        s, j = divmod(v, J)
                        n = n_gu(f, v)
                        if j == 0:
                            wait(h_lo, n_ln(3 if f else 1, s))
                        if not f and v < 2:
                            wait(rope_mul, 2 * U0)
                        elif f and v < 2:
                            wait(a_max, 8 * W1G)
                        else:
                            wait(gu_read, n - 2)
                        bk = bank[(n - 1) % 2]
                        bias = not f and j >= JB
                        for k, name in enumerate((wg, wu)):
                            for c in range(DC):
                                last = mm3(bk[:, k * T:(k + 1) * T],
                                           w_of(name, c * J * P + j * P, P), h_of(s, c), c == 0,
                                           c == DC - 1 and not bias)
                            if bias:
                                a = (BG, BU)[k] + (j - JB) * P
                                last = nc.tensor.matmul(bk[:, k * T:(k + 1) * T], brows[:, a:a + P], ones[:, :],
                                                        start=False, stop=True)
                        last.then_inc(gu_mm.handle, 1)
                        if not f:
                            if j == 0:
                                wait(misc_free, MISC[("ct", s)])
                            if v < 2:
                                wait(s_max, 4 * U0)
                            else:
                                wait(ce_read, v - 1)
                            nc.tensor.matmul(bank[3 + v % 2][:, 0:T], sel[:, j * P:(j + 1) * P], ctt[:, s, :],
                                             start=True, stop=True).then_inc(ce_mm.handle, 1)
                    if v >= 2:
                        s, j = divmod(v - 2, J)
                        n = n_gu(f, v - 2)
                        wait(hid_lo, n)
                        ob = bank[o_bank[(stage_, s)]]
                        if j == 0:
                            if s == 0:
                                wait(*((at_lo, 3 * W1G) if f else (enc_lo, U0)))
                            else:
                                wait(o_read, n_o(stage_ - 1, 1))
                        z = (n - 1) % 3
                        for t in range(TT):
                            last = mm3(ob[:, t * D:(t + 1) * D],
                                       (fh[:, z, t * P:(t + 1) * P], fl[:, z, t * P:(t + 1) * P]),
                                       w_of(wd, j * D, D), j == 0 and t == 0, f == 1 and j == J - 1, skip=True)
                            if not f and j == J - 1:
                                last = nc.tensor.matmul(ob[:, t * D:(t + 1) * D], ones[:, 0:P], brows[:, BD:BD + D],
                                                        start=False, stop=True, skip_group_check=True)
                        if j == J - 1:
                            last.then_inc(o_mm.handle, 1)

                def scores1(w, t):
                    s, gr = divmod(w, 8)
                    c, g = divmod(gr, 4)
                    if gr % 4 == 0:
                        wait(qm_ready, 2 * s + c + 1)
                        wait(misc_free, MISC[("k1", s)])
                    if w == 0:
                        wait(gu_read, 2 * J0)
                        wait(ce_read, 2 * J0)
                    rows = slice(32 * g, 32 * g + 32)
                    if t == 0:
                        wait(a_max, 8 * w - 4)
                        for j in range(4):
                            q = slice(c * T, c * T + P)
                            last = mm3(bank[0][:, j * P:(j + 1) * P], (qmh[rows, j, q], qml[rows, j, q]),
                                       (k1h[rows, s, c, 0:P], k1l[rows, s, c, 0:P]), True, True)
                        last.then_inc(a_mm.handle, 1)
                        return
                    wait(a_max, 8 * w)
                    for j in range(4):
                        q = slice(c * T + P, (c + 1) * T)
                        last = mm3(bank[(1, 3)[j // 2]][:, j % 2 * T:(j % 2 + 1) * T],
                                   (qmh[rows, j, q], qml[rows, j, q]),
                                   (k1h[rows, s, c, :], k1l[rows, s, c, :]), True, True)
                        if j % 2:
                            last.then_inc(a_mm.handle, 1)

                def p_turn1(w, b):
                    y = w % 2
                    wait(a_exp, 8 * w + (4 if b == 0 else 8))
                    wait(at_lo, 3 * (w - 1) + b + 1)
                    if w == 0 and b == 2:
                        wait(o_read, n_o(1, 0))
                    for j in range(4):
                        last = nc.tensor.transpose(bank[4 + b][:, j * P:(j + 1) * P],
                                                   s1[:, y, j, b * P:(b + 1) * P], ident)
                    last.then_inc(at_mm.handle, 1)

                def attend1(w):
                    s, gr = divmod(w, 8)
                    y = w % 2
                    wait(at_lo, 3 * (w + 1))
                    if gr == 0:
                        wait(misc_free, MISC[("v1", s)])
                        wait(o_read, n_o(1, 1) if s == 0 else n_o(2, 0))
                    for j in range(4):
                        d = (4 * gr + j) * HD1
                        for t in range(TT):
                            for kt in range(t + 1):
                                b = t + kt
                                last = mm3(bank[7][:, t * D + d:t * D + d + HD1],
                                           (p1h[:, y, b, j, :], p1l[:, y, b, j, :]),
                                           (v1h[:, s, kt, d:d + HD1], v1l[:, s, kt, d:d + HD1]),
                                           gr == 0 and j == 0 and t == 0, kt == t, skip=True)
                    if gr == 7:
                        last.then_inc(o_mm.handle, 1)

                def at1(w):
                    if w < W1G:
                        scores1(w, 0)
                    if w < W1G:
                        scores1(w, 1)
                    if 0 <= w - 1 < W1G:
                        p_turn1(w - 1, 0)
                    if 0 <= w - 1 < W1G:
                        p_turn1(w - 1, 1)
                    if 0 <= w - 1 < W1G:
                        p_turn1(w - 1, 2)
                    if 0 <= w - 2:
                        attend1(w - 2)

                def stage(item):
                    kind = item[0]
                    if kind == "at0":
                        at0(item[1])
                    elif kind == "first":
                        for t in range(TT):
                            qkv(U0, t)
                    elif kind in ("ff0", "ff1"):
                        ff(int(kind == "ff1"), item[1])
                    elif kind == "at1":
                        at1(item[1])
                    elif kind == "lnc":
                        misc_begin(item)
                        wait(ln_norm, n_ln(item[1], item[2], item[1:] == (0, 0)))
                        transposes4(xn)
                    elif kind == "rt":
                        misc_begin(item)
                        s = item[1]
                        wait(h_lo, n_ln(1, s))
                        for t in range(TT):
                            for c in range(DC):
                                last = mm3(misc[:, t * EXPERTS:(t + 1) * EXPERTS], h_of(s, c, t),
                                           w_of("r", c * EXPERTS, EXPERTS), c == 0, c == DC - 1)
                        last.then_inc(misc_mm.handle, 1)
                    elif kind == "ct":
                        misc_begin(item)
                        wait(c_ready, item[1] + 1)
                        for t in range(TT):
                            last = nc.tensor.transpose(misc[0:17, t * P:(t + 1) * P], c17[:, t, :], ident)
                        last.then_inc(misc_mm.handle, 1)
                    elif kind in ("q1", "k1"):
                        misc_begin(item)
                        s = item[1]
                        wait(h_lo, n_ln(2, s))
                        a = 0 if kind == "q1" else D
                        for c2 in range(DC):
                            for c in range(DC):
                                mm3(misc[:, c2 * T:(c2 + 1) * T], w_of("a1", c * 3 * D + a + c2 * P, P),
                                    h_of(s, c), c == 0, False)
                            b = BA + a + c2 * P
                            last = nc.tensor.matmul(misc[:, c2 * T:(c2 + 1) * T], brows[:, b:b + P], ones[:, :],
                                                    start=False, stop=True)
                        last.then_inc(misc_mm.handle, 1)
                    elif kind == "v1":
                        misc_begin(item)
                        s = item[1]
                        wait(h_lo, n_ln(2, s))
                        for t in range(TT):
                            for c in range(DC):
                                mm3(misc[:, t * D:(t + 1) * D], h_of(s, c, t),
                                    w_of("a1", c * 3 * D + 2 * D, D), c == 0, False)
                            last = nc.tensor.matmul(misc[:, t * D:(t + 1) * D], ones[:, 0:P],
                                                    brows[:, BA + 2 * D:BA + 3 * D], start=False, stop=True)
                        last.then_inc(misc_mm.handle, 1)
                    elif kind == "at":
                        misc_begin(item)
                        wait(o_read, n_o(2, item[1]))
                        transposes4(xn)
                    elif kind == "pj":
                        misc_begin(item)
                        wait(misc_free, MISC[("at", item[1])])
                        for t in range(TT):
                            for c in range(DC):
                                q = slice(c * T + t * P, c * T + (t + 1) * P)
                                mm3(misc[:, t * D:(t + 1) * D], (q1h[:, q], q1l[:, q]), w_of("p1", c * D, D),
                                    c == 0, False)
                            last = nc.tensor.matmul(misc[:, t * D:(t + 1) * D], ones[:, 0:P],
                                                    brows[:, BP:BP + D], start=False, stop=True)
                        last.then_inc(misc_mm.handle, 1)

                for t in range(TT):
                    qkv(0, t)
                with pe.Fori(0, NPAIR) as i:
                    for item in ORDER:
                        stage(item)

            @block.scalar
            def _(act):
                i = 0
                def wait(z, n):
                    act.wait_ge(z.handle, z.count(i, n))

                def copy_hi(dst, src, key, scale):
                    wait(misc_mm, MISC[key])
                    nc.scalar.activation(dst, src, ACT.Copy, scale=scale).then_inc(misc_hi.handle, 1)

                def qk_hi(e, t):
                    copy_hi(qkh[:, e % 2, :, t * P:(t + 1) * P], misc[:, 0:3 * P].rearrange("p (k n) -> p k n", k=3),
                            ("t1", e, t), 1.0 / WS)

                def p_hi(e, b):
                    lo, hi = ((0, 2), (2, 6))[b]
                    wait(pt_mm, 2 * e + b + 1)
                    nc.scalar.activation(pth[:, lo:hi, :], bank[5][:, 0:(hi - lo) * P]
                                         .rearrange("p (k n) -> p k n", n=P), ACT.Copy).then_inc(pt_hi.handle, 1)

                def stats(e, t):
                    wait(qkv_mm, 2 * e + t + 1)
                    nc.scalar.activation(vh0[:, e % 4, t, :], bank[t][:, 3 * P:4 * P], ACT.Copy, scale=1.0 / WS)
                    for k in range(3):
                        last = nc.scalar.activation(rb[:, t, k, :], bank[t][:, k * P:(k + 1) * P], ACT.Square,
                                                    accum_out=ss[:, 3 * t + k:3 * t + k + 1])
                    last.then_inc(qkv_act.handle, 1)

                def key_norm(e, t):
                    wait(rope_sum, 2 * e + t + 1)
                    wait(qk_rstd, 2 * e + t + 1)
                    nc.scalar.activation(ra[:, t, 2, :], ra[:, t, 2, :], ACT.Copy,
                                         scale=rs0[:, e % 4, 3 * t + 2:3 * t + 3]).then_inc(k_norm.handle, 1)

                def exps(e, t):
                    y = e % 2
                    if t == 0:
                        wait(s_shift, e + 1)
                    for k in range(2):
                        a = smx[:, y, k, t * P:t * P + (t + 1) * P]
                        nc.scalar.activation(a, a, ACT.Exp, bias=nb0[:, y, 2 * t + k:2 * t + k + 1],
                                             scale=rs0[:, e % 4, 3 * t + k:3 * t + k + 1],
                                             accum_out=sm0[:, y, 2 * t + k:2 * t + k + 1]).then_inc(s_exp.handle, 1)

                def exps1(w, t):
                    s, gr = divmod(w, 8)
                    y = w % 2
                    wait(a_shift, 2 * w + t + 1)
                    for j in range(4):
                        a = s1[:, y, j, t * P:t * P + (t + 1) * P]
                        nc.scalar.activation(a, a, ACT.Exp, bias=nb1[:, y, 4 * t + j:4 * t + j + 1],
                                             accum_out=sum1[:, s, t, 4 * gr + j:4 * gr + j + 1])\
                            .then_inc(a_exp.handle, 1)

                def p1_hi(w, b):
                    wait(at_mm, 3 * w + b + 1)
                    nc.scalar.activation(p1h[:, w % 2, b, :, :].rearrange("p j n -> p (j n)"),
                                         bank[4 + b][:, :], ACT.Copy).then_inc(at_hi.handle, 1)

                def stage(item):
                    kind = item[0]
                    if kind == "at0":
                        u = item[1]
                        if 0 <= u - 1 < U0:
                            key_norm(u - 1, 0)
                        if 0 <= u - 3 < U0:
                            p_hi(u - 3, 0)
                        if 0 <= u - 1 < U0:
                            qk_hi(u - 1, 0)
                        if 0 <= u - 1 < U0:
                            key_norm(u - 1, 1)
                        if 0 < u < U0:
                            stats(u, 0)
                        if 0 <= u - 3 < U0:
                            p_hi(u - 3, 1)
                        if 0 <= u - 1 < U0:
                            qk_hi(u - 1, 1)
                        if 0 <= u - 2 < U0:
                            exps(u - 2, 0)
                        if 0 < u < U0:
                            stats(u, 1)
                        if 0 <= u - 2 < U0:
                            exps(u - 2, 1)
                        for mid in MID_AT0.get(u, []):
                            stage(mid)
                        if 0 <= u - 3 < U0:
                            wait(enc_mm, u - 2)
                            nc.scalar.activation(ench[:, :, :, :].rearrange("p t k n -> p (t k n)"), bank[6][:, :],
                                                 ACT.Copy).then_inc(enc_hi.handle, 1)
                    elif kind == "first":
                        for t in range(TT):
                            stats(U0, t)
                    elif kind in ("ff0", "ff1"):
                        f, v = int(kind == "ff1"), item[1]
                        J = ff_dims(f)[0]
                        if v < 2 * J:
                            n = n_gu(f, v)
                            wait(gu_mm, n)
                            nc.scalar.activation(th[:, (n - 1) % 2, :], bank[(n - 1) % 2][:, 0:T], ACT.Tanh,
                                                 scale=0.5 / WS).then_inc(gu_tanh.handle, 1)
                        if 1 <= v <= 2 * J:
                            n = n_gu(f, v - 1)
                            z = (n - 1) % 3
                            if f:
                                wait(gu_read, n)
                            else:
                                wait(ce_read, v)
                            nc.scalar.activation(fh[:, z, :], fa[:, z, :], ACT.Copy).then_inc(hid_hi.handle, 1)
                    elif kind == "at1":
                        w = item[1]
                        if 0 <= w - 1 < W1G:
                            p1_hi(w - 1, 0)
                        if 0 <= w - 1 < W1G:
                            p1_hi(w - 1, 1)
                        if w < W1G:
                            exps1(w, 0)
                        if 0 <= w - 1 < W1G:
                            p1_hi(w - 1, 2)
                        if w < W1G:
                            exps1(w, 1)
                    elif kind == "lnc":
                        k, s = item[1:]
                        wait(misc_free, MISC[item])
                        nc.scalar.activation(hth[:, s].rearrange("p c n -> p (c n)"), hf[:, :],
                                             ACT.Copy).then_inc(h_hi.handle, 1)
                    elif kind == "rt":
                        wait(rt_sub, item[1] + 1)
                        nc.scalar.activation(rt_e, rt_a, ACT.Exp).then_inc(rt_exp.handle, 1)
                    elif kind == "q1":
                        copy_hi(q1h[:, :], misc[:, :], item, 1.0 / WS)
                    elif kind == "k1":
                        copy_hi(k1h[:, item[1]].rearrange("p c n -> p (c n)"), misc[:, :], item, 1.0 / WS)
                    elif kind == "v1":
                        copy_hi(v1h[:, item[1]].rearrange("p c n -> p (c n)"), misc[:, :], item, 1.0 / WS)
                    elif kind == "at":
                        copy_hi(q1h[:, :], misc[:, :], item, 1.0)

                for t in range(TT):
                    stats(0, t)
                with act.Fori(0, NPAIR) as i:
                    for item in ORDER:
                        stage(item)

            @block.gpsimd
            def _(pool):
                i = 0
                chained = [0]

                def wait(z, n):
                    pool.wait_ge(z.handle, z.count(i, n))

                def link(ins):
                    chained[0] += 1
                    ins.then_inc(g_chain.handle, 1)
                    wait(g_chain, chained[0])

                def norms_and_rope(u):
                    for t in range(TT):
                        k3 = slice(3 * t, 3 * t + 3)
                        wait(qkv_act, 2 * u + t + 1)
                        pool.sem_inc(passed_pool, 1)
                        link(nc.gpsimd.tensor_scalar(ms[:, k3], ss[:, k3], 1.0 / (HD * WS * WS), 1e-6,
                                                     ALU.mult, ALU.add))
                        nc.gpsimd.tensor_tensor(rs0[:, u % 4, k3], ms[:, k3], half[:, 0:3], ALU.pow)\
                            .then_inc(qk_rstd.handle, 1)
                        wait(rope_mul, 2 * u + t + 1)
                        a, b = (z[:, t].rearrange("p k h -> p (k h)") for z in (ra, rb))
                        nc.gpsimd.tensor_tensor(a, a, b, ALU.add).then_inc(rope_sum.handle, 1)

                def stage(item):
                    kind = item[0]
                    if kind == "lna":
                        wait(ln_stats, n_ln(item[1], item[2], item[1:] == (0, 0)))
                        pool.sem_inc(passed_pool, 1)
                        link(nc.gpsimd.tensor_scalar(lv, mv[:, :, 1], 1e-5, None, ALU.add))
                        nc.gpsimd.tensor_tensor(lr[:, 0:TT], lv, half[:, 0:TT], ALU.pow).then_inc(ln_rstd.handle, 1)
                    elif kind == "at0":
                        u = item[1]
                        for mid in MID_AT0.get(u, []):
                            stage(mid)
                        if 0 < u < U0:
                            norms_and_rope(u)
                    elif kind == "first":
                        norms_and_rope(U0)
                    elif kind in ("ff0", "ff1"):
                        f, v = int(kind == "ff1"), item[1]
                        J = ff_dims(f)[0]
                        if 1 <= v <= 2 * J:
                            n = n_gu(f, v - 1)
                            z = (n - 1) % 3
                            wait(hid_hi, n)
                            nc.gpsimd.tensor_tensor(fl[:, z, :], fa[:, z, :], fh[:, z, :], ALU.subtract)\
                                .then_inc(hid_lo.handle, 1)

                norms_and_rope(0)
                with pool.Fori(0, NPAIR) as i:
                    for item in ORDER:
                        stage(item)
                    assert chained[0] == g_chain.per + TT, chained[0]

            @block.vector
            def _(dve):
                i = 0
                chained = [0]

                def wait(z, n):
                    dve.wait_ge(z.handle, z.count(i, n))

                def link(ins):
                    chained[0] += 1
                    ins.then_inc(v_chain.handle, 1)
                    wait(v_chain, chained[0])

                def split_lo(dst, src, hi, key, scale):
                    wait(misc_hi, MISC_HI[key])
                    nc.vector.scalar_tensor_tensor(out=dst, in0=src, scalar=scale, in1=hi, op0=ALU.mult,
                                                   op1=ALU.subtract).then_inc(misc_free.handle, 1)

                def residual(ps, s, k, into, base):
                    tmp = hf[:, :].rearrange("p (t d) -> p t d", t=TT)
                    g = gate[:, s, k:k + 1, :].to_broadcast([P, TT, D])
                    n = nc.vector.tensor_tensor(tmp, ps[:, :].rearrange("p (t d) -> p t d", t=TT), g, ALU.mult)
                    return n, lambda: nc.vector.tensor_tensor(into, tmp, base, ALU.add)

                def qk_lo(e, t):
                    c = slice(t * P, (t + 1) * P)
                    split_lo(qkl[:, e % 2, :, c], misc[:, 0:3 * P].rearrange("p (k n) -> p k n", k=3),
                             qkh[:, e % 2, :, c], ("t1", e, t), 1.0 / WS)

                def p_lo(e, b):
                    lo, hi = ((0, 2), (2, 6))[b]
                    wait(pt_hi, 2 * e + b + 1)
                    nc.vector.tensor_tensor(ptl[:, lo:hi, :], bank[5][:, 0:(hi - lo) * P]
                                            .rearrange("p (k n) -> p k n", n=P), pth[:, lo:hi, :],
                                            ALU.subtract).then_inc(pt_lo.handle, 1)

                def rope_products(e, t):
                    wait(qkv_act, 2 * e + t + 1)
                    nc.vector.scalar_tensor_tensor(out=vl0[:, e % 4, t, :], in0=bank[t][:, 3 * P:4 * P],
                                                   scalar=1.0 / WS, in1=vh0[:, e % 4, t, :],
                                                   op0=ALU.mult, op1=ALU.subtract)
                    src = bank[t][:, 0:3 * P].rearrange("p (k h) -> p k h", k=3)
                    nc.vector.tensor_tensor(ra[:, t], src, ropec[:, t], ALU.mult)
                    hh = HD // 2
                    nc.vector.tensor_tensor(rb[:, t, :, 0:hh], src[:, :, hh:HD], ropes[:, t, :, 0:hh], ALU.mult)
                    nc.vector.tensor_tensor(rb[:, t, :, hh:HD], src[:, :, 0:hh], ropes[:, t, :, hh:HD], ALU.mult)\
                        .then_inc(rope_mul.handle, 1)

                def mask_max(e):
                    y = e % 2
                    for t in range(TT):
                        wait(s_mm, 2 * e + t + 1)
                        dve.sem_inc(passed_dve, 1)
                        n = (t + 1) * P
                        for k in range(2):
                            nc.vector.tensor_tensor_reduce(
                                out=smx[:, y, k, t * P:t * P + n], in0=bank[3 + t][:, k * n:(k + 1) * n],
                                in1=mask0[:, t * P:t * P + n], scale=1.0, scalar=-3e38, op0=ALU.add,
                                op1=ALU.max, accum_out=mx0[:, y, 2 * t + k:2 * t + k + 1]).then_inc(s_max.handle, 1)
                    wait(s_max, 4 * (e + 1))
                    wait(qk_rstd, 2 * (e + 1))
                    nc.vector.scalar_tensor_tensor(
                        out=nb0[:, y, :].rearrange("p (t k) -> p t k", t=TT),
                        in0=mx0[:, y, :].rearrange("p (t k) -> p t k", t=TT), scalar=-1.0,
                        in1=rs0[:, e % 4, :].rearrange("p (t k) -> p t k", t=TT)[:, :, 0:2],
                        op0=ALU.mult, op1=ALU.mult).then_inc(s_shift.handle, 1)

                def normalise(e, t):
                    y = e % 2
                    wait(s_exp, 4 * e + 2 * (t + 1))
                    link(nc.vector.reciprocal(ri0[:, y, 2 * t:2 * t + 2], sm0[:, y, 2 * t:2 * t + 2]))
                    for k in range(2):
                        a = smx[:, y, k, t * P:t * P + (t + 1) * P]
                        nc.vector.tensor_scalar(a, a, ri0[:, y, 2 * t + k:2 * t + k + 1], None,
                                                ALU.mult).then_inc(p_norm.handle, 1)

                def at0(u):
                    if 0 <= u - 1 < U0:
                        qk_lo(u - 1, 0)
                    if 0 <= u - 3 < U0:
                        p_lo(u - 3, 0)
                    if 0 <= u - 2 < U0:
                        mask_max(u - 2)
                    if 0 < u < U0:
                        rope_products(u, 0)
                    if 0 <= u - 3 < U0:
                        p_lo(u - 3, 1)
                    if 0 <= u - 1 < U0:
                        qk_lo(u - 1, 1)
                    if 0 <= u - 2 < U0:
                        normalise(u - 2, 0)
                    for item in MID_AT0.get(u, []):
                        stage(item)
                    if 0 < u < U0:
                        rope_products(u, 1)
                    if 0 <= u - 2 < U0:
                        normalise(u - 2, 1)
                    if 0 <= u - 3 < U0:
                        wait(enc_hi, u - 2)
                        nc.vector.tensor_tensor(encl[:, :, :, :].rearrange("p t k n -> p (t k n)"), bank[6][:, :],
                                                ench[:, :, :, :].rearrange("p t k n -> p (t k n)"),
                                                ALU.subtract).then_inc(enc_lo.handle, 1)

                def ff(f, v):
                    J = ff_dims(f)[0]
                    if v >= 2 * J:
                        return
                    n = n_gu(f, v)
                    z, bk = (n - 1) % 3, bank[(n - 1) % 2]
                    wait(gu_tanh, n)
                    link(nc.vector.scalar_tensor_tensor(out=fa[:, z, :], in0=th[:, (n - 1) % 2, :], scalar=1.0,
                                                        in1=bk[:, 0:T], op0=ALU.add, op1=ALU.mult))
                    nc.vector.scalar_tensor_tensor(out=fa[:, z, :], in0=fa[:, z, :],
                                                   scalar=0.5 / (WS * WS) if f else 1.0, in1=bk[:, T:2 * T],
                                                   op0=ALU.mult, op1=ALU.mult).then_inc(gu_read.handle, 1)
                    if not f:
                        wait(gu_read, n)
                        wait(ce_mm, v + 1)
                        nc.vector.tensor_tensor(fa[:, z, :], fa[:, z, :], bank[3 + v % 2][:, 0:T], ALU.mult)\
                            .then_inc(ce_read.handle, 1)

                def max1(w, t):
                    y = w % 2
                    n = (t + 1) * P
                    for j in range(4):
                        if t == 0 and j == 0:
                            wait(a_mm, 3 * w + 1)
                        if t == 1 and j % 2 == 0:
                            wait(a_mm, 3 * w + 2 + j // 2)
                        dve.sem_inc(passed_dve, 1)
                        src = bank[0][:, j * P:(j + 1) * P] if t == 0 else \
                            bank[(1, 3)[j // 2]][:, j % 2 * T:(j % 2 + 1) * T]
                        nc.vector.tensor_tensor_reduce(
                            out=s1[:, y, j, t * P:t * P + n], in0=src, in1=bias1[:, t * P:t * P + n],
                            scale=1.0, scalar=-3e38, op0=ALU.add, op1=ALU.max,
                            accum_out=mx1[:, y, 4 * t + j:4 * t + j + 1]).then_inc(a_max.handle, 1)
                    wait(a_max, 8 * w + 4 * (t + 1))
                    nc.vector.tensor_scalar(nb1[:, y, 4 * t:4 * t + 4], mx1[:, y, 4 * t:4 * t + 4], -1.0,
                                            None, ALU.mult).then_inc(a_shift.handle, 1)

                def p1_lo(w, b):
                    wait(at_hi, 3 * w + b + 1)
                    z = w % 2
                    nc.vector.tensor_tensor(p1l[:, z, b, :, :].rearrange("p j n -> p (j n)"), bank[4 + b][:, :],
                                            p1h[:, z, b, :, :].rearrange("p j n -> p (j n)"),
                                            ALU.subtract).then_inc(at_lo.handle, 1)

                def at1(w):
                    if w < W1G:
                        max1(w, 0)
                    if w < W1G:
                        max1(w, 1)
                    if 0 <= w - 1 < W1G:
                        p1_lo(w - 1, 0)
                    if 0 <= w - 1 < W1G:
                        p1_lo(w - 1, 1)
                    if 0 <= w - 1 < W1G:
                        p1_lo(w - 1, 2)

                over = lambda k: rt_m[:, k, :].unsqueeze(2).to_broadcast([P, TT, EXPERTS])
                io = iota.unsqueeze(1).to_broadcast([P, TT, EXPERTS])

                def pick(src, k, kept):
                    link(nc.vector.tensor_tensor(kept, src, over(k), ALU.is_ge))
                    link(nc.vector.tensor_tensor(kept, kept, io, ALU.mult))
                    link(nc.vector.tensor_reduce(rt_m[:, 2, :], kept, AX.X, ALU.max))
                    link(nc.vector.tensor_tensor(kept, io, over(2), ALU.is_equal))

                def route(part, s):
                    if part == 0:
                        nc.vector.tensor_scalar(rt_l, misc[:, 0:TT * EXPERTS].rearrange("p (t e) -> p t e", t=TT),
                                                1.0 / WS, None, ALU.mult).then_inc(misc_free.handle, 1)
                        wait(misc_free, MISC[("rt", s)])
                        link(nc.vector.tensor_reduce(rt_m[:, 0, :], rt_l, AX.X, ALU.max))
                        nc.vector.tensor_tensor(rt_a, rt_l, over(0), ALU.subtract).then_inc(rt_sub.handle, 1)
                        pick(rt_l, 0, rt_k)
                    if part == 1:
                        link(nc.vector.scalar_tensor_tensor(out=rt_l, in0=rt_k, scalar=-3e38, in1=rt_l,
                                                            op0=ALU.mult, op1=ALU.add))
                        link(nc.vector.tensor_reduce(rt_m[:, 1, :], rt_l, AX.X, ALU.max))
                        pick(rt_l, 1, rt_k2)
                    if part == 2:
                        link(nc.vector.tensor_tensor(rt_k, rt_k, rt_k2, ALU.add))
                        wait(rt_exp, s + 1)
                        link(nc.vector.tensor_tensor(rt_e, rt_e, rt_k, ALU.mult))
                        link(nc.vector.tensor_reduce(rt_m[:, 3, :], rt_e, AX.X, ALU.add))
                        link(nc.vector.reciprocal(rt_m[:, 3, :], rt_m[:, 3, :]))
                        link(nc.vector.tensor_tensor(rt_e, rt_e, over(3), ALU.mult))
                        link(nc.vector.tensor_copy(ch16, rt_e))
                        link(nc.vector.tensor_copy(c17[:, :, 0:8], ch16))
                        nc.vector.tensor_tensor(c17[:, :, 9:17], rt_e, ch16, ALU.subtract)\
                            .then_inc(c_ready.handle, 1)

                def stage(item):
                    kind = item[0]
                    if kind == "at0":
                        at0(item[1])
                    elif kind == "first":
                        for t in range(TT):
                            rope_products(U0, t)
                    elif kind in ("ff0", "ff1"):
                        ff(int(kind == "ff1"), item[1])
                    elif kind == "at1":
                        at1(item[1])
                    elif kind == "mc":
                        s = item[1]
                        link(nc.vector.tensor_copy(mcol[:, s, :], modt[:, 2 * i + (1 if s else 2), :]))
                    elif kind == "lna":
                        k, s = item[1:]
                        if k == 0:
                            wait(ld_x[s], 0 if s else 1)
                        src = xin if k == 0 else xs
                        for t in range(TT):
                            ins = nc.vector.bn_stats(st6[:, t, :], src[:, s, t, :])
                        link(ins)
                        dve.sem_inc(passed_dve, 1)
                        for t in range(TT):
                            ins = nc.vector.bn_aggr(mv[:, t, :], st6[:, t, :])
                        ins.then_inc(ln_stats.handle, 1)
                    elif kind == "lnb":
                        k, s = item[1:]
                        src = xin if k == 0 else xs
                        wait(ln_rstd, n_ln(k, s, item[1:] == (0, 0)))
                        for t in range(TT):
                            ins = nc.vector.tensor_scalar(xn[:, t, :], src[:, s, t, :], mv[:, t, 0:1],
                                                          lr[:, t:t + 1], ALU.subtract, ALU.mult)
                        ins.then_inc(ln_norm.handle, 1)
                    elif kind == "lnc":
                        k, s = item[1:]
                        wait(misc_mm, MISC[item])
                        for c in range(DC):
                            a = 4 * k + c
                            ins = nc.vector.tensor_scalar(hf[:, c * T:(c + 1) * T], misc[:, c * T:(c + 1) * T],
                                                          mcol[:, s, a:a + 1], mcol[:, s, a + 2:a + 3],
                                                          ALU.mult, ALU.add)
                        ins.then_inc(misc_free.handle, 1)
                    elif kind == "lnd":
                        k, s = item[1:]
                        wait(misc_free, MISC[("lnc", k, s)])
                        wait(h_hi, n_ln(k, s, item[1:] == (0, 0)))
                        nc.vector.tensor_tensor(htl[:, s].rearrange("p c n -> p (c n)"), hf[:, :],
                                                hth[:, s].rearrange("p c n -> p (c n)"), ALU.subtract)\
                            .then_inc(h_lo.handle, 1)
                    elif kind == "rt":
                        wait(misc_mm, MISC[item])
                        route(0, item[1])
                    elif kind in ("rt2", "rt3"):
                        route(1 if kind == "rt2" else 2, item[1])
                    elif kind == "ct":
                        wait(misc_mm, MISC[item])
                        nc.vector.tensor_copy(ctt[:, item[1], :], misc[0:17, 0:T]).then_inc(misc_free.handle, 1)
                    elif kind == "res0":
                        s = item[1]
                        wait(o_mm, n_o(0, s))
                        wait(ld_g[s], 1)
                        wait(st_x[s], 0)
                        ins, add = residual(bank[7], s, 0, xs[:, s], xin[:, s])
                        link(ins)
                        add().then_inc(o_read.handle, 1)
                        wait(o_read, n_o(0, s))
                    elif kind == "resf":
                        f, s = item[1:]
                        stage_ = 3 if f else 1
                        wait(o_mm, n_o(stage_, s))
                        ins, add = residual(bank[o_bank[(stage_, s)]], s, 1, xs[:, s], xs[:, s])
                        link(ins)
                        add().then_inc(o_read.handle, 1)
                        wait(o_read, n_o(stage_, s))
                    elif kind == "q1":
                        split_lo(q1l[:, :], misc[:, :], q1h[:, :], item, 1.0 / WS)
                        wait(misc_free, MISC[item])
                    elif kind == "k1":
                        s = item[1]
                        split_lo(k1l[:, s].rearrange("p c n -> p (c n)"), misc[:, :],
                                 k1h[:, s].rearrange("p c n -> p (c n)"), item, 1.0 / WS)
                    elif kind == "v1":
                        s = item[1]
                        split_lo(v1l[:, s].rearrange("p c n -> p (c n)"), misc[:, :],
                                 v1h[:, s].rearrange("p c n -> p (c n)"), item, 1.0 / WS)
                    elif kind == "qm":
                        s, c = item[1:]
                        wait(a_mm, 24 * (s - 1) + 12 * (c + 1))
                        cc = slice(c * T, (c + 1) * T)
                        for j in range(4):
                            for src, dst in ((q1h, qmh), (q1l, qml)):
                                ins = nc.vector.tensor_scalar(dst[:, j, cc], src[:, cc], con[:, K_HM + j:K_HM + j + 1],
                                                              None, ALU.mult)
                        ins.then_inc(qm_ready.handle, 1)
                    elif kind == "pvr":
                        s = item[1]
                        link(nc.vector.reciprocal(ri1, sum1[:, s]))
                        wait(o_mm, n_o(2, s))
                        rb1 = ri1.rearrange("p t h -> p (t h)").unsqueeze(2).to_broadcast([P, TT * H1, HD1])
                        nc.vector.tensor_tensor(xn[:, :, :].rearrange("p t (h e) -> p (t h) e", e=HD1),
                                                bank[7][:, :].rearrange("p (n e) -> p n e", e=HD1), rb1,
                                                ALU.mult).then_inc(o_read.handle, 1)
                    elif kind == "at":
                        split_lo(q1l[:, :], misc[:, :], q1h[:, :], item, 1.0)
                    elif kind == "pj":
                        s = item[1]
                        wait(misc_mm, MISC[item])
                        wait(ld_g[s], 2)
                        ins, add = residual(misc, s, 0, xs[:, s], xs[:, s])
                        link(ins)
                        add().then_inc(misc_free.handle, 1)
                        wait(misc_free, MISC[item])

                for t in range(TT):
                    rope_products(0, t)
                with dve.Fori(0, NPAIR) as i:
                    for item in ORDER:
                        stage(item)
                    assert chained[0] <= CHAIN, chained[0]
                    dve.sem_inc(v_chain.handle, CHAIN - chained[0])


def _constants():
    rows = np.arange(P)[:, None]
    con = np.zeros((P, NC), np.float32)
    con[:, K_ID:K_ID + P] = np.eye(P)
    ramp = 2.0 ** (-8.0 / H1)
    for t in range(TT):
        keys = np.arange((t + 1) * P)[None, :]
        q = t * P + rows
        seen = keys <= q
        a, b = t * P, t * P + (t + 1) * P
        con[:, K_M0 + a:K_M0 + b] = np.where(seen & (q - keys < WINDOW), 0.0, NEG)
        con[:, K_M1 + a:K_M1 + b] = np.where(seen, (keys - q) * ramp, NEG)
    for j in range(4):
        con[:, K_HM + j] = (np.arange(P) % 32 // HD1 == j) * (HD1 ** -0.5)
    con[:, K_IO:K_IO + EXPERTS] = np.arange(EXPERTS, 0, -1)
    con[0, K_BS] = 1.0
    con[1, K_BS + 1] = 1.0
    bits = np.arange(P)[:, None] & np.arange(P)[None, :]
    ones = np.array([[bin(v).count("1") % 2 for v in row] for row in bits])
    had = (1.0 - 2.0 * ones).astype(np.float32)
    frac = np.arange(0, HD, 2, dtype=np.float32) / np.float32(HD)
    turn = np.arange(T, dtype=np.float32)[:, None] / (np.float32(10000.0) ** frac)
    cos, sin = np.cos(turn).astype(np.float32), np.sin(turn).astype(np.float32)
    rope = np.stack([np.concatenate([cos, cos], 1), np.concatenate([-sin, sin], 1)])
    rope = np.ascontiguousarray(rope.reshape(2, TT, P, HD).transpose(2, 0, 1, 3))
    sel = np.zeros((17, HP), np.float16)
    for h in range(HID0):
        e = h // INNER
        if e < EXPERTS:
            sel[e, h] = sel[9 + e, h] = 0.5 / (WS * WS)
        else:
            sel[8, h] = 0.5 / (WS * WS)
    return con, had, rope, sel


def _tiles(w, n=None):
    w = np.asarray(w)
    if n is not None and w.shape[1] < n:
        w = np.concatenate([w, np.zeros((w.shape[0], n - w.shape[1]), w.dtype)], 1)
    return w.reshape(-1, P, w.shape[1]).transpose(1, 0, 2).reshape(P, -1)


def _layout(v):
    v = {k: np.asarray(a) for k, a in v.items()}
    q, kv = v["L0_attn_q_kernel"], v["L0_attn_kv_kernel"]
    qkv = np.stack([q[0::2], q[1::2], kv[0], kv[1]], 0)
    qkv = qkv.reshape(4, NKV, DC, P, HD).transpose(3, 2, 1, 0, 4).reshape(P, -1)
    side = lambda name: v[name].transpose(1, 0, 2).reshape(D, EXPERTS * INNER)
    gate = np.concatenate([side("L0_ffn_gate_w"), v["L0_ffn_s_gate_w"]], 1)
    up = np.concatenate([side("L0_ffn_up_w"), v["L0_ffn_s_up_w"]], 1)
    down = np.concatenate([v["L0_ffn_down_w"].reshape(EXPERTS * INNER, D), v["L0_ffn_s_down_w"],
                           np.zeros((HP - HID0, D), np.float32)], 0)
    wall = np.concatenate([
        qkv, v["L0_attn_out_kernel"].transpose(1, 0, 2).reshape(P, NH * D), _tiles(gate, HP), _tiles(up, HP),
        _tiles(down), _tiles(v["L0_ffn_router_w"].T), _tiles(v["L1_attn_W_attn"]), _tiles(v["L1_attn_W_proj"]),
        _tiles(v["L1_ffn_W1"].T), _tiles(v["L1_ffn_W3"].T)], 1)
    w2t = _tiles(v["L1_ffn_W2"].T)
    shared = np.zeros((2, (J0 - JB) * P), np.float32)
    shared[0, :SHARED] = v["L0_ffn_s_gate_b"]
    shared[1, :SHARED] = v["L0_ffn_s_up_b"]
    brow = np.concatenate([shared.reshape(-1), v["L0_ffn_s_down_b"], v["L1_attn_b_attn"], v["L1_attn_b_proj"]])
    qs, ks = v["L0_attn_q_norm_scale"], v["L0_attn_k_norm_scale"]
    turned = lambda s: np.concatenate([s[HD // 2:], s[:HD // 2]])
    nsc = np.stack([np.stack([qs, qs, ks]), np.stack([turned(qs), turned(qs), turned(ks)])])
    per_layer = lambda a, b: np.stack([_tiles(a).reshape(P, DC, -1), _tiles(b).reshape(P, DC, -1)], 1)
    ct = per_layer(v["L0_c"].T, v["L1_c"].T)
    wmod = per_layer(v["L0_wmod"], v["L1_wmod"])
    con, had, rope, sel = _constants()
    x = np.concatenate([v["L0_attn_x"], np.zeros((2, T, D), np.float32)])
    return {"x": x, "wall": wall, "w2t": w2t, "brow": brow, "con": con, "had": had, "rope": rope,
            "nsc": nsc, "sel": sel, "ct": ct, "wmod": wmod}


def kernel(**inputs):
    import concourse.bacc as _bacc
    from concourse.bass_utils import run_bass_kernel_spmd as _run

    assert JB * P == EXPERTS * INNER
    nc = _bacc.Bacc("TRN2", target_bir_lowering=False, num_devices=1, dynamic_dma_scratch_size=1024)
    arrays, args = {}, []
    for name, a in _layout(inputs).items():
        a = np.ascontiguousarray(a)
        arrays[f"in_{name}_dram"] = a
        args.append(nc.dram_tensor(f"in_{name}_dram", a.shape, mybir.dt.from_np(a.dtype), kind="ExternalInput").ap())
    out = nc.dram_tensor("out_dram", (B, T, D), F32, kind="ExternalOutput").ap()
    gates = nc.dram_tensor("gates_dram", (B, 4 * D), F32, kind="Internal").ap()
    build(nc, *args, out, gates)
    r = _run(nc, [arrays], core_ids=[0])
    return r.results[0]["out_dram"]
```
